# Optimizing a Trainium2 kernel written in Bass

```python
import numpy as np
import jax
import jax.numpy as jnp

def _softmax(x, axis=-1):
    return jax.nn.softmax(x, axis=axis)

def _gelu(x):
    return jax.nn.gelu(x, approximate=True)

def _silu(x):
    return jax.nn.silu(x)

def _sigmoid(x):
    return jax.nn.sigmoid(x)

def _layernorm(x, axis=-1, eps=1e-05):
    m = jnp.mean(x, axis=axis, keepdims=True)
    v = jnp.var(x, axis=axis, keepdims=True)
    return (x - m) / jnp.sqrt(v + eps)

def _scatter_add(tgt, idx, src, axis=0):
    return tgt.at[idx].add(src)

def _segment_sum(src, seg, n):
    return jax.ops.segment_sum(src, seg, n)
kernel_name = 'mk_seq_preln_d2_jaxref_r8_acbec3'

def setup_inputs(seed: int=0):
    np.random.seed(seed)
    _w = jnp.asarray

    def _L0_attn_setup():
        import jax, jax.numpy as jnp
        import numpy as np
        B, T, C, NH = (8, 128, 128, 16)
        HD = C // NH
        EPS = 1e-05

        def _decay_mask(nh, t, dtype):
            gamma = 1.0 - 2.0 ** (-5.0 - jnp.arange(nh, dtype=jnp.float32))
            idx = jnp.arange(t)
            diff = idx[:, None] - idx[None, :]
            mask = diff >= 0
            pow_ = gamma[:, None, None] ** jnp.where(mask, diff, 0).astype(jnp.float32)
            return (jnp.where(mask[None], pow_, 0.0).astype(dtype), gamma.astype(dtype))

        def _reference_tuple_inner(x, past_kv, W_qkv, gn_weight, gn_bias):
            b, t, c = x.shape
            nh = gn_weight.shape[0]
            hd = c // nh
            qkv = x @ W_qkv
            q, k, v = jnp.split(qkv, 3, axis=2)
            split_heads = lambda u: u.reshape(b, t, nh, hd).transpose(0, 2, 1, 3)
            q, k, v = (split_heads(q), split_heads(k), split_heads(v))
            decay, gamma = _decay_mask(nh, t, x.dtype)
            ret = jnp.einsum('bhtd,bhsd->bhts', q, k) * decay
            inner = jnp.einsum('bhts,bhsd->bhtd', ret, v)
            inner_decay = float(nh * hd)
            cross = jnp.einsum('bhtd,hde->bhte', q, past_kv) * inner_decay
            r = inner + cross
            current_kv = gamma[:, None, None] * past_kv + jnp.einsum('bhtd,bhte->bhde', k, v)
            current_kv = current_kv.mean(axis=0)
            y = r.transpose(0, 1, 3, 2)
            mu = y.mean(axis=(1, 2, 3), keepdims=True)
            var = y.var(axis=(1, 2, 3), keepdims=True)
            yn = (y - mu) * jax.lax.rsqrt(var + EPS)
            yn = yn * gn_weight[None, :, None, None] + gn_bias[None, :, None, None]
            out = yn.transpose(0, 3, 1, 2).reshape(b, t, c)
            return (out, current_kv)
        key = jax.random.key(seed)
        k1, k2, k3 = jax.random.split(key, 3)
        x = jax.random.normal(k1, (B, T, C), dtype=jnp.float32)
        past_kv = jax.random.normal(k2, (NH, HD, HD), dtype=jnp.float32) * 0.1
        W_qkv = jax.random.normal(k3, (C, 3 * C), dtype=jnp.float32) * 0.02
        gn_weight = jnp.ones((NH,), dtype=jnp.float32)
        gn_bias = jnp.zeros((NH,), dtype=jnp.float32)
        return {'x': x, 'past_kv': past_kv, 'W_qkv': W_qkv, 'gn_weight': gn_weight, 'gn_bias': gn_bias}
    _L0_attn_in = _L0_attn_setup()

    def _L0_ffn_setup():
        import jax, jax.numpy as jnp
        import numpy as np
        N_BLOCKS = 16
        BLOCK = 32
        TOP_K = N_BLOCKS // 4
        key = jax.random.key(seed)
        ks = jax.random.split(key, 7)
        D, H = (128, 512)
        s = lambda k, shape, scale: jax.random.normal(k, shape, dtype=jnp.float32) * scale
        return {'x': s(ks[0], (4, 512, D), 1.0), 'w_router': s(ks[1], (D, N_BLOCKS), 0.03), 'b_router': s(ks[2], (N_BLOCKS,), 0.01), 'w1': s(ks[3], (H, D), 0.03), 'b1': s(ks[4], (H,), 0.01), 'w2': s(ks[5], (D, H), 0.03), 'b2': s(ks[6], (D,), 0.01)}
    _L0_ffn_in = _L0_ffn_setup()

    def _L1_attn_setup():
        import jax, jax.numpy as jnp
        import numpy as np
        D_MODEL, N_HEADS = (128, 16)
        D_H = D_MODEL // N_HEADS
        D_HR = D_H // 2
        D_LATENT = 32
        THETA = 10000.0

        def rope(x, theta=THETA):
            S, d = (x.shape[-2], x.shape[-1])
            inv = theta ** (-jnp.arange(0, d, 2, dtype=jnp.float32) / d)
            ang = jnp.arange(S, dtype=jnp.float32)[:, None] * inv
            cos, sin = (jnp.cos(ang), jnp.sin(ang))
            x1, x2 = (x[..., 0::2], x[..., 1::2])
            r1 = x1 * cos - x2 * sin
            r2 = x1 * sin + x2 * cos
            return jnp.stack([r1, r2], axis=-1).reshape(x.shape)
        key = jax.random.key(seed)
        ks = jax.random.split(key, 9)
        s = lambda fan_in: 1.0 / np.sqrt(fan_in)
        return {'x': jax.random.normal(ks[0], (4, 256, D_MODEL), jnp.float32), 'W_DQ': jax.random.normal(ks[1], (D_MODEL, D_LATENT), jnp.float32) * s(D_MODEL), 'W_UQ': jax.random.normal(ks[2], (D_LATENT, N_HEADS * D_H), jnp.float32) * s(D_LATENT), 'W_QR': jax.random.normal(ks[3], (D_LATENT, N_HEADS * D_HR), jnp.float32) * s(D_LATENT), 'W_DKV': jax.random.normal(ks[4], (D_MODEL, D_LATENT), jnp.float32) * s(D_MODEL), 'W_UK': jax.random.normal(ks[5], (D_LATENT, N_HEADS * D_H), jnp.float32) * s(D_LATENT), 'W_UV': jax.random.normal(ks[6], (D_LATENT, N_HEADS * D_H), jnp.float32) * s(D_LATENT), 'W_KR': jax.random.normal(ks[7], (D_MODEL, D_HR), jnp.float32) * s(D_MODEL), 'W_O': jax.random.normal(ks[8], (N_HEADS * D_H, D_MODEL), jnp.float32) * s(N_HEADS * D_H)}
    _L1_attn_in = _L1_attn_setup()

    def _L1_ffn_setup():
        import jax, jax.numpy as jnp
        import numpy as np
        NUM_EXPERTS = 8
        TOP_K = 2
        CAPACITY_FACTOR = 1.25
        key = jax.random.key(seed)
        ks = jax.random.split(key, 5)
        B, S, D, H, E = (4, 256, 128, 256, NUM_EXPERTS)
        scale = 0.02
        return {'x': jax.random.normal(ks[0], (B, S, D), dtype=jnp.float32), 'gate_w': jax.random.normal(ks[1], (E, D), dtype=jnp.float32) * scale, 'gate_proj_w': jax.random.normal(ks[2], (E, H, D), dtype=jnp.float32) * scale, 'up_proj_w': jax.random.normal(ks[3], (E, H, D), dtype=jnp.float32) * scale, 'down_proj_w': jax.random.normal(ks[4], (E, D, H), dtype=jnp.float32) * scale}
    _L1_ffn_in = _L1_ffn_setup()
    _d = {'L0_attn_x': _L0_attn_in['x'], 'L0_attn_past_kv': _L0_attn_in['past_kv'], 'L0_attn_W_qkv': _L0_attn_in['W_qkv'], 'L0_attn_gn_weight': _L0_attn_in['gn_weight'], 'L0_attn_gn_bias': _L0_attn_in['gn_bias'], 'L0_ffn_w_router': _L0_ffn_in['w_router'], 'L0_ffn_b_router': _L0_ffn_in['b_router'], 'L0_ffn_w1': _L0_ffn_in['w1'], 'L0_ffn_b1': _L0_ffn_in['b1'], 'L0_ffn_w2': _L0_ffn_in['w2'], 'L0_ffn_b2': _L0_ffn_in['b2'], 'L1_attn_W_DQ': _L1_attn_in['W_DQ'], 'L1_attn_W_UQ': _L1_attn_in['W_UQ'], 'L1_attn_W_QR': _L1_attn_in['W_QR'], 'L1_attn_W_DKV': _L1_attn_in['W_DKV'], 'L1_attn_W_UK': _L1_attn_in['W_UK'], 'L1_attn_W_UV': _L1_attn_in['W_UV'], 'L1_attn_W_KR': _L1_attn_in['W_KR'], 'L1_attn_W_O': _L1_attn_in['W_O'], 'L1_ffn_gate_w': _L1_ffn_in['gate_w'], 'L1_ffn_gate_proj_w': _L1_ffn_in['gate_proj_w'], 'L1_ffn_up_proj_w': _L1_ffn_in['up_proj_w'], 'L1_ffn_down_proj_w': _L1_ffn_in['down_proj_w']}
    _x0 = _d['L0_attn_x']
    _d['L0_attn_x'] = jax.random.normal(jax.random.fold_in(jax.random.key(seed), 1), (8, 512, 128), dtype=_x0.dtype)
    del _x0
    return _d

def reference(L0_attn_x, L0_attn_past_kv, L0_attn_W_qkv, L0_attn_gn_weight, L0_attn_gn_bias, L0_ffn_w_router, L0_ffn_b_router, L0_ffn_w1, L0_ffn_b1, L0_ffn_w2, L0_ffn_b2, L1_attn_W_DQ, L1_attn_W_UQ, L1_attn_W_QR, L1_attn_W_DKV, L1_attn_W_UK, L1_attn_W_UV, L1_attn_W_KR, L1_attn_W_O, L1_ffn_gate_w, L1_ffn_gate_proj_w, L1_ffn_up_proj_w, L1_ffn_down_proj_w):

    def _L0_attn_ref(x, past_kv, W_qkv, gn_weight, gn_bias):
        import jax, jax.numpy as jnp
        import numpy as np
        B, T, C, NH = (8, 128, 128, 16)
        HD = C // NH
        EPS = 1e-05

        def _decay_mask(nh, t, dtype):
            gamma = 1.0 - 2.0 ** (-5.0 - jnp.arange(nh, dtype=jnp.float32))
            idx = jnp.arange(t)
            diff = idx[:, None] - idx[None, :]
            mask = diff >= 0
            pow_ = gamma[:, None, None] ** jnp.where(mask, diff, 0).astype(jnp.float32)
            return (jnp.where(mask[None], pow_, 0.0).astype(dtype), gamma.astype(dtype))

        def _reference_tuple_inner(x, past_kv, W_qkv, gn_weight, gn_bias):
            b, t, c = x.shape
            nh = gn_weight.shape[0]
            hd = c // nh
            qkv = x @ W_qkv
            q, k, v = jnp.split(qkv, 3, axis=2)
            split_heads = lambda u: u.reshape(b, t, nh, hd).transpose(0, 2, 1, 3)
            q, k, v = (split_heads(q), split_heads(k), split_heads(v))
            decay, gamma = _decay_mask(nh, t, x.dtype)
            ret = jnp.einsum('bhtd,bhsd->bhts', q, k) * decay
            inner = jnp.einsum('bhts,bhsd->bhtd', ret, v)
            inner_decay = float(nh * hd)
            cross = jnp.einsum('bhtd,hde->bhte', q, past_kv) * inner_decay
            r = inner + cross
            current_kv = gamma[:, None, None] * past_kv + jnp.einsum('bhtd,bhte->bhde', k, v)
            current_kv = current_kv.mean(axis=0)
            y = r.transpose(0, 1, 3, 2)
            mu = y.mean(axis=(1, 2, 3), keepdims=True)
            var = y.var(axis=(1, 2, 3), keepdims=True)
            yn = (y - mu) * jax.lax.rsqrt(var + EPS)
            yn = yn * gn_weight[None, :, None, None] + gn_bias[None, :, None, None]
            out = yn.transpose(0, 3, 1, 2).reshape(b, t, c)
            return (out, current_kv)
        return _reference_tuple_inner(x, past_kv, W_qkv, gn_weight, gn_bias)[0]

    def _L0_ffn_ref(x, w_router, b_router, w1, b1, w2, b2):
        import jax, jax.numpy as jnp
        import numpy as np
        N_BLOCKS = 16
        BLOCK = 32
        TOP_K = N_BLOCKS // 4
        orig_shape = x.shape
        D = orig_shape[-1]
        xf = x.reshape(-1, D)
        prob = jax.nn.softmax(xf @ w_router + b_router, axis=-1)
        _, idx = jax.lax.top_k(prob, TOP_K)
        mask = (idx[:, :, None] == jnp.arange(N_BLOCKS)[None, None, :]).any(axis=1)
        mask = mask.astype(x.dtype)
        w1b = w1.reshape(N_BLOCKS, BLOCK, D)
        b1b = b1.reshape(N_BLOCKS, BLOCK)
        w2b = jnp.transpose(w2.reshape(D, N_BLOCKS, BLOCK), (1, 2, 0))
        h = jax.nn.relu(jnp.einsum('nd,ebd->neb', xf, w1b) + b1b[None])
        y = jnp.einsum('neb,ebd,ne->nd', h, w2b, mask)
        y = y + b2[None, :]
        return y.reshape(orig_shape)

    def _L1_attn_ref(x, W_DQ, W_UQ, W_QR, W_DKV, W_UK, W_UV, W_KR, W_O):
        import jax, jax.numpy as jnp
        import numpy as np
        D_MODEL, N_HEADS = (128, 16)
        D_H = D_MODEL // N_HEADS
        D_HR = D_H // 2
        D_LATENT = 32
        THETA = 10000.0

        def rope(x, theta=THETA):
            S, d = (x.shape[-2], x.shape[-1])
            inv = theta ** (-jnp.arange(0, d, 2, dtype=jnp.float32) / d)
            ang = jnp.arange(S, dtype=jnp.float32)[:, None] * inv
            cos, sin = (jnp.cos(ang), jnp.sin(ang))
            x1, x2 = (x[..., 0::2], x[..., 1::2])
            r1 = x1 * cos - x2 * sin
            r2 = x1 * sin + x2 * cos
            return jnp.stack([r1, r2], axis=-1).reshape(x.shape)
        B, S, _ = x.shape
        d_qk = D_H + D_HR
        c_q = x @ W_DQ
        Qc = (c_q @ W_UQ).reshape(B, S, N_HEADS, D_H).transpose(0, 2, 1, 3)
        Qr = (c_q @ W_QR).reshape(B, S, N_HEADS, D_HR).transpose(0, 2, 1, 3)
        Qr = rope(Qr)
        c_kv = x @ W_DKV
        Kc = (c_kv @ W_UK).reshape(B, S, N_HEADS, D_H).transpose(0, 2, 1, 3)
        Kr = rope((x @ W_KR)[:, None, :, :])
        Kr = jnp.broadcast_to(Kr, (B, N_HEADS, S, D_HR))
        V = (c_kv @ W_UV).reshape(B, S, N_HEADS, D_H).transpose(0, 2, 1, 3)
        Q = jnp.concatenate([Qc, Qr], axis=-1)
        K = jnp.concatenate([Kc, Kr], axis=-1)
        scores = jnp.einsum('bhqd,bhkd->bhqk', Q, K)
        scores = jnp.clip(scores, -80.0, 80.0)
        causal = jnp.tril(jnp.ones((S, S), dtype=bool))
        scores = jnp.where(causal, scores, -jnp.inf)
        weights = jax.nn.softmax(scores / jnp.sqrt(jnp.float32(d_qk)), axis=-1)
        attn = jnp.einsum('bhqk,bhkd->bhqd', weights, V)
        attn = attn.transpose(0, 2, 1, 3).reshape(B, S, N_HEADS * D_H)
        return attn @ W_O

    def _L1_ffn_ref(x, gate_w, gate_proj_w, up_proj_w, down_proj_w):
        import jax, jax.numpy as jnp
        import numpy as np
        NUM_EXPERTS = 8
        TOP_K = 2
        CAPACITY_FACTOR = 1.25
        B, S, D = x.shape
        E, K = (NUM_EXPERTS, TOP_K)
        T = B * S
        xf = x.reshape(T, D)
        logits = xf @ gate_w.T
        probs = jax.nn.softmax(logits, axis=-1)
        top_p, top_i = jax.lax.top_k(probs, K)
        w = top_p / (jnp.sum(top_p, axis=-1, keepdims=True) + 1e-09)
        capacity = int(CAPACITY_FACTOR * T / E)
        oh = jax.nn.one_hot(top_i, E, dtype=jnp.int32)
        rank = jnp.cumsum(oh, axis=0) - 1
        my_rank = jnp.sum(rank * oh, axis=-1)
        keep = (my_rank < capacity).astype(w.dtype)
        comb = jnp.einsum('tk,tke->te', w * keep, oh.astype(w.dtype))
        out = jnp.zeros_like(xf)
        for e in range(E):
            g = jax.nn.silu(xf @ gate_proj_w[e].T)
            u = xf @ up_proj_w[e].T
            y = g * u @ down_proj_w[e].T
            out = out + comb[:, e:e + 1] * y
        return out.reshape(B, S, D)
    x = L0_attn_x
    x = x + _L0_attn_ref(_layernorm(x, axis=-1), L0_attn_past_kv, L0_attn_W_qkv, L0_attn_gn_weight, L0_attn_gn_bias)
    x = x + _L0_ffn_ref(_layernorm(x, axis=-1), L0_ffn_w_router, L0_ffn_b_router, L0_ffn_w1, L0_ffn_b1, L0_ffn_w2, L0_ffn_b2)
    x = x + _L1_attn_ref(_layernorm(x, axis=-1), L1_attn_W_DQ, L1_attn_W_UQ, L1_attn_W_QR, L1_attn_W_DKV, L1_attn_W_UK, L1_attn_W_UV, L1_attn_W_KR, L1_attn_W_O)
    x = x + _L1_ffn_ref(_layernorm(x, axis=-1), L1_ffn_gate_w, L1_ffn_gate_proj_w, L1_ffn_up_proj_w, L1_ffn_down_proj_w)
    return x

_drawn_inputs = setup_inputs


def setup_inputs(seed=0):
    import zlib

    import numpy as np

    out = dict(_drawn_inputs(seed))
    spreads = {'L0_attn_gn_weight': (1.0, 0.2), 'L0_attn_gn_bias': (0.0, 0.1)}
    factors = {'L0_ffn_b_router': 6.443,
     'L0_ffn_b1': 8.0,
     'L0_ffn_b2': 6.974,
     'L1_ffn_gate_w': 8.0,
     'L1_ffn_gate_proj_w': 8.0,
     'L1_ffn_up_proj_w': 8.0,
     'L1_ffn_down_proj_w': 8.0}
    for name, (base, spread) in spreads.items():
        noise = np.random.default_rng([zlib.crc32(name.encode()), seed]).standard_normal(out[name].shape)
        drawn = base * np.exp(spread * noise) if base else spread * noise
        out[name] = jnp.asarray(drawn.astype(out[name].dtype))
    for name, factor in factors.items():
        out[name] = (out[name] * factor).astype(out[name].dtype)
    return out
```

```python
import concourse.bass as bass
from concourse import mybir
from contextlib import ExitStack
import numpy as np

B, T, D = 8, 512, 128
TOK = 128
NT = T // TOK
NH, HD = 16, 8
ROPE = 4
HROW = HD + ROPE
LAT = 32
NBLK, TOPB, HID0 = 16, 4, 512
NE, TOPE, HID1 = 8, 2, 256
CAP = int(1.25 * B * T / NE)
NQ = TOPE * NE
SLOTS = NQ * CAP
CT = CAP // TOK
HALF = CAP // 2
EPS = 1e-5
DROP = 2.0 ** 100
CLIP = 80.0
PAST_END = float(2 ** 15)
QK_SCALE = 1.0 / float(np.sqrt(np.float32(HROW)))
P_LO = float(np.exp(-CLIP * QK_SCALE))
P_HI = float(np.exp(CLIP * QK_SCALE))


def constants():
    f = np.float32
    gamma = 1.0 - 2.0 ** (-5.0 - np.arange(NH, dtype=np.float64))
    t = np.arange(TOK)
    diff = t[None, :] - t[:, None]
    decay = np.where(diff[:, None, :] >= 0, gamma[None, :, None] ** np.maximum(diff, 0)[:, None, :], 0.0)
    head = np.arange(D) // HD
    cos, sin = np.ones((2, 100, T)), np.zeros((2, 100, T))
    inv = (np.float32(10000.0) ** (-np.arange(0, ROPE, 2, dtype=f) / f(ROPE))).astype(f)
    ang = (np.arange(T, dtype=f)[None, :] * inv[:, None]).astype(f).astype(np.float64)
    for r in range(9):
        for i in range(ROPE):
            row = r * HROW + HD + i if r < 8 else 8 * HROW + i
            cos[:, row] = np.cos(ang[i // 2])
            sin[:, row] = np.sin(ang[i // 2]) * (-1.0 if i % 2 == 0 else 1.0)
    pick = np.zeros((D, 8 * HD + 8))
    for g in range(4):
        for s in range(2):
            for e in range(HD):
                pick[32 * g + 8 * s + e, HD * (4 * s + g) + e] = 1.0
            pick[32 * g + 16 + s, 8 * HD + 4 * s + g] = 1.0
    blocks = np.zeros((NBLK, HID0))
    for n in range(NBLK):
        blocks[n, n * 32:(n + 1) * 32] = DROP
    return {
        "c_decay": decay.astype(f),
        "c_qdecay": (gamma[head][:, None] ** t[None, :]).astype(f),
        "c_kdecay": (gamma[head][None, :] ** (TOK - t)[:, None]).astype(f),
        "c_gtile": (gamma[head] ** TOK).astype(f)[:, None],
        "c_heads": (head[:, None] == head[None, :]).astype(f),
        "c_lane": (head[:, None] % 4 == np.arange(4)[None, :]).astype(f),
        "c_cos": cos.astype(f), "c_sin": sin.astype(f),
        "c_pick": pick.astype(f),
        "c_blocks": blocks.astype(f),
        "c_ident": np.eye(D, dtype=f),
        "c_causal": (P_HI * (diff >= 0)).astype(f),
        "c_upto": (diff >= 0).astype(f),
        "c_iota": np.tile(np.arange(NBLK, dtype=f)[None, :], (D, 1)),
        "c_queue": np.tile(np.array([-1.0 + k * NE * CAP for k in range(TOPE)], f)[None, :], (D, 1)),
    }


USES = [("xnT0", 0), ("qT", 1), ("kT", 2), ("v", 0), ("ktm", 1), ("ret", 3), ("kv0", 2), ("kv1", 0), ("kv2", 1),
        ("gn", 2), ("retT", 0), ("xnT1", 1), ("router", 2), ("h0", 0), ("h1", 1), ("dropT", 3), ("h2", 2), ("h3", 3),
        ("y0", 0), ("xnT2", 1), ("cT", 2), ("qa0", 0), ("qb0", 1), ("qa1", 2), ("qb1", 3), ("kn", 0), ("vv", 1),
        ("u0", 3), ("u1", 2), ("om0", 0), ("om1", 1), ("onT", 0), ("y1", 1), ("xnT3", 0), ("gate", 2), ("rank", 3)]
BANK = dict(USES)
PER_BANK = [sum(b == k for _, b in USES) for k in range(4)]
NTH = {name: sum(b == BANK[name] for _, b in USES[:i]) for i, (name, _) in enumerate(USES)}
BY_PV = ("u0", "u1")
FULL_PER_BANK = [sum(b == k for n, b in USES if n not in BY_PV) for k in range(4)]
FULL_NTH = {name: sum(b == BANK[name] for n, b in USES[:i] if n not in BY_PV) for i, (name, _) in enumerate(USES)}
RET_UNITS, QUADS, QUAD_UNITS = 2 * NT, NH // 4, 5
V_STEPS = 123
UNITS = RET_UNITS + QUADS * QUAD_UNITS


def network(nc, io, out):
    f32, f32r, bf16 = mybir.dt.float32, mybir.dt.float32r, mybir.dt.bfloat16
    i32, u32 = mybir.dt.int32, mybir.dt.uint32
    ALU, ACT, AX = mybir.AluOpType, mybir.ActivationFunctionType, mybir.AxisListType
    V, S, PE, G = nc.vector, nc.scalar, nc.tensor, nc.gpsimd
    ctx = ExitStack()
    with ctx:
        def sb(name, shape, dt=f32):
            return ctx.enter_context(nc.sbuf_tensor(name, shape, dt))

        def sem(name):
            return ctx.enter_context(nc.semaphore(name))

        def dram(name, shape):
            return nc.dram_tensor(name, shape, f32, kind="Internal").ap()

        q_rows = dram("q_rows", [NH, 2, HROW, T])
        k_rows = dram("k_rows", [NH, 2, HROW, T])
        queue_x = dram("queue_x", [SLOTS, D])
        queue_y = dram("queue_y", [SLOTS, D])
        x_mid = dram("x_mid", [B, TOK, NT * D])

        decay = sb("decay", [TOK, NH, TOK])
        qdecay = sb("qdecay", [D, TOK])
        kdecay = sb("kdecay", [TOK, D])
        gtile = sb("gtile", [D, 1])
        heads = sb("heads", [D, D])
        lane = sb("lane", [D, 4])
        cos, sin = sb("cos", [100, 2, T]), sb("sin", [100, 2, T])
        pick, ident = sb("pick", [D, 8 * HD + 8]), sb("ident", [D, D])
        blocks32, blocks = sb("blocks32", [NBLK, HID0]), sb("blocks", [NBLK, HID0], bf16)
        causal = sb("causal", [TOK, TOK])
        upto32, upto = sb("upto32", [TOK, TOK]), sb("upto", [TOK, TOK], bf16)
        ones = sb("ones", [TOK, TOK], bf16)
        mean_of = sb("mean_of", [D, D])
        ones_row = sb("ones_row", [1, TOK])
        iota = sb("iota", [D, NBLK])
        queue_of = sb("queue_of", [D, TOPE])
        wqkv = sb("wqkv", [D, 3 * D])
        past, past_in = sb("past", [D, D]), sb("past_in", [D, D])
        gn_w, gn_b = sb("gn_w", [D, 1]), sb("gn_b", [D, 1])
        w_router, b_router = sb("w_router", [D, NBLK]), sb("b_router", [1, NBLK])
        w1, b1 = sb("w1", [D, HID0]), sb("b1", [D, 4])
        w2, b2 = sb("w2", [D, 4, D]), sb("b2", [1, D])
        w_down = sb("w_down", [D, 2 * LAT])
        wqa, wqb = sb("wqa", [LAT, 2, 96]), sb("wqb", [LAT, 2, 96])
        wukv = sb("wukv", [2 * LAT, 2 * D])
        wkr = sb("wkr", [D, 2, ROPE])
        wo = sb("wo", [D, D])
        w_gate = sb("w_gate", [D, NE])

        x_in = sb("x_in", [TOK, NT, D])
        xr = sb("xr", [TOK, NT, D])
        xn = sb("xn", [TOK, NT, D])
        xn3 = sb("xn3", [TOK, NT, D])
        xnT = sb("xnT", [D, T])
        stats, mv = sb("stats", [TOK, NT, 6]), sb("mv", [TOK, NT, 2])
        nv, ny, na = sb("nv", [TOK, NT]), sb("ny", [TOK, NT]), sb("na", [TOK, NT])
        gstat, gsum = sb("gstat", [D, 2]), sb("gsum", [D, 2])
        gscale, gbias, gtmp = sb("gscale", [D, 1]), sb("gbias", [D, 1]), sb("gtmp", [D, 1])
        fence_v, credit, pool_one = sb("fence_v", [1, 1]), sb("credit", [1, 2]), sb("pool_one", [1, 1])
        qT, kT = sb("qT", [D, T]), sb("kT", [D, T])
        q_lanes = sb("q_lanes", [D, NT, 4, TOK])
        q_dec = sb("q_dec", [D, NT, TOK])
        v_tm, k_dec = sb("v_tm", [TOK, NT, D]), sb("k_dec", [TOK, NT, D])
        v_lanes = sb("v_lanes", [TOK, NT, 4, D])
        probs = sb("probs", [TOK, 2, NH, TOK])
        state, kv_own = sb("state", [D, 3, D]), sb("kv_own", [D, D])
        retT = sb("retT", [D, T])
        logits = sb("logits", [TOK, NT, NBLK])
        top, top_i, top_f = sb("top", [TOK, NT, 8]), sb("top_i", [TOK, NT, 8], u32), sb("top_f", [TOK, NT, TOPB])
        hits, dropped = sb("hits", [TOK, NT, NBLK, TOPB]), sb("dropped", [TOK, NT, NBLK])
        dropT = sb("dropT", [NBLK, T], bf16)
        hidden = q_lanes[:].rearrange("p c r t -> p c (r t)")
        cT = sb("cT", [2 * LAT, T])
        rot_a = probs[0:100, 0, 0:8, :].rearrange("p (i a) t -> p i (a t)", i=2)
        rot_b = probs[0:100, 1, 0:8, :].rearrange("p (i a) t -> p i (a t)", i=2)
        rot_s = rot_a
        q_hi, q_lo = sb("q_hi", [100, 2, T], f32r), sb("q_lo", [100, 2, T], f32r)
        k_hi, k_lo = sb("k_hi", [D, T], f32r), sb("k_lo", [D, T], f32r)
        qs, ks = sb("qs", [D, NH // 2, T], f32r), sb("ks", [D, NH // 2, T], f32r)
        vv = sb("vv", [TOK, NT, 2, 4, 2, 32])
        pt = sb("pt", [TOK, 2, QUAD_UNITS, 1024])
        u_sb, o_tm, oT = sb("u_sb", [D, 2, T]), sb("o_tm", [TOK, NT, D]), sb("oT", [D, T])
        den_r = sb("den_r", [TOK, 2, NT, 8])
        glog = sb("glog", [TOK, NT, NE])
        etop, eidx = sb("etop", [TOK, NT, 8]), sb("eidx", [TOK, NT, 8], u32)
        eidf = sb("eidf", [TOK, NT, TOPE])
        esub, eexp = sb("esub", [TOK, NT, 8]), sb("eexp", [TOK, NT, 8])
        esum, ew, edn = sb("esum", [TOK, NT]), sb("ew", [TOK, NT, TOPE]), sb("edn", [TOK, NT])
        oh = sb("oh", [TOK, NT, TOPE, NE], bf16)
        oh_cnt = sb("oh_cnt", [TOK, NQ])
        oh_past = sb("oh_past", [TOK, NQ], bf16)
        rank_oh, rank = sb("rank_oh", [TOK, NT, TOPE, NE]), sb("rank", [TOK, NT, TOPE])
        keep, slot = sb("keep", [TOK, NT, TOPE]), sb("slot", [TOK, NT, TOPE])
        oh_row = sb("oh_row", [TOK, NQ])
        route = sb("route", [TOK, 2, NT * TOPE])
        put_at = sb("put_at", [TOK, NT, TOPE], u32)
        route_all = sb("route_all", [TOK, B, 2 * NT * TOPE])

        late = pt[:].rearrange("p a u c -> p (a u c)")
        taken = [0]

        def part_of_late(*shape):
            size = int(np.prod(shape))
            at = taken[0]
            taken[0] += size
            assert taken[0] <= 2 * QUAD_UNITS * 1024
            names = "abc"[:len(shape)]
            return late[:, at:at + size].rearrange(f"p ({' '.join(names)}) -> p {' '.join(names)}",
                                                   **dict(zip(names, shape)))

        wg, wu, wd = part_of_late(2, HID1), part_of_late(2, HID1), part_of_late(2, 2, D)
        xq, xqT = part_of_late(2, CT, D), part_of_late(2, CAP)
        act_g, act_h = part_of_late(2, HALF), part_of_late(2, 2, CAP)
        yq = part_of_late(2, CT, D)
        get_at, w_now = sb("get_at", [TOK, NT * TOPE], u32), sb("w_now", [TOK, NT * TOPE])
        y_got = v_lanes[:].rearrange("p j a d -> p (j a) d")[:, 0:NT * TOPE, :].rearrange("p (j k) d -> p j k d", j=NT)
        y_part, y_out, x_late = xn, xn3, xr

        ps_score = ctx.enter_context(nc.psum_tensor("ps_score", [128, 2, 1024], f32))
        ps_work = ctx.enter_context(nc.psum_tensor("ps_work", [128, 4, 512], f32))
        xqT_psum = ps_work[:, 0:2, :].rearrange("p a c -> p (a c)")
        y_ps = ps_work[:, 2:4, :].rearrange("p a c -> p (a c)")


        const_in, x_got, past_got = sem("const_in"), sem("x_got"), sem("past_got")
        setup_v, setup_g, setup_s = sem("setup_v"), sem("setup_g"), sem("setup_s")
        queue_zeroed = sem("queue_zeroed")
        full = [sem(f"bank_full{k}") for k in range(4)]
        free = [sem(f"bank_free{k}") for k in range(4)]
        sc_full = [sem(f"score_full{k}") for k in range(2)]
        sc_free = [sem(f"score_free{k}") for k in range(2)]
        v_step = sem("vector_step")
        xn_ready = sem("xn_ready")
        qlanes_ready, qdec_ready, vlanes_ready = sem("qlanes_ready"), sem("qdec_ready"), sem("vlanes_ready")
        state_ready, chunk_done = sem("state_ready"), sem("chunk_done")
        gstat_ready, gaff_ready, drop_ready = sem("gstat_ready"), sem("gaff_ready"), sem("drop_ready")
        rotsum_ready, qhi_ready, qlo_ready, khi_ready = (sem("rotsum_ready"), sem("qhi_ready"), sem("qlo_ready"),
                                                         sem("khi_ready"))
        rows_out, rows_in = sem("rows_out"), sem("rows_in")
        pt_ready, pv_done = sem("pt_ready"), sem("pv_done")
        x3_kept, esub_ready, eexp_ready, oh_ready = sem("x3_kept"), sem("esub_ready"), sem("eexp_ready"), sem("oh_ready")
        route_ready, route_kept = sem("route_ready"), sem("route_kept")
        fence_g, scattered = sem("fence_g"), sem("scattered")
        wexp_in, xq_in, y_kept = ([sem(f"{name}{w}") for w in range(2)] for name in ("wexp_in", "xq_in", "y_kept"))
        xqT_ps, xqT_ready = sem("xqT_ps"), sem("xqT_ready")
        gu_free, queue_done = sem("gate_up_free"), sem("queue_done")
        gu_full, silu_ready, y_ready = sem("gate_up_full"), sem("silu_ready"), sem("y_ready")
        at_ready, got, part_ready, sum_ready, out_done = (sem("at_ready"), sem("got"), sem("part_ready"),
                                                          sem("sum_ready"), sem("out_done"))

        block = ctx.enter_context(nc.Block())

        def bank(name):
            return ps_work[:, BANK[name], :]

        def filled(b, name):
            return full[BANK[name]], b * FULL_PER_BANK[BANK[name]] + FULL_NTH[name] + 1

        def opened(b, name):
            return free[BANK[name]], b * PER_BANK[BANK[name]] + NTH[name]

        def emptied(b, name):
            return free[BANK[name]], b * PER_BANK[BANK[name]] + NTH[name] + 1

        def unit_filled(b, n):
            return sc_full[n % 2], b * (UNITS // 2) + n // 2 + 1

        def unit_opened(b, n):
            return sc_free[n % 2], b * (UNITS // 2) + n // 2

        def unit_emptied(b, n):
            return sc_free[n % 2], b * (UNITS // 2) + n // 2 + 1

        def tiles(ap):
            return ap.rearrange("p (j c) -> p j c", j=NT)

        def tile_of(j, width=TOK):
            return slice(j * width, (j + 1) * width)

        consts = [(wqkv[:], io["wqkv"]), (ident[:], io["c_ident"]), (lane[:], io["c_lane"]),
                  (qdecay[:], io["c_qdecay"]), (kdecay[:], io["c_kdecay"]), (decay[:], io["c_decay"]),
                  (gtile[:], io["c_gtile"]), (heads[:], io["c_heads"]), (gn_w[:], io["gn_w"]), (gn_b[:], io["gn_b"]),
                  (cos[:], io["c_cos"].rearrange("i p t -> p i t")), (sin[:], io["c_sin"].rearrange("i p t -> p i t")),
                  (pick[:], io["c_pick"]), (blocks32[:], io["c_blocks"]),
                  (causal[:], io["c_causal"]), (upto32[:], io["c_upto"]), (iota[:], io["c_iota"]),
                  (queue_of[:], io["c_queue"]),
                  (w_router[:], io["w_router"]), (b_router[:], io["b_router"]), (w1[:], io["w1"]), (b1[:], io["b1"]),
                  (w2[:], io["w2"].rearrange("(m p) d -> p m d", m=4)), (b2[:], io["b2"]), (w_down[:], io["w_down"]),
                  (wqa[:], io["wqa"].rearrange("l (i r) -> l i r", i=2)),
                  (wqb[:], io["wqb"].rearrange("l (i r) -> l i r", i=2)),
                  (wukv[LAT:2 * LAT, :], io["wukv"]), (wkr[:], io["wkr"].rearrange("p (a r) -> p a r", a=2)),
                  (wo[:], io["wo"]), (w_gate[:], io["w_gate"])]
        N_CONST = 16 * len(consts)
        x_rows = io["x"].rearrange("b (j p) c -> b p j c", p=TOK)
        out_rows = out.rearrange("b (j p) c -> b p j c", p=TOK)
        queue_x_n = queue_x.rearrange("(n p j) c -> n p (j c)", p=TOK, j=CT)
        queue_y_n = queue_y.rearrange("(n p j) c -> n p (j c)", p=TOK, j=CT)

        @block.sync
        def _(sp):
            sp.dma_start(x_in[:], x_rows[0]).then_inc(x_got, 16)
            for dst, src in consts:
                sp.dma_start(dst, src).then_inc(const_in, 16)
            sp.wait_ge(setup_g, 1)
            for h in range(NH):
                r = slice(HD * h, HD * h + HD)
                sp.dma_start(past_in[r, r], io["past_kv"][h]).then_inc(past_got, 16)
            sp.wait_ge(setup_g, 2)
            for z in range(SLOTS // 1024):
                sp.dma_start(queue_x[1024 * z:1024 * z + 1024, :].rearrange("(p r) c -> p (r c)", r=8),
                             late[:, 0:1024]).then_inc(queue_zeroed, 16)

            def row(b, last):
                if not last:
                    sp.wait_ge(*emptied(b, "retT"))
                    sp.dma_start(x_in[:], x_rows[b + 1]).then_inc(x_got, 16)
                sp.wait_ge(rows_in, 128 * b)
                for i in range(2):
                    hs = slice(8 * i, 8 * i + 8)
                    sp.wait_ge(qhi_ready, 2 * b + i + 1)
                    sp.dma_start(q_rows[hs, 0, :, :], q_hi[0:96, i, :].bitcast(f32)).then_inc(rows_out, 16)
                    sp.wait_ge(qlo_ready, 2 * b + i + 1)
                    sp.dma_start(q_rows[hs, 1, :, :], q_lo[0:96, i, :].bitcast(f32)).then_inc(rows_out, 16)
                for part, rope_rows in ((0, q_hi), (1, q_lo)):
                    sp.dma_start(k_rows[:, part, HD:HROW, :].rearrange("h d t -> d h t"),
                                 rope_rows[96:100, 1, :].bitcast(f32).unsqueeze(1).to_broadcast([ROPE, NH, T]))\
                      .then_inc(rows_out, 16)
                sp.wait_ge(khi_ready, b + 1)
                sp.dma_start(k_rows[:, 0, 0:HD, :], k_hi[:].bitcast(f32)).then_inc(rows_out, 16)
                sp.wait_ge(*emptied(b, "kn"))
                sp.dma_start(k_rows[:, 1, 0:HD, :], k_lo[:].bitcast(f32)).then_inc(rows_out, 16)
                sp.wait_ge(rows_out, 128 * (b + 1))
                for i in range(2):
                    at, hs = 64 * i, slice(8 * i, 8 * i + 8)
                    sp.dma_start(qs[at:at + 24, :, :].bitcast(f32),
                                 q_rows[hs].rearrange("h a d t -> h (a d) t").rearrange("h r t -> r h t"))\
                      .then_inc(rows_in, 16)
                    sp.dma_start(qs[at + 24:at + 36, :, :].bitcast(f32), q_rows[hs, 0].rearrange("h r t -> r h t"))\
                      .then_inc(rows_in, 16)
                    sp.dma_start(ks[at:at + 12, :, :].bitcast(f32), k_rows[hs, 0].rearrange("h r t -> r h t"))\
                      .then_inc(rows_in, 16)
                    sp.dma_start(ks[at + 12:at + 36, :, :].bitcast(f32),
                                 k_rows[hs].rearrange("h a d t -> h (a d) t").rearrange("h r t -> r h t"))\
                      .then_inc(rows_in, 16)
                sp.wait_ge(*emptied(b, "y1"))
                sp.dma_start(x_mid[b], xr[:].rearrange("p j c -> p (j c)")).then_inc(x3_kept, 16)
                sp.wait_ge(route_ready, b + 1)
                sp.dma_start(route_all[:, b, :], route[:].rearrange("p a c -> p (a c)")).then_inc(route_kept, 16)

            with sp.Fori(0, B - 1) as b:
                row(b, False)
            row(B - 1, True)

            sp.wait_ge(scattered, 16 * TOPE * NT * B)
            for k in range(TOPE):
                with sp.Fori(0, NE // 2) as i:
                    for w in range(2):
                        n = NE * k + 2 * i + w
                        sp.wait_ge(queue_done, n + 1)
                        sp.dma_start(xq[:, w, :, :].rearrange("p j c -> p (j c)"), queue_x_n[n]).then_inc(xq_in[w], 16)
                        sp.dma_start(wg[:, w, :], io["w_eg"][2 * i + w]).then_inc(wexp_in[w], 16)
                        sp.dma_start(wu[:, w, :], io["w_eu"][2 * i + w]).then_inc(wexp_in[w], 16)
                        sp.dma_start(wd[:, w, :, :].rearrange("p m d -> p (m d)"), io["w_ed"][2 * i + w])\
                          .then_inc(wexp_in[w], 16)
            sp.wait_ge(x3_kept, 16 * B)
            with sp.Fori(0, B) as b:
                sp.wait_ge(part_ready, b)
                sp.dma_start(x_late[:].rearrange("p j c -> p (j c)"), x_mid[b]).then_inc(x_got, 16)
                sp.wait_ge(sum_ready, b + 1)
                sp.dma_start(out_rows[b], y_out[:]).then_inc(out_done, 16)
            sp.wait_ge(out_done, 16 * B)

        @block.gpsimd
        def _(pool):
            G.memset(past_in[:], 0.0).then_inc(setup_g, 1)
            G.memset(late[:, 0:1024], 0.0).then_inc(setup_g, 1)
            G.memset(ones[:], 1.0).then_inc(setup_g, 1)
            G.memset(mean_of[:], 1.0 / D).then_inc(setup_g, 1)
            G.memset(ones_row[:], 1.0).then_inc(setup_g, 1)
            G.memset(v_lanes[:], 0.0).then_inc(setup_g, 1)
            G.memset(vv[:], 0.0).then_inc(setup_g, 1)
            G.memset(pool_one[:], 0.0).then_inc(setup_g, 1)
            pool.wait_ge(setup_g, 8)
            for s in range(2):
                G.memset(vv[:, :, :, :, s, 16 + s:17 + s], 1.0).then_inc(setup_g, 1)
            with pool.Fori(0, B) as b:
                for i in range(2):
                    n = 96 + ROPE * i
                    pool.wait_ge(*emptied(b, f"qa{i}"))
                    pool.wait_ge(*emptied(b, f"qb{i}"))
                    G.tensor_tensor(rot_s[0:n, i, :], rot_a[0:n, i, :], rot_b[0:n, i, :], ALU.add)\
                     .then_inc(rotsum_ready, 1)
                for i in range(2):
                    n = 96 + ROPE * i
                    pool.wait_ge(qhi_ready, 2 * b + i + 1)
                    G.tensor_tensor(q_lo[0:n, i, :], rot_s[0:n, i, :], q_hi[0:n, i, :].bitcast(f32), ALU.subtract)\
                     .then_inc(qlo_ready, 1)
                pool.wait_ge(fence_g, b)
                pool.wait_ge(route_ready, b + 1)
                G.tensor_tensor(pool_one[:], pool_one[:], pool_one[:], ALU.add).then_inc(fence_g, 1)
                pool.wait_ge(queue_zeroed, 16 * (SLOTS // 1024))
                for j in range(NT):
                    for k in range(TOPE):
                        pool.indirect_dma_start(queue_x[:, :], bass.IndirectOffsetOnAxis(ap=put_at[:, j, k:k + 1], axis=0),
                                                xn3[:, j, :], None, bounds_check=SLOTS - 1, oob_is_err=False)\
                            .then_inc(scattered, 16)
            for w in range(2):
                pool.wait_ge(y_kept[w], 16 * NQ // 2)
            with pool.Fori(0, B) as b:
                pool.wait_ge(sum_ready, b)
                pool.wait_ge(fence_g, B + b)
                pool.wait_ge(at_ready, b + 1)
                G.tensor_tensor(pool_one[:], pool_one[:], pool_one[:], ALU.add).then_inc(fence_g, 1)
                for j in range(NT):
                    for k in range(TOPE):
                        pool.indirect_dma_start(y_got[:, j, k, :], None, queue_y[:, :],
                                                bass.IndirectOffsetOnAxis(ap=get_at[:, 2 * j + k:2 * j + k + 1], axis=0),
                                                bounds_check=SLOTS - 1, oob_is_err=False).then_inc(got, 16)

        @block.scalar
        def _(act):
            act.wait_ge(const_in, N_CONST)
            act.wait_ge(past_got, 16 * NH)
            act.wait_ge(queue_zeroed, 16 * (SLOTS // 1024))
            S.activation(past[:], past_in[:], ACT.Copy, scale=float(NH * HD)).then_inc(setup_s, 1)
            S.activation(blocks[:], blocks32[:], ACT.Copy).then_inc(setup_s, 1)
            S.activation(upto[:], upto32[:], ACT.Copy).then_inc(setup_s, 1)

            def copy_out(b, name, dst, src):
                act.wait_ge(*filled(b, name))
                S.activation(dst, src, ACT.Copy).then_inc(free[BANK[name]], 1)

            with act.Fori(0, B) as b:
                copy_out(b, "xnT0", xnT[:], bank("xnT0"))
                copy_out(b, "qT", qT[:], bank("qT"))
                copy_out(b, "kT", kT[:], bank("kT"))
                copy_out(b, "v", v_tm[:], tiles(bank("v")))
                act.wait_ge(gaff_ready, b + 1)
                S.activation(retT[:], bank("ret"), ACT.Identity, bias=gbias[:, 0:1], scale=gscale[:, 0:1])\
                 .then_inc(free[BANK["ret"]], 1)
                copy_out(b, "xnT1", xnT[:], bank("xnT1"))
                copy_out(b, "dropT", dropT[:], bank("dropT")[0:NBLK, :])
                for m in range(4):
                    act.wait_ge(*filled(b, f"h{m}"))
                    S.activation(hidden[:, m, :], bank(f"h{m}"), ACT.Relu, bias=b1[:, m:m + 1])\
                     .then_inc(free[BANK[f"h{m}"]], 1)
                copy_out(b, "xnT2", xnT[:], bank("xnT2"))
                copy_out(b, "cT", cT[:], bank("cT")[0:2 * LAT, :])
                for i in range(2):
                    n = 96 + ROPE * i
                    act.wait_ge(rotsum_ready, 2 * b + i + 1)
                    S.activation(q_hi[0:n, i, :], rot_s[0:n, i, :], ACT.Copy).then_inc(qhi_ready, 1)
                act.wait_ge(*filled(b, "kn"))
                S.activation(k_hi[:], bank("kn"), ACT.Copy).then_inc(khi_ready, 1)
                for q in range(QUADS):
                    for un in range(QUAD_UNITS):
                        n = RET_UNITS + QUAD_UNITS * q + un
                        if un == 0:
                            act.wait_ge(pv_done, QUADS * b + max(q - 1, 0))
                        act.wait_ge(*unit_filled(b, n))
                        S.activation(pt[:, q % 2, un, :], ps_score[:, n % 2, :], ACT.Exp, scale=QK_SCALE)\
                         .then_inc(sc_free[n % 2], 1)
                    if q >= 2:
                        u = q - 2
                        act.wait_ge(pv_done, QUADS * b + 2 * u + 2)
                        S.activation(u_sb[:, u, :], bank(f"u{u}"), ACT.Copy).then_inc(free[BANK[f"u{u}"]], 1)
                copy_out(b, "onT", oT[:], bank("onT"))
                copy_out(b, "xnT3", xnT[:], bank("xnT3"))
                act.wait_ge(esub_ready, b + 1)
                S.activation(eexp[:], esub[:], ACT.Exp).then_inc(eexp_ready, 1)

            for k in range(TOPE):
                with act.Fori(0, NE // 2) as i:
                    for w in range(2):
                        n = NE * k + 2 * i + w
                        for t in range(4):
                            act.wait_ge(gu_free, 4 * n + t + 1)
                            act.wait_ge(gu_full, 4 * n + t + 1)
                            S.activation(act_g[:, t % 2, :], ps_score[:, t % 2, 0:HALF], ACT.Silu)\
                             .then_inc(silu_ready, 1)
                        act.wait_ge(y_kept[w], 16 * (NE // 2 * k + i))
                        act.wait_ge(queue_done, n + 3)
                        S.activation(yq[:, w, :, :].rearrange("p j c -> p (j c)"), y_ps[:, 0:CAP], ACT.Copy)\
                         .then_inc(y_ready, 1)
                        act.wait_ge(y_ready, n + 1)
                        act.dma_start(queue_y_n[n], yq[:, w, :, :].rearrange("p j c -> p (j c)")).then_inc(y_kept[w], 16)

        @block.tensor
        def _(pe):
            pe.wait_ge(const_in, N_CONST)
            pe.wait_ge(setup_s, 3)
            pe.wait_ge(setup_g, 10)

            def full_inc(m, name):
                m.then_inc(full[BANK[name]], 1)

            def transposes(b, name, src):
                for j in range(NT):
                    m = PE.transpose(bank(name)[:, tile_of(j)], src(j), ident[:])
                full_inc(m, name)

            def norm_transposes(b, k, src):
                pe.wait_ge(*opened(b, f"xnT{k}"))
                pe.wait_ge(xn_ready, 4 * b + k + 1)
                transposes(b, f"xnT{k}", lambda j: src[:, j, :])

            def ret_scores(b, c):
                for u in range(2):
                    n = 2 * c + u
                    pe.wait_ge(*unit_opened(b, n))
                    for w in range(2):
                        g = 2 * u + w
                        r = slice(32 * g, 32 * g + 32)
                        m = PE.matmul(ps_score[:, n % 2, 512 * w:512 * w + 512], kT[r, tile_of(c)],
                                      q_lanes[r, c, :, :].rearrange("p r t -> p (r t)"), start=True, stop=True)
                    m.then_inc(sc_full[n % 2], 1)

            def ret_kv(b, c):
                pe.wait_ge(*opened(b, f"kv{c}"))
                full_inc(PE.matmul(bank(f"kv{c}")[:, 0:D], k_dec[:, c, :], v_tm[:, c, :], start=True, stop=True),
                         f"kv{c}")

            def ret_sum(b, c):
                ret = bank("ret")
                m = PE.matmul(ret[:, tile_of(c)], past[:], qT[:, tile_of(c)], start=True, stop=False)
                if c == 1:
                    pe.wait_ge(*emptied(b, "kv0"))
                if c >= 2:
                    pe.wait_ge(state_ready, 2 * b + c - 1)
                if c >= 1:
                    PE.matmul(ret[:, tile_of(c)], state[:, c - 1, :], q_dec[:, c, :], start=False, stop=False)
                pe.wait_ge(*unit_emptied(b, 2 * c))
                pe.wait_ge(*unit_emptied(b, 2 * c + 1))
                for r in range(4):
                    for g in range(4):
                        at = slice(32 * g, 32 * g + 32)
                        m = PE.matmul(ret[at, tile_of(c)], v_lanes[:, c, r, at], probs[:, c % 2, 4 * g + r, :],
                                      start=False, stop=(r == 3))
                if c < 2:
                    m.then_inc(chunk_done, 1)
                if c == NT - 1:
                    full_inc(m, "ret")

            def scores(b, q, un):
                n = RET_UNITS + QUAD_UNITS * q + un
                pe.wait_ge(*unit_opened(b, n))
                ps = ps_score[:, n % 2, :]

                def part(g, at, s, t0, t1):
                    h = 4 * q + g
                    r = slice(64 * (h // 8), 64 * (h // 8) + 36)
                    return PE.matmul(ps[:, at:at + t1 - t0], ks[r, h % 8, tile_of(s)], qs[r, h % 8, t0:t1],
                                     start=True, stop=True)

                if un < 4:
                    for s in range(NT):
                        part(un, TOK * s, s, TOK * s, TOK * s + TOK)
                    part(un, 512, 0, TOK, T)
                    m = part(un, 896, 2, 3 * TOK, T)
                else:
                    for g in range(4):
                        m = part(g, 256 * g, 1, 2 * TOK, T)
                m.then_inc(sc_full[n % 2], 1)

            def weigh(b, q):
                u, s = q // 2, q % 2
                acc = bank(f"u{u}")
                if s == 0:
                    pe.wait_ge(*opened(b, f"u{u}"))
                pe.wait_ge(pt_ready, QUADS * QUAD_UNITS * b + QUAD_UNITS * (q + 1))
                diag = [("d", i) for i in range(NT)]
                order = [diag[0], ("e", 0), diag[1], ("f", 1), diag[2], ("e", 2), diag[3]]
                for kind, j in order:
                    for g in range(4):
                        if kind == "d":
                            p, t0, t1 = pt[:, q % 2, g, tile_of(j)], TOK * j, TOK * j + TOK
                        elif kind == "f":
                            p, t0, t1 = pt[:, q % 2, 4, 256 * g:256 * g + 256], 2 * TOK, T
                        elif j == 0:
                            p, t0, t1 = pt[:, q % 2, g, 512:896], TOK, T
                        else:
                            p, t0, t1 = pt[:, q % 2, g, 896:1024], 3 * TOK, T
                        m = PE.matmul(acc[32 * g:32 * g + 32, t0:t1], vv[:, j, u, g, s, :], p,
                                      start=(s == 0 and kind == "d" and j == 0), stop=(s == 1 and kind == "d" and j == 3))
                m.then_inc(pv_done, 1)

            def turn_sums(b, u):
                pe.wait_ge(*opened(b, f"om{u}"))
                pe.wait_ge(*emptied(b, f"u{u}"))
                for j in range(NT):
                    m = PE.matmul(bank(f"om{u}")[:, 72 * j:72 * j + 72], u_sb[:, u, tile_of(j)], pick[:],
                                  start=True, stop=True)
                full_inc(m, f"om{u}")

            with pe.Fori(0, B) as b:
                norm_transposes(b, 0, xn)
                pe.wait_ge(*opened(b, "qT"))
                pe.wait_ge(*emptied(b, "xnT0"))
                full_inc(PE.matmul(bank("qT"), wqkv[:, 0:D], xnT[:], start=True, stop=True), "qT")
                pe.wait_ge(*opened(b, "kT"))
                full_inc(PE.matmul(bank("kT"), wqkv[:, D:2 * D], xnT[:], start=True, stop=True), "kT")
                for name, cols in (("v", slice(2 * D, 3 * D)), ("ktm", slice(D, 2 * D))):
                    pe.wait_ge(*opened(b, name))
                    for j in range(NT):
                        m = PE.matmul(bank(name)[:, tile_of(j)], xnT[:, tile_of(j)], wqkv[:, cols], start=True, stop=True)
                    full_inc(m, name)
                pe.wait_ge(qlanes_ready, b + 1)
                pe.wait_ge(*emptied(b, "kT"))
                ret_scores(b, 0)
                pe.wait_ge(*emptied(b, "v"))
                pe.wait_ge(*emptied(b, "ktm"))
                ret_kv(b, 0)
                pe.wait_ge(qdec_ready, b + 1)
                pe.wait_ge(vlanes_ready, b + 1)
                pe.wait_ge(*opened(b, "ret"))
                for c in range(NT):
                    if c + 1 < NT:
                        ret_scores(b, c + 1)
                    if c + 1 < NT - 1:
                        ret_kv(b, c + 1)
                    ret_sum(b, c)
                pe.wait_ge(*opened(b, "gn"))
                pe.wait_ge(gstat_ready, b + 1)
                full_inc(PE.matmul(bank("gn")[:, 0:2], mean_of[:], gstat[:], start=True, stop=True), "gn")
                pe.wait_ge(*opened(b, "retT"))
                pe.wait_ge(*emptied(b, "ret"))
                transposes(b, "retT", lambda j: retT[:, tile_of(j)])

                norm_transposes(b, 1, xn)
                pe.wait_ge(*opened(b, "router"))
                pe.wait_ge(*emptied(b, "xnT1"))
                for j in range(NT):
                    at = bank("router")[:, tile_of(j, NBLK)]
                    PE.matmul(at, xnT[:, tile_of(j)], w_router[:], start=True, stop=False)
                    m = PE.matmul(at, ones_row[:], b_router[:], start=False, stop=True)
                full_inc(m, "router")

                def hidden_units(k):
                    pe.wait_ge(*opened(b, f"h{k}"))
                    PE.matmul(bank(f"h{k}"), w1[:, tile_of(k)], xnT[:], start=True, stop=False)

                def drop_blocks(k):
                    full_inc(PE.matmul(bank(f"h{k}"), blocks[:, tile_of(k)], dropT[:], start=False, stop=True), f"h{k}")

                hidden_units(0)
                hidden_units(1)
                pe.wait_ge(*opened(b, "dropT"))
                pe.wait_ge(drop_ready, b + 1)
                for j in range(NT):
                    m = PE.matmul(bank("dropT")[0:NBLK, tile_of(j)], dropped[:, j, :], ident[:], start=True, stop=True)
                full_inc(m, "dropT")
                hidden_units(2)
                pe.wait_ge(*emptied(b, "dropT"))
                drop_blocks(0)
                drop_blocks(1)
                drop_blocks(2)
                hidden_units(3)
                drop_blocks(3)
                pe.wait_ge(*opened(b, "y0"))
                for k in range(4):
                    pe.wait_ge(*emptied(b, f"h{k}"))
                for j in range(NT):
                    at = bank("y0")[:, tile_of(j)]
                    for k in range(4):
                        PE.matmul(at, hidden[:, k, tile_of(j)], w2[:, k, :], start=(k == 0), stop=False)
                    m = PE.matmul(at, ones_row[:], b2[:], start=False, stop=True)
                full_inc(m, "y0")

                norm_transposes(b, 2, xn)
                pe.wait_ge(*opened(b, "cT"))
                pe.wait_ge(*emptied(b, "xnT2"))
                full_inc(PE.matmul(bank("cT")[0:2 * LAT, :], w_down[:], xnT[:], start=True, stop=True), "cT")
                for i in range(2):
                    for a, (name, weights) in enumerate(((f"qa{i}", wqa), (f"qb{i}", wqb))):
                        pe.wait_ge(*opened(b, name))
                        if i == 0 and a == 0:
                            pe.wait_ge(*emptied(b, "cT"))
                        m = PE.matmul(bank(name)[0:96, :], weights[:, i, :], cT[0:LAT, :], start=True, stop=True)
                        if i == 1:
                            m = PE.matmul(bank(name)[96:100, :], wkr[:, a, :], xnT[:], start=True, stop=True)
                        full_inc(m, name)
                pe.wait_ge(*opened(b, "kn"))
                full_inc(PE.matmul(bank("kn"), wukv[LAT:2 * LAT, 0:D], cT[LAT:2 * LAT, :], start=True, stop=True), "kn")
                pe.wait_ge(*opened(b, "vv"))
                for j in range(NT):
                    m = PE.matmul(bank("vv")[:, tile_of(j)], cT[LAT:2 * LAT, tile_of(j)], wukv[LAT:2 * LAT, D:2 * D],
                                  start=True, stop=True)
                full_inc(m, "vv")
                pe.wait_ge(rows_in, 128 * (b + 1))
                for q in range(QUADS):
                    for un in range(QUAD_UNITS):
                        scores(b, q, un)
                        if q and un == 1:
                            if q == 1:
                                pe.wait_ge(*emptied(b, "vv"))
                            weigh(b, q - 1)
                        if q == 3 and un == 3:
                            turn_sums(b, 0)
                weigh(b, QUADS - 1)
                turn_sums(b, 1)
                pe.wait_ge(*opened(b, "onT"))
                pe.wait_ge(*emptied(b, "om1"))
                transposes(b, "onT", lambda j: o_tm[:, j, :])
                pe.wait_ge(*opened(b, "y1"))
                pe.wait_ge(*emptied(b, "onT"))
                for j in range(NT):
                    m = PE.matmul(bank("y1")[:, tile_of(j)], oT[:, tile_of(j)], wo[:], start=True, stop=True)
                full_inc(m, "y1")

                norm_transposes(b, 3, xn3)
                pe.wait_ge(*opened(b, "gate"))
                pe.wait_ge(*emptied(b, "xnT3"))
                for j in range(NT):
                    m = PE.matmul(bank("gate")[:, tile_of(j, NE)], xnT[:, tile_of(j)], w_gate[:], start=True, stop=True)
                full_inc(m, "gate")
                pe.wait_ge(*opened(b, "rank"))
                pe.wait_ge(oh_ready, b + 1)
                for j in range(NT):
                    at = bank("rank")[:, tile_of(j, NQ)]
                    PE.matmul(at, upto[:], oh[:, j, :, :].rearrange("p k e -> p (k e)"), start=True, stop=False)
                    for i in range(j):
                        PE.matmul(at, ones[:], oh[:, i, :, :].rearrange("p k e -> p (k e)"), start=False, stop=False)
                    m = PE.matmul(at, ones[:], oh_past[:], start=False, stop=True)
                full_inc(m, "rank")

            for k in range(TOPE):
                with pe.Fori(0, NE // 2) as i:
                    for w in range(2):
                        n = NE * k + 2 * i + w
                        pe.wait_ge(xqT_ready, n)
                        pe.wait_ge(xq_in[w], 16 * (NE // 2 * k + i + 1))
                        for j in range(CT):
                            m = PE.transpose(xqT_psum[:, tile_of(j)], xq[:, w, j, :], ident[:])
                        m.then_inc(xqT_ps, 1)
                        pe.wait_ge(wexp_in[w], 48 * (NE // 2 * k + i + 1))
                        pe.wait_ge(xqT_ready, n + 1)
                        for t in range(4):
                            half, mm = t // 2, t % 2
                            pe.wait_ge(gu_free, 4 * n + t + 1)
                            x_half = xqT[:, w, HALF * half:HALF * half + HALF]
                            PE.matmul(ps_score[:, t % 2, 0:HALF], wg[:, w, tile_of(mm)], x_half, start=True, stop=True)
                            PE.matmul(ps_score[:, t % 2, 512:512 + HALF], wu[:, w, tile_of(mm)], x_half,
                                      start=True, stop=True).then_inc(gu_full, 1)
                        pe.wait_ge(y_ready, n)
                        pe.wait_ge(gu_free, 4 * n + 6)
                        for j in range(CT):
                            for mm in range(2):
                                m = PE.matmul(y_ps[:, tile_of(j)], act_h[:, w, mm, tile_of(j)], wd[:, w, mm, :],
                                              start=(mm == 0), stop=(mm == 1))
                        m.then_inc(queue_done, 1)

        @block.vector
        def _(v):
            V.memset(oh_cnt[:], 0.0).then_inc(setup_v, 1)
            V.memset(oh_past[:], 0.0).then_inc(setup_v, 1)
            V.memset(fence_v[:], 0.0).then_inc(setup_v, 1)
            V.memset(credit[:, 0:1], 0.0).then_inc(gu_free, 2)
            V.memset(credit[:, 1:2], 0.0).then_inc(queue_done, 2)
            v.wait_ge(setup_v, 3)
            v.wait_ge(const_in, N_CONST)
            v.wait_ge(setup_g, 10)
            steps = [0]

            def row(b):
                steps[0] = 0

                def link(ins):
                    steps[0] += 1
                    ins.then_inc(v_step, 1)
                    v.wait_ge(v_step, b * V_STEPS + steps[0])

                def fence():
                    steps[0] += 1
                    V.memset(fence_v[:], 0.0).then_inc(v_step, 1)

                def read(name, ins):
                    ins.then_inc(free[BANK[name]], 1)
                    v.wait_ge(*emptied(b, name))

                def rsqrt(y, x, a):
                    link(V.tensor_scalar(a.bitcast(i32), x.bitcast(i32), 1, None, ALU.logical_shift_right))
                    link(V.tensor_scalar(y.bitcast(i32), a.bitcast(i32), -1.0, float(0x5F3759DF), ALU.mult, ALU.add))
                    for _ in range(4):
                        link(V.tensor_tensor(a, y, y, ALU.mult))
                        link(V.scalar_tensor_tensor(out=a, in0=a, scalar=-0.5, in1=x, op0=ALU.mult, op1=ALU.mult))
                        link(V.scalar_tensor_tensor(out=y, in0=a, scalar=1.5, in1=y, op0=ALU.add, op1=ALU.mult))

                def layer_norm(dst, src):
                    for j in range(NT):
                        ins = V.bn_stats(stats[:, j, :], src[:, j, :])
                    link(ins)
                    fence()
                    for j in range(NT):
                        ins = V.bn_aggr(mv[:, j, :], stats[:, j, :])
                    link(ins)
                    link(V.tensor_scalar(nv[:], mv[:, :, 1], EPS, None, ALU.add))
                    rsqrt(ny[:], nv[:], na[:])
                    for j in range(NT):
                        ins = V.tensor_scalar(dst[:, j, :], src[:, j, :], mv[:, j, 0:1], ny[:, j:j + 1],
                                              ALU.subtract, ALU.mult)
                    ins.then_inc(xn_ready, 1)

                def over_tiles(ap):
                    return ap.unsqueeze(1).to_broadcast([TOK, NT, ap.shape[1]])

                v.wait_ge(x_got, 16 * (b + 1))
                layer_norm(xn, x_in)
                v.wait_ge(*emptied(b, "qT"))
                for r in range(4):
                    ins = V.tensor_scalar(q_lanes[:, :, r, :], tiles(qT[:]), lane[:, r:r + 1], None, ALU.mult)
                ins.then_inc(qlanes_ready, 1)
                V.tensor_tensor(q_dec[:], tiles(qT[:]), over_tiles(qdecay[:]), ALU.mult).then_inc(qdec_ready, 1)
                v.wait_ge(*filled(b, "ktm"))
                V.tensor_tensor(k_dec[:], tiles(bank("ktm")), over_tiles(kdecay[:]), ALU.mult)\
                 .then_inc(free[BANK["ktm"]], 1)
                v.wait_ge(*emptied(b, "v"))
                for r in range(4):
                    at = slice(8 * r, 8 * r + 8)
                    ins = V.tensor_copy(v_lanes[:, :, r, :].rearrange("p c (g w) -> p c g w", w=32)[:, :, :, at],
                                        v_tm[:].rearrange("p c (g w) -> p c g w", w=32)[:, :, :, at])
                ins.then_inc(vlanes_ready, 1)
                for c in range(NT):
                    if c >= 2:
                        v.wait_ge(chunk_done, 2 * b + c - 1)
                    for u in range(2):
                        n = 2 * c + u
                        v.wait_ge(*unit_filled(b, n))
                        V.tensor_tensor(probs[:, c % 2, 8 * u:8 * u + 8, :],
                                        ps_score[:, n % 2, :].rearrange("p (h t) -> p h t", h=8),
                                        decay[:, 8 * u:8 * u + 8, :], ALU.mult).then_inc(sc_free[n % 2], 1)
                    if c < NT - 1:
                        v.wait_ge(*filled(b, f"kv{c}"))
                        dst = state[:, 0, :] if c == 0 else kv_own[:]
                        read(f"kv{c}", V.tensor_tensor(dst, bank(f"kv{c}")[:, 0:D], heads[:], ALU.mult))
                        if c:
                            V.scalar_tensor_tensor(out=state[:, c, :], in0=state[:, c - 1, :], scalar=gtile[:, 0:1],
                                                   in1=kv_own[:], op0=ALU.mult, op1=ALU.add).then_inc(state_ready, 1)
                            v.wait_ge(state_ready, 2 * b + c)
                v.wait_ge(*filled(b, "ret"))
                link(V.bn_stats(stats[:, 0, :], bank("ret")))
                fence()
                link(V.bn_aggr(gstat[:], stats[:, 0, :]))
                V.scalar_tensor_tensor(out=gstat[:, 1:2], in0=gstat[:, 0:1], scalar=gstat[:, 0:1], in1=gstat[:, 1:2],
                                       op0=ALU.mult, op1=ALU.add).then_inc(gstat_ready, 1)
                v.wait_ge(*filled(b, "gn"))
                read("gn", V.tensor_copy(gsum[:], bank("gn")[:, 0:2]))
                link(V.scalar_tensor_tensor(out=gtmp[:], in0=gsum[:, 0:1], scalar=gsum[:, 0:1], in1=gsum[:, 1:2],
                                            op0=ALU.mult, op1=ALU.subtract))
                link(V.tensor_scalar(gtmp[:], gtmp[:], -1.0, 0.0, ALU.mult, ALU.max))
                link(V.tensor_scalar(nv[:, 0:1], gtmp[:], EPS, None, ALU.add))
                rsqrt(ny[:, 0:1], nv[:, 0:1], na[:, 0:1])
                link(V.tensor_tensor(gscale[:], ny[:, 0:1], gn_w[:], ALU.mult))
                link(V.scalar_tensor_tensor(out=gtmp[:], in0=gsum[:, 0:1], scalar=-1.0, in1=gscale[:],
                                            op0=ALU.mult, op1=ALU.mult))
                V.tensor_tensor(gbias[:], gtmp[:], gn_b[:], ALU.add).then_inc(gaff_ready, 1)
                v.wait_ge(x3_kept, 16 * b)
                v.wait_ge(*filled(b, "retT"))
                read("retT", V.tensor_tensor(xr[:], x_in[:], tiles(bank("retT")), ALU.add))

                layer_norm(xn, xr)
                v.wait_ge(*filled(b, "router"))
                read("router", V.tensor_copy(logits[:], bank("router")[:, 0:NT * NBLK]
                                             .rearrange("p (j n) -> p j n", j=NT)))
                fence()
                for j in range(NT):
                    ins = V.max(top[:, j, :], logits[:, j, :])
                link(ins)
                fence()
                for j in range(NT):
                    ins = V.max_index(top_i[:, j, :], top[:, j, :], logits[:, j, :])
                link(ins)
                link(V.tensor_copy(top_f[:], top_i[:, :, 0:TOPB]))
                link(V.tensor_tensor(hits[:], iota[:].unsqueeze(1).unsqueeze(3).to_broadcast([TOK, NT, NBLK, TOPB]),
                                     top_f[:].unsqueeze(2).to_broadcast([TOK, NT, NBLK, TOPB]), ALU.is_equal))
                link(V.tensor_reduce(dropped[:], hits[:], AX.X, ALU.add))
                V.tensor_scalar(dropped[:], dropped[:], -1.0, None, ALU.add).then_inc(drop_ready, 1)
                v.wait_ge(*filled(b, "y0"))
                read("y0", V.tensor_tensor(xr[:], xr[:], tiles(bank("y0")), ALU.add))

                layer_norm(xn, xr)
                for i in range(2):
                    n = 96 + ROPE * i
                    for name, dst, table in ((f"qa{i}", rot_a, cos), (f"qb{i}", rot_b, sin)):
                        v.wait_ge(*filled(b, name))
                        V.tensor_tensor(dst[0:n, i, :], bank(name)[0:n, :], table[0:n, i, :], ALU.mult)\
                         .then_inc(free[BANK[name]], 1)
                v.wait_ge(khi_ready, b + 1)
                V.tensor_tensor(k_lo[:], bank("kn"), k_hi[:].bitcast(f32), ALU.subtract).then_inc(free[BANK["kn"]], 1)
                v.wait_ge(*filled(b, "vv"))
                for s in range(2):
                    ins = V.tensor_copy(vv[:].rearrange("p j u g s c -> p (j u) g s c")[:, :, :, s, 8 * s:8 * s + 8],
                                        bank("vv").rearrange("p (a s g e) -> p a s g e", a=2 * NT, s=2, g=4)[:, :, s])
                ins.then_inc(free[BANK["vv"]], 1)
                for q in range(QUADS):
                    for un in range(QUAD_UNITS):
                        n = RET_UNITS + QUAD_UNITS * q + un
                        v.wait_ge(*unit_emptied(b, n))
                        p = pt[:, q % 2, un, :]
                        if un < 4:
                            d = tiles(p[:, 0:512])
                            V.scalar_tensor_tensor(out=d, in0=d, scalar=P_LO, in1=over_tiles(causal[:]),
                                                   op0=ALU.max, op1=ALU.min)
                            V.tensor_scalar(p[:, 512:1024], p[:, 512:1024], P_LO, P_HI, ALU.max, ALU.min)\
                             .then_inc(pt_ready, 1)
                        else:
                            V.tensor_scalar(p, p, P_LO, P_HI, ALU.max, ALU.min).then_inc(pt_ready, 1)
                for u in range(2):
                    v.wait_ge(*filled(b, f"om{u}"))
                    om = bank(f"om{u}")[:, 0:72 * NT].rearrange("p (j c) -> p j c", j=NT)
                    link(V.reciprocal(den_r[:, u, :, :], om[:, :, 8 * HD:72]))
                    V.tensor_tensor(o_tm[:, :, 64 * u:64 * u + 64].rearrange("p j (h e) -> p j h e", h=8),
                                    om[:, :, 0:8 * HD].rearrange("p j (h e) -> p j h e", h=8),
                                    den_r[:, u, :, :].unsqueeze(3).to_broadcast([TOK, NT, 8, HD]), ALU.mult)\
                     .then_inc(free[BANK[f"om{u}"]], 1)
                v.wait_ge(*filled(b, "y1"))
                read("y1", V.tensor_tensor(xr[:], xr[:], tiles(bank("y1")), ALU.add))

                v.wait_ge(scattered, 16 * NT * TOPE * b)
                layer_norm(xn3, xr)
                v.wait_ge(*filled(b, "gate"))
                read("gate", V.tensor_copy(glog[:], bank("gate")[:, 0:NT * NE].rearrange("p (j n) -> p j n", j=NT)))
                fence()
                for j in range(NT):
                    ins = V.max(etop[:, j, :], glog[:, j, :])
                link(ins)
                V.tensor_tensor(esub[:], etop[:], etop[:, :, 0:1].to_broadcast([TOK, NT, 8]), ALU.subtract)\
                 .then_inc(esub_ready, 1)
                for j in range(NT):
                    ins = V.max_index(eidx[:, j, :], etop[:, j, :], glog[:, j, :])
                link(ins)
                link(V.tensor_copy(eidf[:], eidx[:, :, 0:TOPE]))
                V.tensor_tensor(oh[:], iota[:, 0:NE].unsqueeze(1).unsqueeze(1).to_broadcast([TOK, NT, TOPE, NE]),
                                eidf[:].unsqueeze(3).to_broadcast([TOK, NT, TOPE, NE]), ALU.is_equal)\
                 .then_inc(oh_ready, 1)
                v.wait_ge(eexp_ready, b + 1)
                link(V.tensor_reduce(esum[:], eexp[:], AX.X, ALU.add))
                link(V.reciprocal(esum[:], esum[:]))
                link(V.tensor_tensor(ew[:], eexp[:, :, 0:TOPE], esum[:].unsqueeze(2).to_broadcast([TOK, NT, TOPE]),
                                     ALU.mult))
                link(V.tensor_tensor(edn[:], ew[:, :, 0], ew[:, :, 1], ALU.add))
                link(V.tensor_scalar(edn[:], edn[:], 1e-9, None, ALU.add))
                link(V.reciprocal(edn[:], edn[:]))
                link(V.tensor_tensor(ew[:], ew[:], edn[:].unsqueeze(2).to_broadcast([TOK, NT, TOPE]), ALU.mult))
                v.wait_ge(*filled(b, "rank"))
                read("rank", V.tensor_tensor(rank_oh[:], bank("rank")[:, 0:NT * NQ]
                                             .rearrange("p (j k e) -> p j k e", j=NT, k=TOPE), oh[:], ALU.mult))
                link(V.tensor_reduce(rank[:], rank_oh[:], AX.X, ALU.add))
                link(V.tensor_scalar(keep[:], rank[:], CAP + 0.5, None, ALU.is_le))
                link(V.scalar_tensor_tensor(out=slot[:], in0=eidf[:], scalar=float(CAP), in1=rank[:],
                                            op0=ALU.mult, op1=ALU.add))
                link(V.tensor_tensor(slot[:], slot[:], over_tiles(queue_of[:]), ALU.add))
                v.wait_ge(route_kept, 16 * b)
                slot_g = route[:, 0, :].rearrange("p (j k) -> p j k", j=NT)
                weight = route[:, 1, :].rearrange("p (j k) -> p j k", j=NT)
                link(V.tensor_tensor(slot_g, slot[:], keep[:], ALU.mult))
                link(V.scalar_tensor_tensor(out=slot[:], in0=keep[:], scalar=-PAST_END, in1=slot_g,
                                            op0=ALU.mult, op1=ALU.add))
                V.tensor_scalar(put_at[:], slot[:], PAST_END, None, ALU.add)
                V.tensor_tensor(weight, ew[:], keep[:], ALU.mult).then_inc(route_ready, 1)
                link(V.tensor_reduce(oh_row[:], oh[:].rearrange("p j k e -> p (k e) j"), AX.X, ALU.add))
                link(V.tensor_tensor(oh_cnt[:], oh_cnt[:], oh_row[:], ALU.add))
                link(V.tensor_copy(oh_past[:], oh_cnt[:]))

            with v.Fori(0, B) as b:
                row(b)
            assert steps[0] == V_STEPS, steps[0]

            for k in range(TOPE):
                with v.Fori(0, NE // 2) as i:
                    for w in range(2):
                        n = NE * k + 2 * i + w
                        v.wait_ge(queue_done, n + 1)
                        v.wait_ge(xqT_ps, n + 1)
                        V.tensor_copy(xqT[:, w, :], xqT_psum[:, 0:CAP]).then_inc(xqT_ready, 1)
                        for t in range(4):
                            half, mm = t // 2, t % 2
                            v.wait_ge(silu_ready, 4 * n + t + 1)
                            V.tensor_tensor(act_h[:, w, mm, HALF * half:HALF * half + HALF], act_g[:, t % 2, :],
                                            ps_score[:, t % 2, 512:512 + HALF], ALU.mult).then_inc(gu_free, 1)
            v.wait_ge(route_kept, 16 * B)
            v.wait_ge(x3_kept, 16 * B)
            with v.Fori(0, B) as b:
                v.wait_ge(got, 16 * NT * TOPE * b)
                v.wait_ge(sum_ready, b)
                V.tensor_scalar(w_now[:], route_all[:, b, NT * TOPE:2 * NT * TOPE], 0.0, None, ALU.add)
                V.tensor_scalar(get_at[:], route_all[:, b, 0:NT * TOPE], 0.0, None, ALU.add).then_inc(at_ready, 1)
                v.wait_ge(at_ready, b + 1)
                v.wait_ge(got, 16 * NT * TOPE * (b + 1))
                v.wait_ge(x_got, 16 * (B + b + 1))
                for j in range(NT):
                    ins = V.scalar_tensor_tensor(out=y_part[:, j, :], in0=y_got[:, j, 0, :], scalar=w_now[:, 2 * j:2 * j + 1],
                                                 in1=x_late[:, j, :], op0=ALU.mult, op1=ALU.add)
                ins.then_inc(part_ready, 1)
                v.wait_ge(out_done, 16 * b)
                v.wait_ge(part_ready, b + 1)
                for j in range(NT):
                    ins = V.scalar_tensor_tensor(out=y_out[:, j, :], in0=y_got[:, j, 1, :],
                                                 scalar=w_now[:, 2 * j + 1:2 * j + 2],
                                                 in1=y_part[:, j, :], op0=ALU.mult, op1=ALU.add)
                ins.then_inc(sum_ready, 1)


def kernel(**inputs):
    import concourse.bacc as bacc
    from concourse.bass_utils import run_bass_kernel_spmd as run

    a = {k: np.asarray(v) for k, v in inputs.items()}
    wuq = a["L1_attn_W_UQ"].reshape(LAT, NH, HD)
    wqr = a["L1_attn_W_QR"].reshape(LAT, NH, ROPE)
    swap = [1, 0, 3, 2]
    wqb = np.zeros((LAT, NH, HROW), wuq.dtype)
    wqb[:, :, HD:] = wqr[:, :, swap]
    wkr = a["L1_attn_W_KR"]
    arrays = {
        "x": a["L0_attn_x"], "past_kv": a["L0_attn_past_kv"], "wqkv": a["L0_attn_W_qkv"],
        "gn_w": np.repeat(a["L0_attn_gn_weight"], HD)[:, None], "gn_b": np.repeat(a["L0_attn_gn_bias"], HD)[:, None],
        "w_router": a["L0_ffn_w_router"], "b_router": a["L0_ffn_b_router"][None, :],
        "w1": a["L0_ffn_w1"].T, "b1": a["L0_ffn_b1"].reshape(4, D).T, "w2": a["L0_ffn_w2"].T,
        "b2": a["L0_ffn_b2"][None, :],
        "w_down": np.concatenate([a["L1_attn_W_DQ"], a["L1_attn_W_DKV"]], axis=1),
        "wqa": np.concatenate([wuq, wqr], axis=2).reshape(LAT, NH * HROW), "wqb": wqb.reshape(LAT, NH * HROW),
        "wukv": np.concatenate([a["L1_attn_W_UK"], a["L1_attn_W_UV"]], axis=1),
        "wkr": np.concatenate([wkr, wkr[:, swap]], axis=1),
        "wo": a["L1_attn_W_O"], "w_gate": a["L1_ffn_gate_w"].T,
        "w_eg": a["L1_ffn_gate_proj_w"].transpose(0, 2, 1), "w_eu": a["L1_ffn_up_proj_w"].transpose(0, 2, 1),
        "w_ed": a["L1_ffn_down_proj_w"].transpose(0, 2, 1).reshape(NE, 2, D, D).transpose(0, 2, 1, 3)
        .reshape(NE, D, 2 * D),
        **constants(),
    }
    arrays = {f"in_{k}": np.ascontiguousarray(v) for k, v in arrays.items()}
    nc = bacc.Bacc("TRN2", target_bir_lowering=False, num_devices=1)
    io = {k[3:]: nc.dram_tensor(k, v.shape, mybir.dt.from_np(v.dtype), kind="ExternalInput").ap()
          for k, v in arrays.items()}
    out = nc.dram_tensor("out", (B, T, D), mybir.dt.float32, kind="ExternalOutput").ap()
    network(nc, io, out)
    return run(nc, [arrays], core_ids=[0]).results[0]["out"]
```

```python
import concourse.bass as bass
from concourse import mybir
from contextlib import ExitStack
import numpy as np

B, T, D = 8, 512, 128
TOK = 128
NT = T // TOK
NH, HD = 16, 8
ROPE = 4
HROW = HD + ROPE
LAT = 32
NBLK, TOPB, HID0 = 16, 4, 512
NE, TOPE, HID1 = 8, 2, 256
CAP = int(1.25 * B * T / NE)
NQ = TOPE * NE
SLOTS = NQ * CAP
CT = CAP // TOK
HALF = CAP // 2
EPS = 1e-5
DROP = 2.0 ** 100
CLIP = 80.0
PAST_END = float(2 ** 15)
QK_SCALE = 1.0 / float(np.sqrt(np.float32(HROW)))
P_LO = float(np.exp(-CLIP * QK_SCALE))
P_HI = float(np.exp(CLIP * QK_SCALE))


def constants():
    f = np.float32
    gamma = 1.0 - 2.0 ** (-5.0 - np.arange(NH, dtype=np.float64))
    t = np.arange(TOK)
    diff = t[None, :] - t[:, None]
    decay = np.where(diff[:, None, :] >= 0, gamma[None, :, None] ** np.maximum(diff, 0)[:, None, :], 0.0)
    head = np.arange(D) // HD
    cos, sin = np.ones((2, 100, T)), np.zeros((2, 100, T))
    inv = (np.float32(10000.0) ** (-np.arange(0, ROPE, 2, dtype=f) / f(ROPE))).astype(f)
    ang = (np.arange(T, dtype=f)[None, :] * inv[:, None]).astype(f).astype(np.float64)
    for r in range(9):
        for i in range(ROPE):
            row = r * HROW + HD + i if r < 8 else 8 * HROW + i
            cos[:, row] = np.cos(ang[i // 2])
            sin[:, row] = np.sin(ang[i // 2]) * (-1.0 if i % 2 == 0 else 1.0)
    pick = np.zeros((D, 8 * HD + 8))
    for g in range(4):
        for s in range(2):
            for e in range(HD):
                pick[32 * g + 8 * s + e, HD * (4 * s + g) + e] = 1.0
            pick[32 * g + 16 + s, 8 * HD + 4 * s + g] = 1.0
    blocks = np.zeros((NBLK, HID0))
    for n in range(NBLK):
        blocks[n, n * 32:(n + 1) * 32] = DROP
    return {
        "c_decay": decay.astype(f),
        "c_qdecay": (gamma[head][:, None] ** t[None, :]).astype(f),
        "c_kdecay": (gamma[head][None, :] ** (TOK - t)[:, None]).astype(f),
        "c_gtile": (gamma[head] ** TOK).astype(f)[:, None],
        "c_heads": (head[:, None] == head[None, :]).astype(f),
        "c_lane": (head[:, None] % 8 == np.arange(8)[None, :]).astype(f),
        "c_cos": cos.astype(f), "c_sin": sin.astype(f),
        "c_pick": pick.astype(f),
        "c_blocks": blocks.astype(f),
        "c_ident": np.eye(D, dtype=f),
        "c_causal": (P_HI * (diff >= 0)).astype(f),
        "c_upto": (diff >= 0).astype(f),
        "c_iota": np.tile(np.arange(NBLK, dtype=f)[None, :], (D, 1)),
        "c_queue": np.tile(np.array([-1.0 + k * NE * CAP for k in range(TOPE)], f)[None, :], (D, 1)),
    }


QUADS, QUAD_UNITS = NH // 4, 10
QUAD_KINDS = [("diag", 0), ("off", 0), ("diag", 1), ("off", 1), ("second", 0),
              ("diag", 2), ("off", 2), ("diag", 3), ("off", 3), ("second", 1)]
UNIT_OF = {kind: n for n, kind in enumerate(QUAD_KINDS)}
ATT = QUADS * QUAD_UNITS
FRONT_USES = ([("xnT0", 0), ("qT", 1), ("kT", 2), ("v", 3), ("ktm", 0), ("ret", 3)]
              + [(f"r{n}", 1 + n % 2) for n in range(4 * NT)]
              + [("kv0", 0), ("kv1", 0), ("kv2", 0), ("gn", 0), ("retT", 1), ("xnT1", 2), ("router", 0), ("h0", 1),
                 ("h1", 2), ("dropT", 3), ("h2", 0), ("h3", 3), ("y0", 1), ("xnT2", 2), ("cT", 0), ("qa0", 1),
                 ("qb0", 3), ("qa1", 2), ("qb1", 0), ("kn", 1), ("vv", 3)])
BACK_USES = ([(f"s{n}", 4 + n % 3) for n in range(ATT)]
             + [("u0", 7), ("u1", 7), ("om0", 5), ("om1", 6), ("onT", 4), ("y1", 5), ("xnT3", 6), ("gate", 4),
                ("rank", 5)])
USES = FRONT_USES + BACK_USES
BANK = dict(USES)
PER_BANK = [sum(b == k for _, b in USES) for k in range(8)]
CREDIT = [0] * 4 + [1] * 4
NTH = {name: sum(b == BANK[name] for _, b in USES[:i]) for i, (name, _) in enumerate(USES)}
FRONT_STEPS, BACK_STEPS = 71, 37

ORDER = [("front", "norm0"), ("back", "take"), ("front", "turn0"), ("front", "project"), ("front", "lanes"),
         ("front", "chunk", 0), ("back", "attend", 0, 4), ("front", "chunk", 1), ("back", "attend", 4, 9),
         ("front", "chunk", 2), ("back", "attend", 9, 14), ("front", "chunk", 3), ("back", "attend", 14, 18),
         ("front", "last_sum"), ("front", "gn_moments"), ("back", "attend", 18, 21), ("front", "gn_affine"),
         ("back", "attend", 21, 25), ("front", "gn_apply"), ("front", "norm1"), ("back", "attend", 25, 30),
         ("front", "turn1"), ("front", "router"), ("front", "best"), ("back", "attend", 30, 37), ("front", "mlp"),
         ("back", "attend", 37, 40), ("front", "norm2"), ("back", "sums"), ("front", "turn2"), ("back", "output"),
         ("front", "latent"), ("back", "norm3"), ("front", "rotate"), ("back", "turn3"), ("back", "gate"),
         ("front", "split"), ("back", "route")]


def network(nc, io, out):
    f32, f32r, bf16 = mybir.dt.float32, mybir.dt.float32r, mybir.dt.bfloat16
    i32, u32 = mybir.dt.int32, mybir.dt.uint32
    ALU, ACT, AX = mybir.AluOpType, mybir.ActivationFunctionType, mybir.AxisListType
    V, S, PE, G = nc.vector, nc.scalar, nc.tensor, nc.gpsimd
    ctx = ExitStack()
    with ctx:
        def sb(name, shape, dt=f32):
            return ctx.enter_context(nc.sbuf_tensor(name, shape, dt))

        def sem(name):
            return ctx.enter_context(nc.semaphore(name))

        def dram(name, shape):
            return nc.dram_tensor(name, shape, f32, kind="Internal").ap()

        q_rows = dram("q_rows", [NH, 2, HROW, T])
        k_rows = dram("k_rows", [NH, 2, HROW, T])
        queue_x = dram("queue_x", [SLOTS, D])
        queue_y = dram("queue_y", [SLOTS, D])
        x_mid = dram("x_mid", [B, TOK, NT * D])

        decay = sb("decay", [TOK, NH, TOK])
        qdecay = sb("qdecay", [D, TOK])
        kdecay = sb("kdecay", [TOK, D])
        gtile = sb("gtile", [D, 1])
        heads = sb("heads", [D, D])
        lane = sb("lane", [D, 8])
        cos, sin = sb("cos", [100, 2, T]), sb("sin", [100, 2, T])
        pick, ident = sb("pick", [D, 8 * HD + 8]), sb("ident", [D, D])
        blocks = sb("blocks", [NBLK, HID0], bf16)
        causal = sb("causal", [TOK, TOK])
        upto = sb("upto", [TOK, TOK], bf16)
        ones = sb("ones", [TOK, TOK], bf16)
        mean_of = sb("mean_of", [D, D])
        ones_row = sb("ones_row", [1, TOK])
        iota = sb("iota", [D, NBLK])
        queue_of = sb("queue_of", [D, TOPE])
        wqkv = sb("wqkv", [D, 3 * D])
        past, past_in = sb("past", [D, D]), sb("past_in", [D, D])
        gn_w, gn_b = sb("gn_w", [D, 1]), sb("gn_b", [D, 1])
        w_router, b_router = sb("w_router", [D, NBLK]), sb("b_router", [1, NBLK])
        w1, b1 = sb("w1", [D, HID0]), sb("b1", [D, 4])
        w2, b2 = sb("w2", [D, 4, D]), sb("b2", [1, D])
        w_down = sb("w_down", [D, 2 * LAT])
        wqa, wqb = sb("wqa", [LAT, 2, 96]), sb("wqb", [LAT, 2, 96])
        wukv = sb("wukv", [2 * LAT, 2 * D])
        wkr = sb("wkr", [D, 2, ROPE])
        wo = sb("wo", [D, D])
        w_gate = sb("w_gate", [D, NE])

        x_in = sb("x_in", [TOK, NT, D])
        xr, xb = sb("xr", [TOK, NT, D]), sb("xb", [TOK, NT, D])
        xn = sb("xn", [TOK, NT, D])
        xn3 = sb("xn3", [TOK, NT, D])
        xnT = sb("xnT", [D, T])
        stats, mv = sb("stats", [TOK, NT, 6]), sb("mv", [TOK, NT, 2])
        nv, ny, na = sb("nv", [TOK, NT]), sb("ny", [TOK, NT]), sb("na", [TOK, NT])
        stats3, mv3 = sb("stats3", [TOK, NT, 6]), sb("mv3", [TOK, NT, 2])
        nv3, ny3, na3 = sb("nv3", [TOK, NT]), sb("ny3", [TOK, NT]), sb("na3", [TOK, NT])
        gstat, gsum = sb("gstat", [D, 2]), sb("gsum", [D, 2])
        gscale, gbias, gtmp = sb("gscale", [D, 1]), sb("gbias", [D, 1]), sb("gtmp", [D, 1])
        fence_v, credit, pool_one = sb("fence_v", [1, 1]), sb("credit", [1, 8]), sb("pool_one", [1, 1])
        qT, kT = sb("qT", [D, T]), sb("kT", [D, T])
        q_lanes = sb("q_lanes", [D, NT, 8, TOK])
        q_dec = sb("q_dec", [D, NT, TOK])
        v_tm, k_dec = sb("v_tm", [TOK, NT, D]), sb("k_dec", [TOK, NT, D])
        v_lanes = sb("v_lanes", [TOK, NT, 4, D])
        probs = sb("probs", [TOK, 2, NH, TOK])
        state, kv_own = sb("state", [D, 3, D]), sb("kv_own", [D, D])
        retT = sb("retT", [D, T])
        logits = sb("logits", [TOK, NT, NBLK])
        top, top_i, top_f = sb("top", [TOK, NT, 8]), sb("top_i", [TOK, NT, 8], u32), sb("top_f", [TOK, NT, TOPB])
        hits, dropped = sb("hits", [TOK, NT, NBLK, TOPB]), sb("dropped", [TOK, NT, NBLK])
        dropT = sb("dropT", [NBLK, T], bf16)
        hidden = q_lanes[:, 0:2, :, :].rearrange("p c (a r) t -> p (c a) (r t)", a=2)
        cT = sb("cT", [2 * LAT, T])
        rot_a = probs[0:100, 0, 0:8, :].rearrange("p (i a) t -> p i (a t)", i=2)
        rot_b = probs[0:100, 1, 0:8, :].rearrange("p (i a) t -> p i (a t)", i=2)
        rot_s = rot_a
        q_hi, q_lo = sb("q_hi", [100, 2, T], f32r), sb("q_lo", [100, 2, T], f32r)
        k_hi, k_lo = sb("k_hi", [D, T], f32r), sb("k_lo", [D, T], f32r)
        qs, ks = sb("qs", [D, NH // 2, T], f32r), sb("ks", [D, NH // 2, T], f32r)
        vv = sb("vv", [TOK, NT, 2, 4, 2, 32])
        pt = sb("pt", [TOK, 2, QUAD_UNITS, 512])
        u_sb = sb("u_sb", [D, 2, T])
        oT, xnT3 = u_sb[:, 0, :], u_sb[:, 1, :]
        o_tm = xn3
        den_r = sb("den_r", [TOK, 2, NT, 8])
        glog = sb("glog", [TOK, NT, NE])
        etop, eidx = sb("etop", [TOK, NT, 8]), sb("eidx", [TOK, NT, 8], u32)
        eidf = sb("eidf", [TOK, NT, TOPE])
        esub, eexp = sb("esub", [TOK, NT, 8]), sb("eexp", [TOK, NT, 8])
        esum, ew, edn = sb("esum", [TOK, NT]), sb("ew", [TOK, NT, TOPE]), sb("edn", [TOK, NT])
        oh = sb("oh", [TOK, NT, TOPE, NE], bf16)
        oh_cnt = sb("oh_cnt", [TOK, NQ])
        oh_past = sb("oh_past", [TOK, NQ], bf16)
        rank_oh, rank = sb("rank_oh", [TOK, NT, TOPE, NE]), sb("rank", [TOK, NT, TOPE])
        keep, slot = sb("keep", [TOK, NT, TOPE]), sb("slot", [TOK, NT, TOPE])
        oh_row = sb("oh_row", [TOK, NQ])
        route = sb("route", [TOK, 2, NT * TOPE])
        put_at = sb("put_at", [TOK, NT, TOPE], u32)
        route_all = sb("route_all", [TOK, B, 2 * NT * TOPE])

        late = pt[:].rearrange("p a u c -> p (a u c)")
        taken = [0]

        def part_of_late(*shape):
            size = int(np.prod(shape))
            at = taken[0]
            taken[0] += size
            assert taken[0] <= 2 * QUAD_UNITS * 512
            names = "abc"[:len(shape)]
            return late[:, at:at + size].rearrange(f"p ({' '.join(names)}) -> p {' '.join(names)}",
                                                   **dict(zip(names, shape)))

        wg, wu, wd = part_of_late(2, HID1), part_of_late(2, HID1), part_of_late(2, 2, D)
        xq, xqT = part_of_late(2, CT, D), part_of_late(2, CAP)
        act_g, act_h = part_of_late(2, HALF), part_of_late(2, 2, CAP)
        yq = part_of_late(2, CT, D)
        get_at, w_now = sb("get_at", [TOK, NT * TOPE], u32), sb("w_now", [TOK, NT * TOPE])
        y_got = v_lanes[:].rearrange("p j a d -> p (j a) d")[:, 0:NT * TOPE, :].rearrange("p (j k) d -> p j k d", j=NT)
        y_part, y_out, x_late = xn, xn3, xb

        blocks32, upto32 = pt[0:NBLK, 1, 0, :], pt[:, 1, 1, 0:TOK]

        ps = ctx.enter_context(nc.psum_tensor("ps", [128, 8, 512], f32))
        gu_ps = ps[:, 0:4, :].rearrange("p (t a) c -> p t (a c)", t=2)
        xqT_psum = ps[:, 4:6, :].rearrange("p a c -> p (a c)")
        y_ps = ps[:, 6:8, :].rearrange("p a c -> p (a c)")

        const_in, x_got, past_got = sem("const_in"), sem("x_got"), sem("past_got")
        setup_v, setup_g, setup_s = sem("setup_v"), sem("setup_g"), sem("setup_s")
        queue_zeroed = sem("queue_zeroed")
        full = [sem(f"bank_full{k}") for k in range(8)]
        free = [sem(f"bank_free{k}") for k in range(8)]
        front_step, back_step = sem("front_step"), sem("back_step")
        xn_ready, xn3_ready = sem("xn_ready"), sem("xn3_ready")
        qlanes_ready, qdec_ready, vlanes_ready = sem("qlanes_ready"), sem("qdec_ready"), sem("vlanes_ready")
        state_ready, chunk_done = sem("state_ready"), sem("chunk_done")
        gstat_ready, gaff_ready, drop_ready = sem("gstat_ready"), sem("gaff_ready"), sem("drop_ready")
        rotsum_ready, qhi_ready, qlo_ready, khi_ready = (sem("rotsum_ready"), sem("qhi_ready"), sem("qlo_ready"),
                                                         sem("khi_ready"))
        rows_out, rows_in = sem("rows_out"), sem("rows_in")
        pt_ready, pv_done = sem("pt_ready"), sem("pv_done")
        xb_taken = sem("xb_taken")
        x3_kept, esub_ready, eexp_ready, oh_ready = sem("x3_kept"), sem("esub_ready"), sem("eexp_ready"), sem("oh_ready")
        route_ready, route_kept = sem("route_ready"), sem("route_kept")
        fence_g, scattered = sem("fence_g"), sem("scattered")
        wexp_in, xq_in, y_kept = ([sem(f"{name}{w}") for w in range(2)] for name in ("wexp_in", "xq_in", "y_kept"))
        xqT_ps, xqT_ready = sem("xqT_ps"), sem("xqT_ready")
        gu_free, queue_done = sem("gate_up_free"), sem("queue_done")
        gu_full, silu_ready, y_ready = sem("gate_up_full"), sem("silu_ready"), sem("y_ready")
        at_ready, got, part_ready, sum_ready, out_done = (sem("at_ready"), sem("got"), sem("part_ready"),
                                                          sem("sum_ready"), sem("out_done"))

        block = ctx.enter_context(nc.Block())

        def after(engine, semaphore, value):
            if not isinstance(value, int) or value > 0:
                engine.wait_ge(semaphore, value)

        def pair_of_rows(stages, f, a):
            rows = {"front": f, "back": a}
            for part, name, *which in ORDER:
                if rows[part] is not None and name in stages:
                    stages[name](rows[part], *which)

        def bank(name):
            return ps[:, BANK[name], :]

        def filled(b, name):
            return full[BANK[name]], b * PER_BANK[BANK[name]] + NTH[name] + 1

        def opened(b, name):
            return free[BANK[name]], b * PER_BANK[BANK[name]] + NTH[name] + CREDIT[BANK[name]]

        def emptied(b, name):
            return free[BANK[name]], b * PER_BANK[BANK[name]] + NTH[name] + CREDIT[BANK[name]] + 1

        def tiles(ap):
            return ap.rearrange("p (j c) -> p j c", j=NT)

        def tile_of(j, width=TOK):
            return slice(j * width, (j + 1) * width)

        consts = [(wqkv[:], io["wqkv"]), (ident[:], io["c_ident"]), (lane[:], io["c_lane"]),
                  (qdecay[:], io["c_qdecay"]), (kdecay[:], io["c_kdecay"]), (decay[:], io["c_decay"]),
                  (gtile[:], io["c_gtile"]), (heads[:], io["c_heads"]), (gn_w[:], io["gn_w"]), (gn_b[:], io["gn_b"]),
                  (cos[:], io["c_cos"].rearrange("i p t -> p i t")), (sin[:], io["c_sin"].rearrange("i p t -> p i t")),
                  (pick[:], io["c_pick"]), (blocks32, io["c_blocks"]),
                  (causal[:], io["c_causal"]), (upto32, io["c_upto"]), (iota[:], io["c_iota"]),
                  (queue_of[:], io["c_queue"]),
                  (w_router[:], io["w_router"]), (b_router[:], io["b_router"]), (w1[:], io["w1"]), (b1[:], io["b1"]),
                  (w2[:], io["w2"].rearrange("(m p) d -> p m d", m=4)), (b2[:], io["b2"]), (w_down[:], io["w_down"]),
                  (wqa[:], io["wqa"].rearrange("l (i r) -> l i r", i=2)),
                  (wqb[:], io["wqb"].rearrange("l (i r) -> l i r", i=2)),
                  (wukv[LAT:2 * LAT, :], io["wukv"]), (wkr[:], io["wkr"].rearrange("p (a r) -> p a r", a=2)),
                  (wo[:], io["wo"]), (w_gate[:], io["w_gate"])]
        N_CONST = 16 * len(consts)
        x_rows = io["x"].rearrange("b (j p) c -> b p j c", p=TOK)
        out_rows = out.rearrange("b (j p) c -> b p j c", p=TOK)
        queue_x_n = queue_x.rearrange("(n p j) c -> n p (j c)", p=TOK, j=CT)
        queue_y_n = queue_y.rearrange("(n p j) c -> n p (j c)", p=TOK, j=CT)

        @block.sync
        def _(sp):
            sp.dma_start(x_in[:], x_rows[0]).then_inc(x_got, 16)
            for dst, src in consts:
                sp.dma_start(dst, src).then_inc(const_in, 16)
            sp.wait_ge(setup_g, 1)
            for h in range(NH):
                r = slice(HD * h, HD * h + HD)
                sp.dma_start(past_in[r, r], io["past_kv"][h]).then_inc(past_got, 16)
            sp.wait_ge(setup_g, 2)
            for z in range(SLOTS // 1024):
                sp.dma_start(queue_x[1024 * z:1024 * z + 1024, :].rearrange("(p r) c -> p (r c)", r=8),
                             late[:, 0:1024]).then_inc(queue_zeroed, 16)

            def next_x(b):
                sp.wait_ge(*emptied(b, "retT"))
                sp.dma_start(x_in[:], x_rows[b + 1]).then_inc(x_got, 16)

            def rows_to_heads(b):
                for i in range(2):
                    hs = slice(8 * i, 8 * i + 8)
                    sp.wait_ge(qhi_ready, 2 * b + i + 1)
                    sp.dma_start(q_rows[hs, 0, :, :], q_hi[0:96, i, :].bitcast(f32)).then_inc(rows_out, 16)
                    sp.wait_ge(qlo_ready, 2 * b + i + 1)
                    sp.dma_start(q_rows[hs, 1, :, :], q_lo[0:96, i, :].bitcast(f32)).then_inc(rows_out, 16)
                if not isinstance(b, int) or b:
                    sp.wait_ge(*filled(b - 1, f"s{ATT - 1}"))
                for part, rope_rows in ((0, q_hi), (1, q_lo)):
                    sp.dma_start(k_rows[:, part, HD:HROW, :].rearrange("h d t -> d h t"),
                                 rope_rows[96:100, 1, :].bitcast(f32).unsqueeze(1).to_broadcast([ROPE, NH, T]))\
                      .then_inc(rows_out, 16)
                sp.wait_ge(khi_ready, b + 1)
                sp.dma_start(k_rows[:, 0, 0:HD, :], k_hi[:].bitcast(f32)).then_inc(rows_out, 16)
                sp.wait_ge(*emptied(b, "kn"))
                sp.dma_start(k_rows[:, 1, 0:HD, :], k_lo[:].bitcast(f32)).then_inc(rows_out, 16)
                sp.wait_ge(rows_out, 128 * (b + 1))
                for i in range(2):
                    at, hs = 64 * i, slice(8 * i, 8 * i + 8)
                    sp.dma_start(qs[at:at + 24, :, :].bitcast(f32),
                                 q_rows[hs].rearrange("h a d t -> h (a d) t").rearrange("h r t -> r h t"))\
                      .then_inc(rows_in, 16)
                    sp.dma_start(qs[at + 24:at + 36, :, :].bitcast(f32), q_rows[hs, 0].rearrange("h r t -> r h t"))\
                      .then_inc(rows_in, 16)
                    sp.dma_start(ks[at:at + 12, :, :].bitcast(f32), k_rows[hs, 0].rearrange("h r t -> r h t"))\
                      .then_inc(rows_in, 16)
                    sp.dma_start(ks[at + 12:at + 36, :, :].bitcast(f32),
                                 k_rows[hs].rearrange("h a d t -> h (a d) t").rearrange("h r t -> r h t"))\
                      .then_inc(rows_in, 16)

            def keep_x(b):
                sp.wait_ge(*emptied(b, "y1"))
                sp.dma_start(x_mid[b], xb[:].rearrange("p j c -> p (j c)")).then_inc(x3_kept, 16)

            def keep_route(b):
                sp.wait_ge(route_ready, b + 1)
                sp.dma_start(route_all[:, b, :], route[:].rearrange("p a c -> p (a c)")).then_inc(route_kept, 16)

            next_x(0)
            rows_to_heads(0)
            with sp.Fori(1, B - 1) as b:
                next_x(b)
                keep_x(b - 1)
                rows_to_heads(b)
                keep_route(b - 1)
            keep_x(B - 2)
            rows_to_heads(B - 1)
            keep_route(B - 2)
            keep_x(B - 1)
            keep_route(B - 1)

            sp.wait_ge(scattered, 16 * TOPE * NT * B)
            for k in range(TOPE):
                with sp.Fori(0, NE // 2) as i:
                    for w in range(2):
                        n = NE * k + 2 * i + w
                        sp.wait_ge(queue_done, n + 1)
                        sp.dma_start(xq[:, w, :, :].rearrange("p j c -> p (j c)"), queue_x_n[n]).then_inc(xq_in[w], 16)
                        sp.dma_start(wg[:, w, :], io["w_eg"][2 * i + w]).then_inc(wexp_in[w], 16)
                        sp.dma_start(wu[:, w, :], io["w_eu"][2 * i + w]).then_inc(wexp_in[w], 16)
                        sp.dma_start(wd[:, w, :, :].rearrange("p m d -> p (m d)"), io["w_ed"][2 * i + w])\
                          .then_inc(wexp_in[w], 16)
            sp.wait_ge(x3_kept, 16 * (B + 1))
            with sp.Fori(0, B) as b:
                sp.wait_ge(part_ready, b)
                sp.dma_start(x_late[:].rearrange("p j c -> p (j c)"), x_mid[b]).then_inc(x_got, 16)
                sp.wait_ge(sum_ready, b + 1)
                sp.dma_start(out_rows[b], y_out[:]).then_inc(out_done, 16)
            sp.wait_ge(out_done, 16 * B)

        @block.gpsimd
        def _(pool):
            G.memset(past_in[:], 0.0).then_inc(setup_g, 1)
            G.memset(late[:, 0:1024], 0.0).then_inc(setup_g, 1)
            G.memset(ones[:], 1.0).then_inc(setup_g, 1)
            G.memset(mean_of[:], 1.0 / D).then_inc(setup_g, 1)
            G.memset(ones_row[:], 1.0).then_inc(setup_g, 1)
            G.memset(v_lanes[:], 0.0).then_inc(setup_g, 1)
            G.memset(vv[:], 0.0).then_inc(setup_g, 1)
            G.memset(pool_one[:], 0.0).then_inc(fence_g, 1)
            pool.wait_ge(setup_g, 7)
            for s in range(2):
                G.memset(vv[:, :, :, :, s, 16 + s:17 + s], 1.0).then_inc(setup_g, 1)
            def rotate(b):
                for i in range(2):
                    n = 96 + ROPE * i
                    pool.wait_ge(*emptied(b, f"qa{i}"))
                    pool.wait_ge(*emptied(b, f"qb{i}"))
                    G.tensor_tensor(rot_s[0:n, i, :], rot_a[0:n, i, :], rot_b[0:n, i, :], ALU.add)\
                     .then_inc(rotsum_ready, 1)

            def split(b):
                for i in range(2):
                    n = 96 + ROPE * i
                    pool.wait_ge(qhi_ready, 2 * b + i + 1)
                    G.tensor_tensor(q_lo[0:n, i, :], rot_s[0:n, i, :], q_hi[0:n, i, :].bitcast(f32), ALU.subtract)\
                     .then_inc(qlo_ready, 1)

            def route_rows(b):
                pool.wait_ge(fence_g, 2 * b + 1)
                pool.wait_ge(route_ready, b + 1)
                G.tensor_tensor(pool_one[:], pool_one[:], pool_one[:], ALU.add).then_inc(fence_g, 1)
                pool.wait_ge(queue_zeroed, 16 * (SLOTS // 1024))
                for j in range(NT):
                    for k in range(TOPE):
                        pool.indirect_dma_start(queue_x[:, :], bass.IndirectOffsetOnAxis(ap=put_at[:, j, k:k + 1], axis=0),
                                                xn3[:, j, :], None, bounds_check=SLOTS - 1, oob_is_err=False)\
                            .then_inc(scattered, 16)
                pool.wait_ge(fence_g, 2 * b + 2)
                pool.wait_ge(scattered, 16 * NT * TOPE * (b + 1))
                G.tensor_tensor(pool_one[:], pool_one[:], pool_one[:], ALU.add).then_inc(fence_g, 1)

            stages = {"rotate": rotate, "split": split, "route": route_rows}
            pair_of_rows(stages, 0, None)
            with pool.Fori(1, B) as b:
                pair_of_rows(stages, b, b - 1)
            pair_of_rows(stages, None, B - 1)
            for w in range(2):
                pool.wait_ge(y_kept[w], 16 * NQ // 2)
            with pool.Fori(0, B) as b:
                pool.wait_ge(sum_ready, b)
                pool.wait_ge(fence_g, 2 * B + b + 1)
                pool.wait_ge(at_ready, b + 1)
                G.tensor_tensor(pool_one[:], pool_one[:], pool_one[:], ALU.add).then_inc(fence_g, 1)
                for j in range(NT):
                    for k in range(TOPE):
                        pool.indirect_dma_start(y_got[:, j, k, :], None, queue_y[:, :],
                                                bass.IndirectOffsetOnAxis(ap=get_at[:, 2 * j + k:2 * j + k + 1], axis=0),
                                                bounds_check=SLOTS - 1, oob_is_err=False).then_inc(got, 16)

        @block.scalar
        def _(act):
            act.wait_ge(const_in, N_CONST)
            act.wait_ge(past_got, 16 * NH)
            act.wait_ge(queue_zeroed, 16 * (SLOTS // 1024))
            S.activation(past[:], past_in[:], ACT.Copy, scale=float(NH * HD)).then_inc(setup_s, 1)
            S.activation(blocks[:], blocks32, ACT.Copy).then_inc(setup_s, 1)
            S.activation(upto[:], upto32, ACT.Copy).then_inc(setup_s, 1)

            def copy_out(b, name, dst, src):
                act.wait_ge(*filled(b, name))
                S.activation(dst, src, ACT.Copy).then_inc(free[BANK[name]], 1)

            def turn(k, dst):
                return lambda b: copy_out(b, f"xnT{k}", dst, bank(f"xnT{k}"))

            def project(b):
                copy_out(b, "qT", qT[:], bank("qT"))
                copy_out(b, "kT", kT[:], bank("kT"))
                copy_out(b, "v", v_tm[:], tiles(bank("v")))

            def gn_apply(b):
                act.wait_ge(gaff_ready, b + 1)
                S.activation(retT[:], bank("ret"), ACT.Identity, bias=gbias[:, 0:1], scale=gscale[:, 0:1])\
                 .then_inc(free[BANK["ret"]], 1)

            def mlp(b):
                copy_out(b, "dropT", dropT[:], bank("dropT")[0:NBLK, :])
                for m in range(4):
                    act.wait_ge(*filled(b, f"h{m}"))
                    S.activation(hidden[:, m, :], bank(f"h{m}"), ACT.Relu, bias=b1[:, m:m + 1])\
                     .then_inc(free[BANK[f"h{m}"]], 1)

            def latent(b):
                copy_out(b, "cT", cT[:], bank("cT")[0:2 * LAT, :])

            def split(b):
                for i in range(2):
                    n = 96 + ROPE * i
                    act.wait_ge(rotsum_ready, 2 * b + i + 1)
                    S.activation(q_hi[0:n, i, :], rot_s[0:n, i, :], ACT.Copy).then_inc(qhi_ready, 1)
                act.wait_ge(*filled(b, "kn"))
                S.activation(k_hi[:], bank("kn"), ACT.Copy).then_inc(khi_ready, 1)

            def attend(b, lo, hi):
                for n in range(lo, hi):
                    q, un = divmod(n, QUAD_UNITS)
                    if un == 0 and q >= 2:
                        act.wait_ge(pv_done, QUADS * b + q - 1)
                    act.wait_ge(*filled(b, f"s{n}"))
                    S.activation(pt[:, q % 2, un, :], bank(f"s{n}"), ACT.Exp, scale=QK_SCALE)\
                     .then_inc(free[BANK[f"s{n}"]], 1)
                    if n == 2 * QUAD_UNITS + 5:
                        copy_sums(b, 0)

            def copy_sums(b, u):
                act.wait_ge(pv_done, QUADS * b + 2 * u + 2)
                S.activation(u_sb[:, u, :], bank(f"u{u}"), ACT.Copy).then_inc(free[BANK[f"u{u}"]], 1)

            def output(b):
                copy_out(b, "onT", oT, bank("onT"))

            def route(b):
                act.wait_ge(esub_ready, b + 1)
                S.activation(eexp[:], esub[:], ACT.Exp).then_inc(eexp_ready, 1)

            stages = {"turn0": turn(0, xnT[:]), "project": project, "gn_apply": gn_apply, "turn1": turn(1, xnT[:]), "mlp": mlp,
                      "turn2": turn(2, xnT[:]), "latent": latent, "split": split, "attend": attend,
                      "sums": lambda b: copy_sums(b, 1), "output": output, "turn3": turn(3, xnT3), "route": route}
            pair_of_rows(stages, 0, None)
            with act.Fori(1, B) as b:
                pair_of_rows(stages, b, b - 1)
            pair_of_rows(stages, None, B - 1)

            for k in range(TOPE):
                with act.Fori(0, NE // 2) as i:
                    for w in range(2):
                        n = NE * k + 2 * i + w
                        for t in range(4):
                            act.wait_ge(gu_free, 4 * n + t + 1)
                            act.wait_ge(gu_full, 4 * n + t + 1)
                            S.activation(act_g[:, t % 2, :], gu_ps[:, t % 2, 0:HALF], ACT.Silu)\
                             .then_inc(silu_ready, 1)
                        act.wait_ge(y_kept[w], 16 * (NE // 2 * k + i))
                        act.wait_ge(queue_done, n + 3)
                        S.activation(yq[:, w, :, :].rearrange("p j c -> p (j c)"), y_ps[:, 0:CAP], ACT.Copy)\
                         .then_inc(y_ready, 1)
                        act.wait_ge(y_ready, n + 1)
                        act.dma_start(queue_y_n[n], yq[:, w, :, :].rearrange("p j c -> p (j c)")).then_inc(y_kept[w], 16)

        @block.tensor
        def _(pe):
            pe.wait_ge(const_in, N_CONST)
            pe.wait_ge(setup_s, 3)
            pe.wait_ge(setup_g, 9)

            def full_inc(m, name):
                m.then_inc(full[BANK[name]], 1)

            def transposes(b, name, src):
                for j in range(NT):
                    m = PE.transpose(bank(name)[:, tile_of(j)], src(j), ident[:])
                full_inc(m, name)

            def turn(k, ready, count, src):
                def stage(b):
                    after(pe, *opened(b, f"xnT{k}"))
                    pe.wait_ge(ready, count * b + k % 3 + 1)
                    transposes(b, f"xnT{k}", lambda j: src[:, j, :])
                return stage

            def project(b):
                after(pe, *opened(b, "qT"))
                pe.wait_ge(*emptied(b, "xnT0"))
                full_inc(PE.matmul(bank("qT"), wqkv[:, 0:D], xnT[:], start=True, stop=True), "qT")
                after(pe, *opened(b, "kT"))
                full_inc(PE.matmul(bank("kT"), wqkv[:, D:2 * D], xnT[:], start=True, stop=True), "kT")
                for name, cols in (("v", slice(2 * D, 3 * D)), ("ktm", slice(D, 2 * D))):
                    after(pe, *opened(b, name))
                    for j in range(NT):
                        m = PE.matmul(bank(name)[:, tile_of(j)], xnT[:, tile_of(j)], wqkv[:, cols], start=True, stop=True)
                    full_inc(m, name)

            def chunk(b, c):
                if c == 0:
                    pe.wait_ge(qlanes_ready, b + 1)
                    pe.wait_ge(*emptied(b, "kT"))
                for g in range(4):
                    name, half = f"r{4 * c + g}", slice(64 * (g // 2), 64 * (g // 2) + 64)
                    pe.wait_ge(*opened(b, name))
                    full_inc(PE.matmul(bank(name), kT[half, tile_of(c)],
                                       q_lanes[half, c, 4 * (g % 2):4 * (g % 2) + 4, :].rearrange("p r t -> p (r t)"),
                                       start=True, stop=True), name)
                if c < NT - 1:
                    if c == 0:
                        pe.wait_ge(*emptied(b, "v"))
                    pe.wait_ge(*opened(b, f"kv{c}"))
                    full_inc(PE.matmul(bank(f"kv{c}")[:, 0:D], k_dec[:, c, :], v_tm[:, c, :], start=True, stop=True),
                             f"kv{c}")
                if c:
                    ret_sum(b, c - 1)

            def ret_sum(b, c):
                ret = bank("ret")
                if c == 0:
                    pe.wait_ge(qdec_ready, b + 1)
                    pe.wait_ge(vlanes_ready, b + 1)
                    pe.wait_ge(*opened(b, "ret"))
                m = PE.matmul(ret[:, tile_of(c)], past[:], qT[:, tile_of(c)], start=True, stop=False)
                if c == 1:
                    pe.wait_ge(*emptied(b, "kv0"))
                if c >= 2:
                    pe.wait_ge(state_ready, 2 * b + c - 1)
                if c >= 1:
                    PE.matmul(ret[:, tile_of(c)], state[:, c - 1, :], q_dec[:, c, :], start=False, stop=False)
                pe.wait_ge(*emptied(b, f"r{4 * c + 2}"))
                pe.wait_ge(*emptied(b, f"r{4 * c + 3}"))
                for r in range(4):
                    for g in range(4):
                        at = slice(32 * g, 32 * g + 32)
                        m = PE.matmul(ret[at, tile_of(c)], v_lanes[:, c, r, at], probs[:, c % 2, 4 * g + r, :],
                                      start=False, stop=(r == 3))
                if c < 2:
                    m.then_inc(chunk_done, 1)
                if c == NT - 1:
                    full_inc(m, "ret")

            def gn_moments(b):
                pe.wait_ge(*opened(b, "gn"))
                pe.wait_ge(gstat_ready, b + 1)
                full_inc(PE.matmul(bank("gn")[:, 0:2], mean_of[:], gstat[:], start=True, stop=True), "gn")

            def gn_apply(b):
                pe.wait_ge(*opened(b, "retT"))
                pe.wait_ge(*emptied(b, "ret"))
                transposes(b, "retT", lambda j: retT[:, tile_of(j)])

            def router(b):
                pe.wait_ge(*opened(b, "router"))
                pe.wait_ge(*emptied(b, "xnT1"))
                for j in range(NT):
                    at = bank("router")[:, tile_of(j, NBLK)]
                    PE.matmul(at, xnT[:, tile_of(j)], w_router[:], start=True, stop=False)
                    m = PE.matmul(at, ones_row[:], b_router[:], start=False, stop=True)
                full_inc(m, "router")
                hidden_units(b, 0)
                hidden_units(b, 1)

            def hidden_units(b, k):
                pe.wait_ge(*opened(b, f"h{k}"))
                PE.matmul(bank(f"h{k}"), w1[:, tile_of(k)], xnT[:], start=True, stop=False)

            def drop_blocks(b, k):
                full_inc(PE.matmul(bank(f"h{k}"), blocks[:, tile_of(k)], dropT[:], start=False, stop=True), f"h{k}")

            def mlp(b):
                pe.wait_ge(*opened(b, "dropT"))
                pe.wait_ge(drop_ready, b + 1)
                for j in range(NT):
                    m = PE.matmul(bank("dropT")[0:NBLK, tile_of(j)], dropped[:, j, :], ident[:], start=True, stop=True)
                full_inc(m, "dropT")
                hidden_units(b, 2)
                pe.wait_ge(*emptied(b, "dropT"))
                drop_blocks(b, 0)
                drop_blocks(b, 1)
                drop_blocks(b, 2)
                hidden_units(b, 3)
                drop_blocks(b, 3)
                pe.wait_ge(*opened(b, "y0"))
                for k in range(4):
                    pe.wait_ge(*emptied(b, f"h{k}"))
                for j in range(NT):
                    at = bank("y0")[:, tile_of(j)]
                    for k in range(4):
                        PE.matmul(at, hidden[:, k, tile_of(j)], w2[:, k, :], start=(k == 0), stop=False)
                    m = PE.matmul(at, ones_row[:], b2[:], start=False, stop=True)
                full_inc(m, "y0")

            def latent(b):
                pe.wait_ge(*opened(b, "cT"))
                pe.wait_ge(*emptied(b, "xnT2"))
                full_inc(PE.matmul(bank("cT")[0:2 * LAT, :], w_down[:], xnT[:], start=True, stop=True), "cT")

            def rotate(b):
                for i in range(2):
                    for k, (name, weights) in enumerate(((f"qa{i}", wqa), (f"qb{i}", wqb))):
                        pe.wait_ge(*opened(b, name))
                        if i == 0 and k == 0:
                            pe.wait_ge(*emptied(b, "cT"))
                        m = PE.matmul(bank(name)[0:96, :], weights[:, i, :], cT[0:LAT, :], start=True, stop=True)
                        if i == 1:
                            m = PE.matmul(bank(name)[96:100, :], wkr[:, k, :], xnT[:], start=True, stop=True)
                        full_inc(m, name)

            def split(b):
                pe.wait_ge(*opened(b, "kn"))
                full_inc(PE.matmul(bank("kn"), wukv[LAT:2 * LAT, 0:D], cT[LAT:2 * LAT, :], start=True, stop=True), "kn")
                pe.wait_ge(*opened(b, "vv"))
                for j in range(NT):
                    m = PE.matmul(bank("vv")[:, tile_of(j)], cT[LAT:2 * LAT, tile_of(j)], wukv[LAT:2 * LAT, D:2 * D],
                                  start=True, stop=True)
                full_inc(m, "vv")

            def attend(b, lo, hi):
                for n in range(lo, hi):
                    q, un = divmod(n, QUAD_UNITS)
                    if n == 0:
                        pe.wait_ge(rows_in, 128 * (b + 1))
                    pe.wait_ge(*opened(b, f"s{n}"))
                    at = bank(f"s{n}")

                    def part(head, col, s, t0, t1):
                        h = 4 * q + head
                        r = slice(64 * (h // 8), 64 * (h // 8) + 36)
                        return PE.matmul(at[:, col:col + t1 - t0], ks[r, h % 8, tile_of(s)], qs[r, h % 8, t0:t1],
                                         start=True, stop=True)

                    kind, g = QUAD_KINDS[un]
                    if kind == "diag":
                        for s in range(NT):
                            m = part(g, TOK * s, s, TOK * s, TOK * s + TOK)
                    elif kind == "off":
                        part(g, 0, 0, TOK, T)
                        m = part(g, 384, 2, 3 * TOK, T)
                    else:
                        part(2 * g, 0, 1, 2 * TOK, T)
                        m = part(2 * g + 1, 256, 1, 2 * TOK, T)
                    full_inc(m, f"s{n}")
                    if q and un == 2:
                        weigh(b, q - 1)

            def weigh(b, q):
                u, s = q // 2, q % 2
                acc = bank(f"u{u}")
                if s == 0:
                    pe.wait_ge(*opened(b, f"u{u}"))
                if q == 0:
                    pe.wait_ge(*emptied(b, "vv"))
                pe.wait_ge(pt_ready, ATT * b + QUAD_UNITS * (q + 1))
                half = pt[:, q % 2, :, :]
                for kind, j in (("diag", 0), ("off", 0), ("diag", 1), ("second", 1), ("diag", 2), ("off", 2), ("diag", 3)):
                    for g in range(4):
                        if kind == "diag":
                            p, t0, t1 = half[:, UNIT_OF["diag", g], tile_of(j)], TOK * j, TOK * j + TOK
                        elif kind == "second":
                            at = 256 * (g % 2)
                            p, t0, t1 = half[:, UNIT_OF["second", g // 2], at:at + 256], 2 * TOK, T
                        elif j == 0:
                            p, t0, t1 = half[:, UNIT_OF["off", g], 0:384], TOK, T
                        else:
                            p, t0, t1 = half[:, UNIT_OF["off", g], 384:512], 3 * TOK, T
                        m = PE.matmul(acc[32 * g:32 * g + 32, t0:t1], vv[:, j, u, g, s, :], p,
                                      start=(s == 0 and kind == "diag" and j == 0),
                                      stop=(s == 1 and kind == "diag" and j == 3))
                m.then_inc(pv_done, 1)

            def turn_sums(b, u):
                pe.wait_ge(*opened(b, f"om{u}"))
                pe.wait_ge(*emptied(b, f"u{u}"))
                for j in range(NT):
                    m = PE.matmul(bank(f"om{u}")[:, 72 * j:72 * j + 72], u_sb[:, u, tile_of(j)], pick[:],
                                  start=True, stop=True)
                full_inc(m, f"om{u}")

            def sums(b):
                weigh(b, QUADS - 1)
                turn_sums(b, 0)
                turn_sums(b, 1)

            def output(b):
                pe.wait_ge(*opened(b, "onT"))
                pe.wait_ge(*emptied(b, "om0"))
                pe.wait_ge(*emptied(b, "om1"))
                transposes(b, "onT", lambda j: o_tm[:, j, :])
                pe.wait_ge(*opened(b, "y1"))
                pe.wait_ge(*emptied(b, "onT"))
                for j in range(NT):
                    m = PE.matmul(bank("y1")[:, tile_of(j)], oT[:, tile_of(j)], wo[:], start=True, stop=True)
                full_inc(m, "y1")

            def gate(b):
                pe.wait_ge(*opened(b, "gate"))
                pe.wait_ge(*emptied(b, "xnT3"))
                for j in range(NT):
                    m = PE.matmul(bank("gate")[:, tile_of(j, NE)], xnT3[:, tile_of(j)], w_gate[:], start=True, stop=True)
                full_inc(m, "gate")

            def route(b):
                pe.wait_ge(*opened(b, "rank"))
                pe.wait_ge(oh_ready, b + 1)
                for j in range(NT):
                    at = bank("rank")[:, tile_of(j, NQ)]
                    PE.matmul(at, upto[:], oh[:, j, :, :].rearrange("p k e -> p (k e)"), start=True, stop=False)
                    for i in range(j):
                        PE.matmul(at, ones[:], oh[:, i, :, :].rearrange("p k e -> p (k e)"), start=False, stop=False)
                    m = PE.matmul(at, ones[:], oh_past[:], start=False, stop=True)
                full_inc(m, "rank")

            stages = {"turn0": turn(0, xn_ready, 3, xn), "project": project, "chunk": chunk,
                      "last_sum": lambda b: ret_sum(b, NT - 1), "gn_moments": gn_moments, "gn_apply": gn_apply,
                      "turn1": turn(1, xn_ready, 3, xn), "router": router, "mlp": mlp,
                      "turn2": turn(2, xn_ready, 3, xn), "latent": latent, "rotate": rotate, "split": split,
                      "attend": attend, "sums": sums, "output": output, "turn3": turn(3, xn3_ready, 1, xn3),
                      "gate": gate, "route": route}
            pair_of_rows(stages, 0, None)
            with pe.Fori(1, B) as b:
                pair_of_rows(stages, b, b - 1)
            pair_of_rows(stages, None, B - 1)

            for k in range(TOPE):
                with pe.Fori(0, NE // 2) as i:
                    for w in range(2):
                        n = NE * k + 2 * i + w
                        pe.wait_ge(xqT_ready, n)
                        pe.wait_ge(xq_in[w], 16 * (NE // 2 * k + i + 1))
                        for j in range(CT):
                            m = PE.transpose(xqT_psum[:, tile_of(j)], xq[:, w, j, :], ident[:])
                        m.then_inc(xqT_ps, 1)
                        pe.wait_ge(wexp_in[w], 48 * (NE // 2 * k + i + 1))
                        pe.wait_ge(xqT_ready, n + 1)
                        for t in range(4):
                            half, mm = t // 2, t % 2
                            pe.wait_ge(gu_free, 4 * n + t + 1)
                            x_half = xqT[:, w, HALF * half:HALF * half + HALF]
                            PE.matmul(gu_ps[:, t % 2, 0:HALF], wg[:, w, tile_of(mm)], x_half, start=True, stop=True)
                            PE.matmul(gu_ps[:, t % 2, 512:512 + HALF], wu[:, w, tile_of(mm)], x_half,
                                      start=True, stop=True).then_inc(gu_full, 1)
                        pe.wait_ge(y_ready, n)
                        pe.wait_ge(gu_free, 4 * n + 6)
                        for j in range(CT):
                            for mm in range(2):
                                m = PE.matmul(y_ps[:, tile_of(j)], act_h[:, w, mm, tile_of(j)], wd[:, w, mm, :],
                                              start=(mm == 0), stop=(mm == 1))
                        m.then_inc(queue_done, 1)

        @block.vector
        def _(v):
            V.memset(oh_cnt[:], 0.0).then_inc(setup_v, 1)
            V.memset(oh_past[:], 0.0).then_inc(setup_v, 1)
            V.memset(fence_v[:], 0.0).then_inc(setup_v, 1)
            for k, (semaphore, amount) in enumerate([(gu_free, 2), (queue_done, 2), (x3_kept, 16), (route_kept, 16)] + [(free[k], 1) for k in range(4, 8)]):
                V.memset(credit[:, k:k + 1], 0.0).then_inc(semaphore, amount)
            v.wait_ge(setup_v, 3)
            v.wait_ge(const_in, N_CONST)
            v.wait_ge(setup_g, 9)
            class Steps:
                def __init__(self, sem, per_row):
                    self.sem, self.per_row, self.n = sem, per_row, 0

                def link(self, b, ins):
                    self.n += 1
                    ins.then_inc(self.sem, 1)
                    v.wait_ge(self.sem, b * self.per_row + self.n)

                def fence(self):
                    self.n += 1
                    V.memset(fence_v[:], 0.0).then_inc(self.sem, 1)

            front, back = Steps(front_step, FRONT_STEPS), Steps(back_step, BACK_STEPS)

            def read(b, name, ins):
                ins.then_inc(free[BANK[name]], 1)
                v.wait_ge(*emptied(b, name))

            def rsqrt(link, y, x, a):
                link(V.tensor_scalar(a.bitcast(i32), x.bitcast(i32), 1, None, ALU.logical_shift_right))
                link(V.tensor_scalar(y.bitcast(i32), a.bitcast(i32), -1.0, float(0x5F3759DF), ALU.mult, ALU.add))
                for _ in range(3):
                    link(V.tensor_tensor(a, y, y, ALU.mult))
                    link(V.scalar_tensor_tensor(out=a, in0=a, scalar=-0.5, in1=x, op0=ALU.mult, op1=ALU.mult))
                    link(V.scalar_tensor_tensor(out=y, in0=a, scalar=1.5, in1=y, op0=ALU.add, op1=ALU.mult))

            def layer_norm(steps, b, dst, src, st, m, n, y, a, ready):
                def link(ins):
                    steps.link(b, ins)
                for j in range(NT):
                    ins = V.bn_stats(st[:, j, :], src[:, j, :])
                link(ins)
                steps.fence()
                for j in range(NT):
                    ins = V.bn_aggr(m[:, j, :], st[:, j, :])
                link(ins)
                link(V.tensor_scalar(n[:], m[:, :, 1], EPS, None, ALU.add))
                rsqrt(link, y[:], n[:], a[:])
                for j in range(NT):
                    ins = V.tensor_scalar(dst[:, j, :], src[:, j, :], m[:, j, 0:1], y[:, j:j + 1],
                                          ALU.subtract, ALU.mult)
                ins.then_inc(ready, 1)

            def over_tiles(ap):
                return ap.unsqueeze(1).to_broadcast([TOK, NT, ap.shape[1]])

            def norm0(b):
                v.wait_ge(x_got, 16 * (b + 1))
                layer_norm(front, b, xn, x_in, stats, mv, nv, ny, na, xn_ready)

            def lanes(b):
                v.wait_ge(*emptied(b, "qT"))
                for r in range(8):
                    ins = V.tensor_scalar(q_lanes[:, :, r, :], tiles(qT[:]), lane[:, r:r + 1], None, ALU.mult)
                ins.then_inc(qlanes_ready, 1)
                V.tensor_tensor(q_dec[:], tiles(qT[:]), over_tiles(qdecay[:]), ALU.mult).then_inc(qdec_ready, 1)
                v.wait_ge(*filled(b, "ktm"))
                V.tensor_tensor(k_dec[:], tiles(bank("ktm")), over_tiles(kdecay[:]), ALU.mult)\
                 .then_inc(free[BANK["ktm"]], 1)
                v.wait_ge(*emptied(b, "v"))
                for r in range(4):
                    at = slice(8 * r, 8 * r + 8)
                    ins = V.tensor_copy(v_lanes[:, :, r, :].rearrange("p c (g w) -> p c g w", w=32)[:, :, :, at],
                                        v_tm[:].rearrange("p c (g w) -> p c g w", w=32)[:, :, :, at])
                ins.then_inc(vlanes_ready, 1)
                after(v, qlo_ready, 2 * b)

            def chunk(b, c):
                if c >= 2:
                    v.wait_ge(chunk_done, 2 * b + c - 1)
                for g in range(4):
                    name = f"r{4 * c + g}"
                    v.wait_ge(*filled(b, name))
                    V.tensor_tensor(probs[:, c % 2, 4 * g:4 * g + 4, :], bank(name).rearrange("p (h t) -> p h t", h=4),
                                    decay[:, 4 * g:4 * g + 4, :], ALU.mult).then_inc(free[BANK[name]], 1)
                if c < NT - 1:
                    v.wait_ge(*filled(b, f"kv{c}"))
                    dst = state[:, 0, :] if c == 0 else kv_own[:]
                    read(b, f"kv{c}", V.tensor_tensor(dst, bank(f"kv{c}")[:, 0:D], heads[:], ALU.mult))
                    if c:
                        V.scalar_tensor_tensor(out=state[:, c, :], in0=state[:, c - 1, :], scalar=gtile[:, 0:1],
                                               in1=kv_own[:], op0=ALU.mult, op1=ALU.add).then_inc(state_ready, 1)
                        v.wait_ge(state_ready, 2 * b + c)

            def gn_moments(b):
                v.wait_ge(*filled(b, "ret"))
                front.link(b, V.bn_stats(stats[:, 0, :], bank("ret")))
                front.fence()
                front.link(b, V.bn_aggr(gstat[:], stats[:, 0, :]))
                V.scalar_tensor_tensor(out=gstat[:, 1:2], in0=gstat[:, 0:1], scalar=gstat[:, 0:1], in1=gstat[:, 1:2],
                                       op0=ALU.mult, op1=ALU.add).then_inc(gstat_ready, 1)

            def gn_affine(b):
                def link(ins):
                    front.link(b, ins)
                v.wait_ge(*filled(b, "gn"))
                read(b, "gn", V.tensor_copy(gsum[:], bank("gn")[:, 0:2]))
                link(V.scalar_tensor_tensor(out=gtmp[:], in0=gsum[:, 0:1], scalar=gsum[:, 0:1], in1=gsum[:, 1:2],
                                            op0=ALU.mult, op1=ALU.subtract))
                link(V.tensor_scalar(gtmp[:], gtmp[:], -1.0, 0.0, ALU.mult, ALU.max))
                link(V.tensor_scalar(nv[:, 0:1], gtmp[:], EPS, None, ALU.add))
                rsqrt(link, ny[:, 0:1], nv[:, 0:1], na[:, 0:1])
                link(V.tensor_tensor(gscale[:], ny[:, 0:1], gn_w[:], ALU.mult))
                link(V.scalar_tensor_tensor(out=gtmp[:], in0=gsum[:, 0:1], scalar=-1.0, in1=gscale[:],
                                            op0=ALU.mult, op1=ALU.mult))
                V.tensor_tensor(gbias[:], gtmp[:], gn_b[:], ALU.add).then_inc(gaff_ready, 1)

            def gn_apply(b):
                v.wait_ge(*filled(b, "retT"))
                after(v, xb_taken, b)
                read(b, "retT", V.tensor_tensor(xr[:], x_in[:], tiles(bank("retT")), ALU.add))

            def norm(b):
                layer_norm(front, b, xn, xr, stats, mv, nv, ny, na, xn_ready)

            def best(b):
                def link(ins):
                    front.link(b, ins)
                v.wait_ge(*filled(b, "router"))
                read(b, "router", V.tensor_copy(logits[:], bank("router")[:, 0:NT * NBLK]
                                                .rearrange("p (j n) -> p j n", j=NT)))
                front.fence()
                for j in range(NT):
                    ins = V.max(top[:, j, :], logits[:, j, :])
                link(ins)
                front.fence()
                for j in range(NT):
                    ins = V.max_index(top_i[:, j, :], top[:, j, :], logits[:, j, :])
                link(ins)
                link(V.tensor_copy(top_f[:], top_i[:, :, 0:TOPB]))
                link(V.tensor_tensor(hits[:], iota[:].unsqueeze(1).unsqueeze(3).to_broadcast([TOK, NT, NBLK, TOPB]),
                                     top_f[:].unsqueeze(2).to_broadcast([TOK, NT, NBLK, TOPB]), ALU.is_equal))
                link(V.tensor_reduce(dropped[:], hits[:], AX.X, ALU.add))
                V.tensor_scalar(dropped[:], dropped[:], -1.0, None, ALU.add).then_inc(drop_ready, 1)

            def mlp(b):
                v.wait_ge(*filled(b, "y0"))
                read(b, "y0", V.tensor_tensor(xr[:], xr[:], tiles(bank("y0")), ALU.add))

            def rotate(b):
                for i in range(2):
                    n = 96 + ROPE * i
                    for name, dst, table in ((f"qa{i}", rot_a, cos), (f"qb{i}", rot_b, sin)):
                        v.wait_ge(*filled(b, name))
                        V.tensor_tensor(dst[0:n, i, :], bank(name)[0:n, :], table[0:n, i, :], ALU.mult)\
                         .then_inc(free[BANK[name]], 1)

            def split(b):
                v.wait_ge(khi_ready, b + 1)
                V.tensor_tensor(k_lo[:], bank("kn"), k_hi[:].bitcast(f32), ALU.subtract).then_inc(free[BANK["kn"]], 1)
                v.wait_ge(*filled(b, "vv"))
                after(v, pv_done, QUADS * b)
                for s in range(2):
                    ins = V.tensor_copy(vv[:].rearrange("p j u g s c -> p (j u) g s c")[:, :, :, s, 8 * s:8 * s + 8],
                                        bank("vv").rearrange("p (a s g e) -> p a s g e", a=2 * NT, s=2, g=4)[:, :, s])
                ins.then_inc(free[BANK["vv"]], 1)

            def take(b):
                v.wait_ge(x3_kept, 16 * (b + 1))
                V.tensor_scalar(xb[:], xr[:], 0.0, None, ALU.add).then_inc(xb_taken, 1)

            def attend(b, lo, hi):
                for n in range(lo, hi):
                    q, un = divmod(n, QUAD_UNITS)
                    v.wait_ge(*emptied(b, f"s{n}"))
                    p = pt[:, q % 2, un, :]
                    if QUAD_KINDS[un][0] == "diag":
                        ins = V.scalar_tensor_tensor(out=tiles(p), in0=tiles(p), scalar=P_LO, in1=over_tiles(causal[:]),
                                                     op0=ALU.max, op1=ALU.min)
                    else:
                        ins = V.tensor_scalar(p, p, P_LO, P_HI, ALU.max, ALU.min)
                    ins.then_inc(pt_ready, 1)

            def sums(b):
                v.wait_ge(fence_g, 2 * b + 1)
                for u in range(2):
                    v.wait_ge(*filled(b, f"om{u}"))
                    om = bank(f"om{u}")[:, 0:72 * NT].rearrange("p (j c) -> p j c", j=NT)
                    back.link(b, V.reciprocal(den_r[:, u, :, :], om[:, :, 8 * HD:72]))
                    V.tensor_tensor(o_tm[:, :, 64 * u:64 * u + 64].rearrange("p j (h e) -> p j h e", h=8),
                                    om[:, :, 0:8 * HD].rearrange("p j (h e) -> p j h e", h=8),
                                    den_r[:, u, :, :].unsqueeze(3).to_broadcast([TOK, NT, 8, HD]), ALU.mult)\
                     .then_inc(free[BANK[f"om{u}"]], 1)

            def output(b):
                v.wait_ge(*filled(b, "y1"))
                v.wait_ge(xb_taken, b + 1)
                read(b, "y1", V.tensor_tensor(xb[:], xb[:], tiles(bank("y1")), ALU.add))

            def norm3(b):
                layer_norm(back, b, xn3, xb, stats3, mv3, nv3, ny3, na3, xn3_ready)

            def gate(b):
                def link(ins):
                    back.link(b, ins)
                v.wait_ge(*filled(b, "gate"))
                read(b, "gate", V.tensor_copy(glog[:], bank("gate")[:, 0:NT * NE].rearrange("p (j n) -> p j n", j=NT)))
                back.fence()
                for j in range(NT):
                    ins = V.max(etop[:, j, :], glog[:, j, :])
                link(ins)
                V.tensor_tensor(esub[:], etop[:], etop[:, :, 0:1].to_broadcast([TOK, NT, 8]), ALU.subtract)\
                 .then_inc(esub_ready, 1)
                for j in range(NT):
                    ins = V.max_index(eidx[:, j, :], etop[:, j, :], glog[:, j, :])
                link(ins)
                link(V.tensor_copy(eidf[:], eidx[:, :, 0:TOPE]))
                V.tensor_tensor(oh[:], iota[:, 0:NE].unsqueeze(1).unsqueeze(1).to_broadcast([TOK, NT, TOPE, NE]),
                                eidf[:].unsqueeze(3).to_broadcast([TOK, NT, TOPE, NE]), ALU.is_equal)\
                 .then_inc(oh_ready, 1)

            def route_rows(b):
                def link(ins):
                    back.link(b, ins)
                v.wait_ge(eexp_ready, b + 1)
                link(V.tensor_reduce(esum[:], eexp[:], AX.X, ALU.add))
                link(V.reciprocal(esum[:], esum[:]))
                link(V.tensor_tensor(ew[:], eexp[:, :, 0:TOPE], esum[:].unsqueeze(2).to_broadcast([TOK, NT, TOPE]),
                                     ALU.mult))
                link(V.tensor_tensor(edn[:], ew[:, :, 0], ew[:, :, 1], ALU.add))
                link(V.tensor_scalar(edn[:], edn[:], 1e-9, None, ALU.add))
                link(V.reciprocal(edn[:], edn[:]))
                link(V.tensor_tensor(ew[:], ew[:], edn[:].unsqueeze(2).to_broadcast([TOK, NT, TOPE]), ALU.mult))
                v.wait_ge(*filled(b, "rank"))
                read(b, "rank", V.tensor_tensor(rank_oh[:], bank("rank")[:, 0:NT * NQ]
                                                .rearrange("p (j k e) -> p j k e", j=NT, k=TOPE), oh[:], ALU.mult))
                link(V.tensor_reduce(rank[:], rank_oh[:], AX.X, ALU.add))
                link(V.tensor_scalar(keep[:], rank[:], CAP + 0.5, None, ALU.is_le))
                link(V.scalar_tensor_tensor(out=slot[:], in0=eidf[:], scalar=float(CAP), in1=rank[:],
                                            op0=ALU.mult, op1=ALU.add))
                link(V.tensor_tensor(slot[:], slot[:], over_tiles(queue_of[:]), ALU.add))
                v.wait_ge(route_kept, 16 * (b + 1))
                slot_g = route[:, 0, :].rearrange("p (j k) -> p j k", j=NT)
                weight = route[:, 1, :].rearrange("p (j k) -> p j k", j=NT)
                link(V.tensor_tensor(slot_g, slot[:], keep[:], ALU.mult))
                link(V.scalar_tensor_tensor(out=slot[:], in0=keep[:], scalar=-PAST_END, in1=slot_g,
                                            op0=ALU.mult, op1=ALU.add))
                V.tensor_scalar(put_at[:], slot[:], PAST_END, None, ALU.add)
                V.tensor_tensor(weight, ew[:], keep[:], ALU.mult).then_inc(route_ready, 1)
                link(V.tensor_reduce(oh_row[:], oh[:].rearrange("p j k e -> p (k e) j"), AX.X, ALU.add))
                link(V.tensor_tensor(oh_cnt[:], oh_cnt[:], oh_row[:], ALU.add))
                link(V.tensor_copy(oh_past[:], oh_cnt[:]))

            stages = {"norm0": norm0, "lanes": lanes, "chunk": chunk, "gn_moments": gn_moments, "gn_affine": gn_affine,
                      "gn_apply": gn_apply, "norm1": norm, "best": best, "mlp": mlp, "norm2": norm, "rotate": rotate,
                      "split": split, "take": take, "attend": attend, "sums": sums, "output": output, "norm3": norm3,
                      "gate": gate, "route": route_rows}

            def rows(f, a):
                front.n = back.n = 0
                pair_of_rows(stages, f, a)

            rows(0, None)
            with v.Fori(1, B) as b:
                rows(b, b - 1)
            assert (front.n, back.n) == (FRONT_STEPS, BACK_STEPS), (front.n, back.n)
            rows(None, B - 1)

            for k in range(TOPE):
                with v.Fori(0, NE // 2) as i:
                    for w in range(2):
                        n = NE * k + 2 * i + w
                        v.wait_ge(queue_done, n + 1)
                        v.wait_ge(xqT_ps, n + 1)
                        V.tensor_copy(xqT[:, w, :], xqT_psum[:, 0:CAP]).then_inc(xqT_ready, 1)
                        for t in range(4):
                            half, mm = t // 2, t % 2
                            v.wait_ge(silu_ready, 4 * n + t + 1)
                            V.tensor_tensor(act_h[:, w, mm, HALF * half:HALF * half + HALF], act_g[:, t % 2, :],
                                            gu_ps[:, t % 2, 512:512 + HALF], ALU.mult).then_inc(gu_free, 1)
            v.wait_ge(route_kept, 16 * (B + 1))
            v.wait_ge(x3_kept, 16 * (B + 1))
            with v.Fori(0, B) as b:
                v.wait_ge(got, 16 * NT * TOPE * b)
                v.wait_ge(sum_ready, b)
                V.tensor_scalar(w_now[:], route_all[:, b, NT * TOPE:2 * NT * TOPE], 0.0, None, ALU.add)
                V.tensor_scalar(get_at[:], route_all[:, b, 0:NT * TOPE], 0.0, None, ALU.add).then_inc(at_ready, 1)
                v.wait_ge(at_ready, b + 1)
                v.wait_ge(got, 16 * NT * TOPE * (b + 1))
                v.wait_ge(x_got, 16 * (B + b + 1))
                for j in range(NT):
                    ins = V.scalar_tensor_tensor(out=y_part[:, j, :], in0=y_got[:, j, 0, :], scalar=w_now[:, 2 * j:2 * j + 1],
                                                 in1=x_late[:, j, :], op0=ALU.mult, op1=ALU.add)
                ins.then_inc(part_ready, 1)
                v.wait_ge(out_done, 16 * b)
                v.wait_ge(part_ready, b + 1)
                for j in range(NT):
                    ins = V.scalar_tensor_tensor(out=y_out[:, j, :], in0=y_got[:, j, 1, :],
                                                 scalar=w_now[:, 2 * j + 1:2 * j + 2],
                                                 in1=y_part[:, j, :], op0=ALU.mult, op1=ALU.add)
                ins.then_inc(sum_ready, 1)


def kernel(**inputs):
    import concourse.bacc as bacc
    from concourse.bass_utils import run_bass_kernel_spmd as run

    a = {k: np.asarray(v) for k, v in inputs.items()}
    wuq = a["L1_attn_W_UQ"].reshape(LAT, NH, HD)
    wqr = a["L1_attn_W_QR"].reshape(LAT, NH, ROPE)
    swap = [1, 0, 3, 2]
    wqb = np.zeros((LAT, NH, HROW), wuq.dtype)
    wqb[:, :, HD:] = wqr[:, :, swap]
    wkr = a["L1_attn_W_KR"]
    arrays = {
        "x": a["L0_attn_x"], "past_kv": a["L0_attn_past_kv"], "wqkv": a["L0_attn_W_qkv"],
        "gn_w": np.repeat(a["L0_attn_gn_weight"], HD)[:, None], "gn_b": np.repeat(a["L0_attn_gn_bias"], HD)[:, None],
        "w_router": a["L0_ffn_w_router"], "b_router": a["L0_ffn_b_router"][None, :],
        "w1": a["L0_ffn_w1"].T, "b1": a["L0_ffn_b1"].reshape(4, D).T, "w2": a["L0_ffn_w2"].T,
        "b2": a["L0_ffn_b2"][None, :],
        "w_down": np.concatenate([a["L1_attn_W_DQ"], a["L1_attn_W_DKV"]], axis=1),
        "wqa": np.concatenate([wuq, wqr], axis=2).reshape(LAT, NH * HROW), "wqb": wqb.reshape(LAT, NH * HROW),
        "wukv": np.concatenate([a["L1_attn_W_UK"], a["L1_attn_W_UV"]], axis=1),
        "wkr": np.concatenate([wkr, wkr[:, swap]], axis=1),
        "wo": a["L1_attn_W_O"], "w_gate": a["L1_ffn_gate_w"].T,
        "w_eg": a["L1_ffn_gate_proj_w"].transpose(0, 2, 1), "w_eu": a["L1_ffn_up_proj_w"].transpose(0, 2, 1),
        "w_ed": a["L1_ffn_down_proj_w"].transpose(0, 2, 1).reshape(NE, 2, D, D).transpose(0, 2, 1, 3)
        .reshape(NE, D, 2 * D),
        **constants(),
    }
    arrays = {f"in_{k}": np.ascontiguousarray(v) for k, v in arrays.items()}
    nc = bacc.Bacc("TRN2", target_bir_lowering=False, num_devices=1)
    io = {k[3:]: nc.dram_tensor(k, v.shape, mybir.dt.from_np(v.dtype), kind="ExternalInput").ap()
          for k, v in arrays.items()}
    out = nc.dram_tensor("out", (B, T, D), mybir.dt.float32, kind="ExternalOutput").ap()
    network(nc, io, out)
    return run(nc, [arrays], core_ids=[0]).results[0]["out"]
```

```python
import concourse.bass as bass
from concourse import mybir
from contextlib import ExitStack
import numpy as np

B, T, D = 8, 512, 128
TOK = 128
NT = T // TOK
NH, HD = 16, 8
ROPE = 4
HROW = HD + ROPE
LAT = 32
NBLK, TOPB, HID0 = 16, 4, 512
NE, TOPE, HID1 = 8, 2, 256
CAP = int(1.25 * B * T / NE)
NQ = TOPE * NE
SLOTS = NQ * CAP
CT = CAP // TOK
HALF = CAP // 2
EPS = 1e-5
DROP = 2.0 ** 100
CLIP = 80.0
PAST_END = float(2 ** 15)
QK_SCALE = 1.0 / float(np.sqrt(np.float32(HROW)))
P_LO = float(np.exp(-CLIP * QK_SCALE))
P_HI = float(np.exp(CLIP * QK_SCALE))


def constants():
    f = np.float32
    gamma = 1.0 - 2.0 ** (-5.0 - np.arange(NH, dtype=np.float64))
    t = np.arange(TOK)
    diff = t[None, :] - t[:, None]
    decay = np.where(diff[:, None, :] >= 0, gamma[None, :, None] ** np.maximum(diff, 0)[:, None, :], 0.0)
    head = np.arange(D) // HD
    cos, sin = np.ones((96 + ROPE, T)), np.zeros((96 + ROPE, T))
    inv = (np.float32(10000.0) ** (-np.arange(0, ROPE, 2, dtype=f) / f(ROPE))).astype(f)
    ang = (np.arange(T, dtype=f)[None, :] * inv[:, None]).astype(f).astype(np.float64)
    for r in range(9):
        for i in range(ROPE):
            row = r * HROW + HD + i if r < 8 else 8 * HROW + i
            cos[row] = np.cos(ang[i // 2])
            sin[row] = np.sin(ang[i // 2]) * (-1.0 if i % 2 == 0 else 1.0)
    pick = np.zeros((D, 8 * HD + 8))
    for g in range(4):
        for s in range(2):
            for e in range(HD):
                pick[32 * g + 8 * s + e, HD * (4 * s + g) + e] = 1.0
            pick[32 * g + 16 + s, 8 * HD + 4 * s + g] = 1.0
    blocks = np.zeros((NBLK, HID0))
    for n in range(NBLK):
        blocks[n, n * 32:(n + 1) * 32] = DROP
    return {
        "c_decay": decay.astype(f),
        "c_qdecay": (gamma[head][:, None] ** t[None, :]).astype(f),
        "c_kdecay": (gamma[head][None, :] ** (TOK - t)[:, None]).astype(f),
        "c_gtile": (gamma[head] ** TOK).astype(f)[:, None],
        "c_heads": (head[:, None] == head[None, :]).astype(f),
        "c_cos": cos.astype(f), "c_sin": sin.astype(f),
        "c_pick": pick.astype(f),
        "c_blocks": blocks.astype(f),
        "c_ident": np.eye(D, dtype=f),
        "c_causal": (P_HI * (diff >= 0)).astype(f),
        "c_upto": (diff >= 0).astype(f),
        "c_iota": np.tile(np.arange(NBLK, dtype=f)[None, :], (D, 1)),
        "c_queue": np.tile(np.array([-1.0 + k * NE * CAP for k in range(TOPE)], f)[None, :], (D, 1)),
    }


QUADS, QUAD_UNITS = NH // 4, 10
QUAD_KINDS = [("first", 0), ("second", 0), ("first", 1), ("second", 1), ("third", 0),
              ("first", 2), ("second", 2), ("first", 3), ("second", 3), ("third", 1)]
UNIT_OF = {kind: n for n, kind in enumerate(QUAD_KINDS)}
ATT = QUADS * QUAD_UNITS
WEIGH_AT = 5
LAST_ROWS = [(0, 4), (4, 7), (7, 8)]
TILES_USES = [(name, k % 3) for k, name in enumerate(
    [name for c in range(NT) for name in [f"r{4 * c + g}" for g in range(4)] + [f"kv{c}"] * (c < NT - 1)])]
NEXT = [("xnT0", 0), ("qT", 1), ("kT", 3), ("v", 0), ("ktm", 2)], TILES_USES[:7]
FRONT_USES = ([("ret", 3)] + TILES_USES[7:]
              + [("gn", 1), ("retT", 2), ("xnT1", 0), ("router", 1), ("h0", 2), ("h1", 0), ("dropT", 3), ("h2", 1),
                 ("h3", 3), ("y0", 2)] + NEXT[0]
              + [("xnT2", 0), ("qa0", 3), ("qb0", 1), ("qa1", 2), ("qb1", 0), ("kn", 3), ("vv", 2)] + NEXT[1])
BACK_USES = ([(f"s{n}", 4 + n % 3) for n in range(ATT)]
             + [("u0", 7), ("u1", 7), ("om0", 5), ("om1", 6), ("onT", 4), ("y1", 5), ("xnT3", 6), ("gate", 4),
                ("rank", 5)])
USES = FRONT_USES + BACK_USES
BANK = dict(USES)
PER_BANK = [sum(b == k for _, b in USES) for k in range(8)]
CREDIT = [0] * 4 + [1] * 4


def uses_before(b, name):
    bank = BANK[name]
    start_uses = [n for part in NEXT for n, k in part if k == bank]
    last = isinstance(b, int) and b == B - 1
    uses = [n for n, k in USES if k == bank and not (last and n in start_uses and name not in start_uses)]
    nth = uses.index(name)
    if name not in start_uses:
        return b * PER_BANK[bank] + nth + len(start_uses)
    if isinstance(b, int) and b == 0:
        return start_uses.index(name)
    return (b - 1) * PER_BANK[bank] + nth + len(start_uses)


START_STEPS, FRONT_STEPS, BACK_STEPS = 14, 53, 36

def attend(lo, hi):
    return [("back", "attend", lo, hi)]


def stage_order():
    order = [("back", "take")] + attend(0, 3)
    done = 3
    for c in range(1, NT):
        for g in range(4):
            if (c, g) >= (1, 2):
                order.append(("front", "score", c, g))
                order += attend(done, done + 1)
                done += 1
        order.append(("front", "state", c))
    order += attend(done, 15)
    order += [("front", "last_sum"), ("front", "gn_moments"), ("front", "gn_affine")] + attend(15, 20)
    order += [("front", "gn_apply"), ("front", "norm1")] + attend(20, 26)
    order += [("front", "turn1"), ("front", "router"), ("front", "best")] + attend(26, 30)
    order += [("next", "norm0"), ("front", "mlp"), ("next", "turn0"), ("front", "norm2"), ("next", "project"),
              ("next", "lanes")]
    order += attend(30, 34) + [("front", "turn2"), ("front", "rotate")] + attend(34, 40)
    order += [("front", "split"), ("front", "keys"), ("back", "last_weigh"), ("back", "sums"), ("front", "values"),
              ("back", "output"), ("back", "norm3"), ("next", "score", 0, 0), ("next", "score", 0, 1),
              ("back", "turn3"), ("back", "gate"), ("next", "score", 0, 2), ("next", "score", 0, 3),
              ("next", "state", 0), ("next", "score", 1, 0), ("next", "score", 1, 1), ("back", "route")]
    return order


ORDER = stage_order()


def network(nc, io, out):
    f32, f32r, bf16 = mybir.dt.float32, mybir.dt.float32r, mybir.dt.bfloat16
    i32, u32 = mybir.dt.int32, mybir.dt.uint32
    ALU, ACT, AX = mybir.AluOpType, mybir.ActivationFunctionType, mybir.AxisListType
    V, S, PE, G = nc.vector, nc.scalar, nc.tensor, nc.gpsimd
    ctx = ExitStack()
    with ctx:
        def sb(name, shape, dt=f32):
            return ctx.enter_context(nc.sbuf_tensor(name, shape, dt))

        def sem(name):
            return ctx.enter_context(nc.semaphore(name))

        def dram(name, shape):
            return nc.dram_tensor(name, shape, f32, kind="Internal").ap()

        q_rows = dram("q_rows", [NH, 2, HROW, T])
        k_rows = dram("k_rows", [NH, 2, HROW, T])
        r_rows = dram("r_rows", [4, D, T])
        queue_x = dram("queue_x", [SLOTS, D])
        queue_y = dram("queue_y", [SLOTS, D])
        x_mid = dram("x_mid", [B, TOK, NT * D])

        decay = sb("decay", [TOK, NH, TOK])
        qdecay = sb("qdecay", [D, TOK])
        kdecay = sb("kdecay", [TOK, D])
        gtile = sb("gtile", [D, 1])
        heads = sb("heads", [D, D])
        cos, sin = sb("cos", [96 + ROPE, T]), sb("sin", [96 + ROPE, T])
        pick, ident = sb("pick", [D, 8 * HD + 8]), sb("ident", [D, D])
        blocks = sb("blocks", [NBLK, HID0], bf16)
        causal = sb("causal", [TOK, TOK])
        upto = sb("upto", [TOK, TOK], bf16)
        ones = sb("ones", [TOK, TOK], bf16)
        mean_of = sb("mean_of", [D, D])
        iota = sb("iota", [D, NBLK])
        queue_of = sb("queue_of", [D, TOPE])
        wqkv = sb("wqkv", [D, 3 * D])
        past = sb("past", [D, D])
        gn_w, gn_b = sb("gn_w", [D, 1]), sb("gn_b", [D, 1])
        w_router, b_router = sb("w_router", [D, NBLK]), sb("b_router", [TOK, NBLK])
        w1, b1 = sb("w1", [D, HID0]), sb("b1", [D, 4])
        w2, b2 = sb("w2", [D, 4, D]), sb("b2", [TOK, D])
        w_q, w_kv = sb("w_q", [D, 4, 96 + ROPE]), sb("w_kv", [D, 2 * D])
        wo = sb("wo", [D, D])
        w_gate = sb("w_gate", [D, NE])

        x_in = sb("x_in", [TOK, NT, D])
        xr, xb = sb("xr", [TOK, NT, D]), sb("xb", [TOK, NT, D])
        xn = sb("xn", [TOK, NT, D])
        xn3 = sb("xn3", [TOK, NT, D])
        xnT = sb("xnT", [D, T])
        stats, mv = sb("stats", [TOK, NT, 6]), sb("mv", [TOK, NT, 2])
        nv, ny, na = sb("nv", [TOK, NT]), sb("ny", [TOK, NT]), sb("na", [TOK, NT])
        stats3, mv3 = sb("stats3", [TOK, NT, 6]), sb("mv3", [TOK, NT, 2])
        nv3, ny3, na3 = sb("nv3", [TOK, NT]), sb("ny3", [TOK, NT]), sb("na3", [TOK, NT])
        gstat, gsum = sb("gstat", [D, 2]), sb("gsum", [D, 2])
        gscale, gbias, gtmp = sb("gscale", [D, 1]), sb("gbias", [D, 1]), sb("gtmp", [D, 1])
        fence_v, credit, pool_one = sb("fence_v", [1, 1]), sb("credit", [1, 10]), sb("pool_one", [1, 1])
        qT = sb("qT", [D, T])
        qe, ke = sb("qe", [64 + 48, 4, 2, T], f32r), sb("ke", [64 + 48, 4, T], f32r)
        q_dec = sb("q_dec", [D, NT, TOK])
        v_tm, k_dec = sb("v_tm", [TOK, NT, D]), sb("k_dec", [TOK, NT, D])
        v_lanes = sb("v_lanes", [TOK, NT, 4, D])
        probs = sb("probs", [TOK, 2, NH, TOK])
        state, kv_own = sb("state", [D, 3, D]), sb("kv_own", [D, D])
        retT = sb("retT", [D, T])
        logits = sb("logits", [TOK, NT, NBLK])
        top, top_i, top_f = sb("top", [TOK, NT, 8]), sb("top_i", [TOK, NT, 8], u32), sb("top_f", [TOK, NT, TOPB])
        hits, dropped = sb("hits", [TOK, NT, NBLK, TOPB]), sb("dropped", [TOK, NT, NBLK])
        dropT = sb("dropT", [NBLK, T], bf16)
        hidden = probs[:, 0, :, :].rearrange("p (m a) t -> p m (a t)", m=4)
        rot_a = probs[0:100, 0, 0:8, :].rearrange("p (i a) t -> p i (a t)", i=2)
        rot_b = probs[0:100, 1, 0:8, :].rearrange("p (i a) t -> p i (a t)", i=2)
        rot_s = rot_a
        q_hi, q_lo = sb("q_hi", [D, 2, T], f32r), sb("q_lo", [D, 2, T], f32r)
        r_hi, r_lo = q_hi, q_lo
        k_hi, k_lo = sb("k_hi", [D, T], f32r), sb("k_lo", [D, T], f32r)
        qs, ks = sb("qs", [D, NH // 2, T], f32r), sb("ks", [D, NH // 2, T], f32r)
        vv = sb("vv", [TOK, NT, 2, 4, 2, 32])
        pt = sb("pt", [TOK, 2, QUAD_UNITS, 512])
        u_sb = sb("u_sb", [D, 2, T])
        oT, xnT3 = u_sb[:, 0, :], u_sb[:, 1, :]
        o_tm = xn3
        den_r = sb("den_r", [TOK, 2, NT, 8])
        glog = sb("glog", [TOK, NT, NE])
        etop, eidx = sb("etop", [TOK, NT, 8]), sb("eidx", [TOK, NT, 8], u32)
        eidf = sb("eidf", [TOK, NT, TOPE])
        esub, eexp = sb("esub", [TOK, NT, 8]), sb("eexp", [TOK, NT, 8])
        esum, ew, edn = sb("esum", [TOK, NT]), sb("ew", [TOK, NT, TOPE]), sb("edn", [TOK, NT])
        oh = sb("oh", [TOK, NT, TOPE, NE], bf16)
        oh_cnt = sb("oh_cnt", [TOK, NQ])
        oh_past = sb("oh_past", [TOK, NQ], bf16)
        rank_oh, rank = sb("rank_oh", [TOK, NT, TOPE, NE]), sb("rank", [TOK, NT, TOPE])
        keep, slot = sb("keep", [TOK, NT, TOPE]), sb("slot", [TOK, NT, TOPE])
        oh_row = sb("oh_row", [TOK, NQ])
        route = sb("route", [TOK, 2, NT * TOPE])
        put_at = sb("put_at", [TOK, NT, TOPE], u32)
        route_all = sb("route_all", [TOK, B, 2 * NT * TOPE])

        late = pt[:].rearrange("p a u c -> p (a u c)")
        taken = [0]

        def part_of_late(*shape):
            size = int(np.prod(shape))
            at = taken[0]
            taken[0] += size
            assert taken[0] <= 2 * QUAD_UNITS * 512
            names = "abc"[:len(shape)]
            return late[:, at:at + size].rearrange(f"p ({' '.join(names)}) -> p {' '.join(names)}",
                                                   **dict(zip(names, shape)))

        wg, wu, wd = part_of_late(2, HID1), part_of_late(2, HID1), part_of_late(2, 2, D)
        xq, xqT = part_of_late(2, CT, D), part_of_late(2, CAP)
        act_g, act_h = part_of_late(2, HALF), part_of_late(2, 2, CAP)
        yq = part_of_late(2, CT, D)
        get_at = sb("get_at", [TOK, B, NT * TOPE], u32)
        y_got = [m[:].bitcast(f32).rearrange("p h t -> p (h t)").rearrange("p (b c) -> p b c", b=B) for m in (qs, ks)]
        x_sum = probs[:].rearrange("p a h t -> p (a h t)").rearrange("p (b c) -> p b c", b=B)

        blocks32, upto32 = pt[0:NBLK, 1, 0, :], pt[:, 1, 1, 0:TOK]
        w_dqT, w_dkvT, past_rows = pt[0:LAT, 1, 1, D:2 * D], pt[0:LAT, 1, 1, 2 * D:3 * D], pt[:, 1, 1, 3 * D:3 * D + HD]
        w_uq, w_ukv = pt[0:LAT, 1, 2, 0:4 * 96], pt[0:LAT, 1, 3, 0:2 * D]

        ps = ctx.enter_context(nc.psum_tensor("ps", [128, 8, 512], f32))
        gu_ps = ps[:, 0:4, :].rearrange("p (t a) c -> p t (a c)", t=2)
        xqT_psum = ps[:, 4:6, :].rearrange("p a c -> p (a c)")
        y_ps = ps[:, 6:8, :].rearrange("p a c -> p (a c)")

        const_in, first_const_in, x_got = sem("const_in"), sem("first_const_in"), sem("x_got")
        setup_v, setup_g, setup_s = sem("setup_v"), sem("setup_g"), sem("setup_s")
        weights_full = sem("weights_full")
        lanes_zeroed = sem("lanes_zeroed")
        queue_zeroed, qe_zeroed, zeros_ready = sem("queue_zeroed"), sem("qe_zeroed"), sem("zeros_ready")
        full = [sem(f"bank_full{k}") for k in range(8)]
        free = [sem(f"bank_free{k}") for k in range(8)]
        start_step, front_step, back_step = sem("start_step"), sem("front_step"), sem("back_step")
        xn_ready = [sem(f"norm{k}_ready") for k in range(4)]
        r_qhi_ready, r_khi_ready, r_rows_out, r_rows_in = (sem("r_qhi_ready"), sem("r_khi_ready"), sem("r_rows_out"),
                                                           sem("r_rows_in"))
        qT_ready = sem("qT_ready")
        qdec_ready = sem("qdec_ready")
        state_ready, chunk_done = sem("state_ready"), sem("chunk_done")
        bias_added = sem("bias_added")
        gstat_ready, gaff_ready, drop_ready = sem("gstat_ready"), sem("gaff_ready"), sem("drop_ready")
        rotsum_ready, qhi_ready, qlo_ready, khi_ready = (sem("rotsum_ready"), sem("qhi_ready"), sem("qlo_ready"),
                                                         sem("khi_ready"))
        rows_out, rows_in = sem("rows_out"), sem("rows_in")
        pt_ready, pv_done = sem("pt_ready"), sem("pv_done")
        xb_taken = sem("xb_taken")
        x3_kept, esub_ready, eexp_ready, oh_ready = sem("x3_kept"), sem("esub_ready"), sem("eexp_ready"), sem("oh_ready")
        route_ready, route_kept = sem("route_ready"), sem("route_kept")
        fence_g, scattered = sem("fence_g"), [sem(f"scattered{k}") for k in range(TOPE)]
        wgu_in, wd_in, xq_in, y_kept = ([sem(f"{name}{w}") for w in range(2)]
                                        for name in ("wgu_in", "wd_in", "xq_in", "y_kept"))
        xqT_ps, xqT_ready = sem("xqT_ps"), sem("xqT_ready")
        gu_free, queue_done = sem("gate_up_free"), sem("queue_done")
        gu_full, silu_ready, y_ready = sem("gate_up_full"), sem("silu_ready"), sem("y_ready")
        got_first, got = sem("got_first"), [sem(f"got{g}") for g in range(len(LAST_ROWS))]
        slots_ready, x_back, part_ready, sum_ready, out_done = (sem("slots_ready"), sem("x_back"), sem("part_ready"),
                                                                sem("sum_ready"), sem("out_done"))

        block = ctx.enter_context(nc.Block())

        def after(engine, semaphore, value):
            if not isinstance(value, int) or value > 0:
                engine.wait_ge(semaphore, value)

        def rows_together(stages, f, a, n):
            rows = {"front": f, "back": a, "next": n}
            for part, name, *which in ORDER:
                if rows[part] is not None and name in stages:
                    stages[name](rows[part], *which)

        def bank(name):
            return ps[:, BANK[name], :]

        def filled(b, name):
            return full[BANK[name]], uses_before(b, name) + 1

        def opened(b, name):
            return free[BANK[name]], uses_before(b, name) + CREDIT[BANK[name]]

        def emptied(b, name):
            return free[BANK[name]], uses_before(b, name) + CREDIT[BANK[name]] + 1

        def tiles(ap):
            return ap.rearrange("p (j c) -> p j c", j=NT)

        def tile_of(j, width=TOK):
            return slice(j * width, (j + 1) * width)

        first_consts = [(ident[:], io["c_ident"]), (wqkv[:], io["wqkv"])]
        sync_consts = [(kdecay[:], io["c_kdecay"]), (qdecay[:], io["c_qdecay"]), (decay[:], io["c_decay"]),
                       (heads[:], io["c_heads"]), (past_rows, io["past_kv"].rearrange("h d e -> (h d) e")),
                       (gtile[:], io["c_gtile"]), (gn_w[:], io["gn_w"]), (gn_b[:], io["gn_b"])]
        act_consts = [(w_dqT, io["w_dqT"]), (w_dkvT, io["w_dkvT"]), (w_uq, io["w_uq"]), (w_ukv, io["w_ukv"]),
                      (blocks32, io["c_blocks"]), (upto32, io["c_upto"]),
                      (w_router[:], io["w_router"]), (b_router[:], io["b_router"]), (w1[:], io["w1"]), (b1[:], io["b1"]),
                      (w2[:], io["w2"].rearrange("(m p) d -> p m d", m=4)), (b2[:], io["b2"]), (iota[:], io["c_iota"]),
                      (w_q[:, 1:4:2, 96:], io["wkr"].rearrange("p (a r) -> p a r", a=2)),
                      (cos[:], io["c_cos"]), (sin[:], io["c_sin"]), (pick[:], io["c_pick"]),
                      (causal[:], io["c_causal"]), (queue_of[:], io["c_queue"]), (wo[:], io["wo"]),
                      (w_gate[:], io["w_gate"])]
        N_FIRST, N_CONST = 16 * len(first_consts), 16 * (len(sync_consts) + len(act_consts))
        R_ROWS_IN = 16 * 18
        x_rows = io["x"].rearrange("b (j p) c -> b p j c", p=TOK)
        out_rows = out.rearrange("b (j p) c -> b p j c", p=TOK)
        queue_x_n = queue_x.rearrange("(n p j) c -> n p (j c)", p=TOK, j=CT)
        queue_y_n = queue_y.rearrange("(n p j) c -> n p (j c)", p=TOK, j=CT)

        @block.sync
        def _(sp):
            sp.dma_start(x_in[:], x_rows[0]).then_inc(x_got, 16)
            for dst, src in first_consts:
                sp.dma_start(dst, src).then_inc(first_const_in, 16)
            for dst, src in sync_consts:
                sp.dma_start(dst, src).then_inc(const_in, 16)

            def next_x(b):
                sp.wait_ge(*emptied(b, "retT"))
                sp.dma_start(x_in[:], x_rows[b + 1]).then_inc(x_got, 16)

            def retention_rows(b):
                for row, (ready, src) in enumerate(((( r_qhi_ready, b + 1), r_hi[:, 0, :]), (emptied(b, "qT"), r_lo[:, 0, :]),
                                                    ((r_khi_ready, b + 1), r_hi[:, 1, :]),
                                                    (emptied(b, "kT"), r_lo[:, 1, :]))):
                    sp.wait_ge(*ready)
                    sp.dma_start(r_rows[row], src.bitcast(f32)).then_inc(r_rows_out, 16)
                sp.wait_ge(r_rows_out, 64 * (b + 1))
                for p in range(2):
                    for part, (q_from, k_from) in enumerate(((0, 2), (1, 2), (0, 3))):
                        at = 64 * p + 16 * part
                        half = slice(64 * p, 64 * p + 64)
                        sp.dma_start(ke[at:at + 16, :, :].bitcast(f32),
                                     r_rows[k_from, half, :].rearrange("(g r) t -> r g t", g=4)).then_inc(r_rows_in, 16)
                        for r in range(2):
                            sp.dma_start(qe[at + 8 * r:at + 8 * r + 8, :, r, :].bitcast(f32),
                                         r_rows[q_from, half, :].rearrange("(g r e) t -> r e g t", g=4, r=2)[r])\
                              .then_inc(r_rows_in, 16)

            def rows_to_heads(b):
                for i in range(2):
                    hs = slice(8 * i, 8 * i + 8)
                    sp.wait_ge(qhi_ready, 2 * b + i + 1)
                    sp.dma_start(q_rows[hs, 0, :, :], q_hi[0:96, i, :].bitcast(f32)).then_inc(rows_out, 16)
                    sp.wait_ge(qlo_ready, 2 * b + i + 1)
                    sp.dma_start(q_rows[hs, 1, :, :], q_lo[0:96, i, :].bitcast(f32)).then_inc(rows_out, 16)
                if not isinstance(b, int) or b:
                    sp.wait_ge(*filled(b - 1, f"s{ATT - 1}"))
                for part, rope_rows in ((0, q_hi), (1, q_lo)):
                    sp.dma_start(k_rows[:, part, HD:HROW, :].rearrange("h d t -> d h t"),
                                 rope_rows[96:100, 1, :].bitcast(f32).unsqueeze(1).to_broadcast([ROPE, NH, T]))\
                      .then_inc(rows_out, 16)
                sp.wait_ge(khi_ready, b + 1)
                sp.dma_start(k_rows[:, 0, 0:HD, :], k_hi[:].bitcast(f32)).then_inc(rows_out, 16)
                sp.wait_ge(*emptied(b, "kn"))
                sp.dma_start(k_rows[:, 1, 0:HD, :], k_lo[:].bitcast(f32)).then_inc(rows_out, 16)
                sp.wait_ge(rows_out, 128 * (b + 1))
                for i in range(2):
                    at, hs = 64 * i, slice(8 * i, 8 * i + 8)
                    sp.dma_start(qs[at:at + 24, :, :].bitcast(f32),
                                 q_rows[hs].rearrange("h a d t -> h (a d) t").rearrange("h r t -> r h t"))\
                      .then_inc(rows_in, 16)
                    sp.dma_start(qs[at + 24:at + 36, :, :].bitcast(f32), q_rows[hs, 0].rearrange("h r t -> r h t"))\
                      .then_inc(rows_in, 16)
                    sp.dma_start(ks[at:at + 12, :, :].bitcast(f32), k_rows[hs, 0].rearrange("h r t -> r h t"))\
                      .then_inc(rows_in, 16)
                    sp.dma_start(ks[at + 12:at + 36, :, :].bitcast(f32),
                                 k_rows[hs].rearrange("h a d t -> h (a d) t").rearrange("h r t -> r h t"))\
                      .then_inc(rows_in, 16)

            def keep_x(b):
                sp.wait_ge(*emptied(b, "y1"))
                sp.dma_start(x_mid[b], xb[:].rearrange("p j c -> p (j c)")).then_inc(x3_kept, 16)

            def keep_route(b):
                sp.wait_ge(route_ready, b + 1)
                sp.dma_start(route_all[:, b, :], route[:].rearrange("p a c -> p (a c)")).then_inc(route_kept, 16)

            sp.wait_ge(qe_zeroed, 1)
            retention_rows(0)
            next_x(0)
            retention_rows(1)
            rows_to_heads(0)
            with sp.Fori(1, B - 1) as b:
                next_x(b)
                retention_rows(b + 1)
                rows_to_heads(b)
                keep_x(b - 1)
                keep_route(b - 1)
            rows_to_heads(B - 1)
            keep_x(B - 2)
            keep_route(B - 2)
            keep_x(B - 1)
            keep_route(B - 1)

            def load_expert(w):
                sp.dma_start(wg[:, w, :], io["w_eg"][w]).then_inc(wgu_in[w], 16)
                sp.dma_start(wu[:, w, :], io["w_eu"][w]).then_inc(wgu_in[w], 16)
                sp.dma_start(wd[:, w, :, :].rearrange("p m d -> p (m d)"), io["w_ed"][w]).then_inc(wd_in[w], 16)

            def load_queue(i, w, k):
                n, e = 2 * i + w, 2 * i + w - NE * k
                sp.wait_ge(xqT_ps, n - 1)
                sp.dma_start(xq[:, w, :, :].rearrange("p j c -> p (j c)"), queue_x_n[n]).then_inc(xq_in[w], 16)
                sp.wait_ge(gu_full, 4 * n - 4)
                sp.dma_start(wg[:, w, :], io["w_eg"][e]).then_inc(wgu_in[w], 16)
                sp.dma_start(wu[:, w, :], io["w_eu"][e]).then_inc(wgu_in[w], 16)
                sp.wait_ge(queue_done, n + 1)
                sp.dma_start(wd[:, w, :, :].rearrange("p m d -> p (m d)"), io["w_ed"][e]).then_inc(wd_in[w], 16)

            sp.wait_ge(pv_done, QUADS * B)
            for w in range(2):
                load_expert(w)
            for k in range(TOPE):
                sp.wait_ge(scattered[k], 16 * NT * B)
                if k == 0:
                    for w in range(2):
                        sp.dma_start(xq[:, w, :, :].rearrange("p j c -> p (j c)"), queue_x_n[w]).then_inc(xq_in[w], 16)
                with sp.Fori(NE // 2 * k + (k == 0), NE // 2 * (k + 1)) as i:
                    for w in range(2):
                        load_queue(i, w, k)
            sp.wait_ge(x3_kept, 16 * (B + 1))
            sp.dma_start(x_sum, x_mid.rearrange("b p c -> p b c")).then_inc(x_back, 16)
            for lo, hi in LAST_ROWS:
                sp.wait_ge(sum_ready, hi)
                for b in range(lo, hi):
                    sp.dma_start(out_rows[b], x_sum[:, b, :].rearrange("p (j c) -> p j c", j=NT)).then_inc(out_done, 16)
            sp.wait_ge(out_done, 16 * B)

        @block.gpsimd
        def _(pool):
            G.memset(qe[:].bitcast(f32), 0.0).then_inc(qe_zeroed, 1)
            G.memset(v_lanes[:], 0.0).then_inc(lanes_zeroed, 1)
            G.memset(ones[:], 1.0).then_inc(setup_g, 1)
            G.memset(mean_of[:], 1.0 / D).then_inc(setup_g, 1)
            G.memset(vv[:], 0.0).then_inc(setup_g, 1)
            G.memset(pool_one[:], 0.0).then_inc(fence_g, 1)
            G.memset(late[:, 0:1024], 0.0).then_inc(zeros_ready, 1)
            pool.wait_ge(setup_g, 3)
            for s in range(2):
                G.memset(vv[:, :, :, :, s, 16 + s:17 + s], 1.0).then_inc(setup_g, 1)
            def best(b):
                pool.wait_ge(xn_ready[1], b + 1)
                G.tensor_tensor(xr[:], xr[:], b2[:].unsqueeze(1).to_broadcast([TOK, NT, D]), ALU.add)\
                 .then_inc(bias_added, 1)

            def lanes(b):
                pool.wait_ge(qT_ready, b + 1)
                G.tensor_tensor(q_dec[:], tiles(qT[:]), qdecay[:].unsqueeze(1).to_broadcast([D, NT, TOK]), ALU.mult)\
                 .then_inc(qdec_ready, 1)

            def rotate(b):
                for i in range(2):
                    n = 96 + ROPE * i
                    pool.wait_ge(*emptied(b, f"qa{i}"))
                    pool.wait_ge(*emptied(b, f"qb{i}"))
                    G.tensor_tensor(rot_s[0:n, i, :], rot_a[0:n, i, :], rot_b[0:n, i, :], ALU.add)\
                     .then_inc(rotsum_ready, 1)

            def split(b):
                for i in range(2):
                    n = 96 + ROPE * i
                    pool.wait_ge(qhi_ready, 2 * b + i + 1)
                    G.tensor_tensor(q_lo[0:n, i, :], rot_s[0:n, i, :], q_hi[0:n, i, :].bitcast(f32), ALU.subtract)\
                     .then_inc(qlo_ready, 1)

            def route_rows(b):
                pool.wait_ge(fence_g, 2 * b + 1)
                pool.wait_ge(route_ready, b + 1)
                G.tensor_tensor(pool_one[:], pool_one[:], pool_one[:], ALU.add).then_inc(fence_g, 1)
                pool.wait_ge(queue_zeroed, 16 * (SLOTS // 1024))
                for k in range(TOPE):
                    for j in range(NT):
                        pool.indirect_dma_start(queue_x[:, :], bass.IndirectOffsetOnAxis(ap=put_at[:, j, k:k + 1], axis=0),
                                                xn3[:, j, :], None, bounds_check=SLOTS - 1, oob_is_err=False)\
                            .then_inc(scattered[k], 16)
                pool.wait_ge(fence_g, 2 * b + 2)
                pool.wait_ge(scattered[0], 16 * NT * (b + 1))
                pool.wait_ge(scattered[1], 16 * NT * (b + 1))
                G.tensor_tensor(pool_one[:], pool_one[:], pool_one[:], ALU.add).then_inc(fence_g, 1)

            stages = {"best": best, "lanes": lanes, "rotate": rotate, "split": split, "route": route_rows}
            pool.wait_ge(const_in, N_CONST)
            rows_together(stages, None, None, 0)
            rows_together(stages, 0, None, 1)
            with pool.Fori(1, B - 1) as b:
                rows_together(stages, b, b - 1, b + 1)
            rows_together(stages, B - 1, B - 2, None)
            rows_together(stages, None, B - 1, None)
            pool.wait_ge(slots_ready, 1)
            for k in range(TOPE):
                for w in range(2):
                    pool.wait_ge(y_kept[w], 16 * (NE // 2 * (k + 1) + 1))
                for group, (lo, hi) in enumerate(LAST_ROWS):
                    for b in range(lo, hi):
                        for j in range(NT):
                            pool.indirect_dma_start(y_got[k][:, b, tile_of(j)], None, queue_y[0:NE * CAP * (k + 1), :],
                                                    bass.IndirectOffsetOnAxis(ap=get_at[:, b, 2 * j + k:2 * j + k + 1],
                                                                              axis=0),
                                                    bounds_check=NE * CAP * (k + 1) - 1, oob_is_err=False)\
                                .then_inc(got_first if k == 0 else got[group], 16)

        @block.scalar
        def _(act):
            for dst, src in act_consts:
                act.dma_start(dst, src).then_inc(const_in, 16)

            def copy_out(b, name, dst, src):
                act.wait_ge(*filled(b, name))
                S.activation(dst, src, ACT.Copy).then_inc(free[BANK[name]], 1)

            def turn(k, dst):
                return lambda b: copy_out(b, f"xnT{k}", dst, bank(f"xnT{k}"))

            def take(b):
                act.wait_ge(x3_kept, 16 * (b + 1))
                act.wait_ge(*emptied(b, "y0"))
                S.activation(xb[:], xr[:], ACT.Copy).then_inc(xb_taken, 1)

            def values(b):
                after(act, pv_done, QUADS * b)
                act.wait_ge(*filled(b, "vv"))
                for s in range(2):
                    ins = S.activation(vv[:].rearrange("p j u g s c -> p (j u) g s c")[:, :, :, s, 8 * s:8 * s + 8],
                                       bank("vv").rearrange("p (a s g e) -> p a s g e", a=2 * NT, s=2, g=4)[:, :, s],
                                       ACT.Copy)
                ins.then_inc(free[BANK["vv"]], 1)

            def project(b):
                act.wait_ge(*filled(b, "qT"))
                S.activation(r_hi[:, 0, :], bank("qT"), ACT.Copy).then_inc(r_qhi_ready, 1)
                S.activation(qT[:], bank("qT"), ACT.Copy).then_inc(qT_ready, 1)
                act.wait_ge(*filled(b, "kT"))
                S.activation(r_hi[:, 1, :], bank("kT"), ACT.Copy).then_inc(r_khi_ready, 1)
                if isinstance(b, int) and b == 0:
                    act.wait_ge(lanes_zeroed, 1)
                act.wait_ge(*filled(b, "v"))
                for r in range(4):
                    at = slice(8 * r, 8 * r + 8)
                    S.activation(v_lanes[:, :, r, :].rearrange("p c (g w) -> p c g w", w=32)[:, :, :, at],
                                 tiles(bank("v")).rearrange("p c (g w) -> p c g w", w=32)[:, :, :, at], ACT.Copy)
                S.activation(v_tm[:], tiles(bank("v")), ACT.Copy).then_inc(free[BANK["v"]], 1)

            def gn_apply(b):
                act.wait_ge(gaff_ready, b + 1)
                S.activation(retT[:], bank("ret"), ACT.Identity, bias=gbias[:, 0:1], scale=gscale[:, 0:1])\
                 .then_inc(free[BANK["ret"]], 1)

            def mlp(b):
                copy_out(b, "dropT", dropT[:], bank("dropT")[0:NBLK, :])
                for m in range(4):
                    act.wait_ge(*filled(b, f"h{m}"))
                    S.activation(hidden[:, m, :], bank(f"h{m}"), ACT.Relu, bias=b1[:, m:m + 1])\
                     .then_inc(free[BANK[f"h{m}"]], 1)

            def split(b):
                act.wait_ge(r_rows_out, 64 * (B if isinstance(b, int) and b == B - 1 else b + 2))
                for i in range(2):
                    n = 96 + ROPE * i
                    act.wait_ge(rotsum_ready, 2 * b + i + 1)
                    S.activation(q_hi[0:n, i, :], rot_s[0:n, i, :], ACT.Copy).then_inc(qhi_ready, 1)

            def keys(b):
                act.wait_ge(*filled(b, "kn"))
                S.activation(k_hi[:], bank("kn"), ACT.Copy).then_inc(khi_ready, 1)

            def attend(b, lo, hi):
                for n in range(lo, hi):
                    q, un = divmod(n, QUAD_UNITS)
                    if un == 0 and q >= 2:
                        act.wait_ge(pv_done, QUADS * b + q - 1)
                    act.wait_ge(*filled(b, f"s{n}"))
                    S.activation(pt[:, q % 2, un, :], bank(f"s{n}"), ACT.Exp, scale=QK_SCALE)\
                     .then_inc(free[BANK[f"s{n}"]], 1)
                    if n == 2 * QUAD_UNITS + WEIGH_AT + 2:
                        copy_sums(b, 0)

            def copy_sums(b, u):
                act.wait_ge(pv_done, QUADS * b + 2 * u + 2)
                S.activation(u_sb[:, u, :], bank(f"u{u}"), ACT.Copy).then_inc(free[BANK[f"u{u}"]], 1)

            def output(b):
                copy_out(b, "onT", oT, bank("onT"))

            def route(b):
                act.wait_ge(esub_ready, b + 1)
                S.activation(eexp[:], esub[:], ACT.Exp).then_inc(eexp_ready, 1)

            stages = {"turn0": turn(0, xnT[:]), "take": take, "values": values, "project": project,
                      "gn_apply": gn_apply, "turn1": turn(1, xnT[:]), "mlp": mlp,
                      "turn2": turn(2, xnT[:]), "split": split, "keys": keys, "attend": attend,
                      "sums": lambda b: copy_sums(b, 1), "output": output, "turn3": turn(3, xnT3), "route": route}
            rows_together(stages, None, None, 0)
            act.wait_ge(const_in, N_CONST)
            S.activation(blocks[:], blocks32, ACT.Copy).then_inc(setup_s, 1)
            S.activation(upto[:], upto32, ACT.Copy).then_inc(setup_s, 1)
            act.wait_ge(weights_full, 1)
            S.activation(w_q[:, :, 0:96], ps[:, 6, 0:4 * 96].rearrange("p (i r) -> p i r", i=4), ACT.Copy)\
             .then_inc(setup_s, 1)
            S.activation(w_kv[:], ps[:, 7, 0:2 * D], ACT.Copy).then_inc(setup_s, 1)
            act.wait_ge(setup_g, 5)
            act.wait_ge(zeros_ready, 1)
            for z in range(SLOTS // 1024):
                act.dma_start(queue_x[1024 * z:1024 * z + 1024, :].rearrange("(p r) c -> p (r c)", r=8),
                              late[:, 0:1024]).then_inc(queue_zeroed, 16)
            rows_together(stages, 0, None, 1)
            act.wait_ge(queue_zeroed, 16 * (SLOTS // 1024))
            act.wait_ge(setup_v, 4)
            with act.Fori(1, B - 1) as b:
                rows_together(stages, b, b - 1, b + 1)
            rows_together(stages, B - 1, B - 2, None)
            rows_together(stages, None, B - 1, None)

            def keep_results(i, w):
                n = 2 * i + w
                act.wait_ge(y_kept[w], 16 * i + 16)
                act.wait_ge(queue_done, n + 3)
                S.activation(yq[:, w, :, :].rearrange("p j c -> p (j c)"), y_ps[:, 0:CAP], ACT.Copy).then_inc(y_ready, 1)
                act.wait_ge(y_ready, n + 1)
                act.dma_start(queue_y_n[n], yq[:, w, :, :].rearrange("p j c -> p (j c)")).then_inc(y_kept[w], 16)

            def act_pair(i):
                for w in range(2):
                    n = 2 * i + w
                    for t in range(4):
                        act.wait_ge(gu_free, 4 * n + t + 1)
                        act.wait_ge(gu_full, 4 * n + t + 1)
                        S.activation(act_g[:, t % 2, :], gu_ps[:, t % 2, 0:HALF], ACT.Silu).then_inc(silu_ready, 1)
                    if w or not isinstance(i, int) or i:
                        keep_results(i if w else i - 1, 1 - w)

            act_pair(0)
            with act.Fori(1, NQ // 2 - 1) as i:
                act_pair(i)
            act_pair(NQ // 2 - 1)
            keep_results(NQ // 2 - 1, 1)

        @block.tensor
        def _(pe):
            pe.wait_ge(first_const_in, N_FIRST)

            def full_inc(m, name):
                m.then_inc(full[BANK[name]], 1)

            def transposes(b, name, src):
                for j in range(NT):
                    m = PE.transpose(bank(name)[:, tile_of(j)], src(j), ident[:])
                full_inc(m, name)

            def turn(k, src):
                def stage(b):
                    after(pe, *opened(b, f"xnT{k}"))
                    pe.wait_ge(xn_ready[k], b + 1)
                    transposes(b, f"xnT{k}", lambda j: src[:, j, :])
                return stage

            def project(b):
                after(pe, *opened(b, "qT"))
                pe.wait_ge(*emptied(b, "xnT0"))
                full_inc(PE.matmul(bank("qT"), wqkv[:, 0:D], xnT[:], start=True, stop=True), "qT")
                after(pe, *opened(b, "kT"))
                full_inc(PE.matmul(bank("kT"), wqkv[:, D:2 * D], xnT[:], start=True, stop=True), "kT")
                for name, cols in (("v", slice(2 * D, 3 * D)), ("ktm", slice(D, 2 * D))):
                    after(pe, *opened(b, name))
                    for j in range(NT):
                        m = PE.matmul(bank(name)[:, tile_of(j)], xnT[:, tile_of(j)], wqkv[:, cols], start=True, stop=True)
                    full_inc(m, name)

            def score(b, c, g):
                if c == 0 and g == 0:
                    pe.wait_ge(r_rows_in, R_ROWS_IN * (b + 1))
                name, half = f"r{4 * c + g}", slice(64 * (g // 2), 64 * (g // 2) + 48)
                after(pe, *opened(b, name))
                for i in range(2):
                    two = 2 * (g % 2) + i
                    m = PE.matmul(bank(name)[:, 256 * i:256 * i + 256], ke[half, two, tile_of(c)],
                                  qe[half, two, :, tile_of(c)], start=True, stop=True)
                full_inc(m, name)

            def chunk_state(b, c):
                if c < NT - 1:
                    if c == 0:
                        pe.wait_ge(*emptied(b, "v"))
                    after(pe, *opened(b, f"kv{c}"))
                    full_inc(PE.matmul(bank(f"kv{c}")[:, 0:D], k_dec[:, c, :], v_tm[:, c, :], start=True, stop=True),
                             f"kv{c}")
                if c:
                    ret_sum(b, c - 1)

            def ret_sum(b, c):
                ret = bank("ret")
                if c == 0:
                    pe.wait_ge(qT_ready, b + 1)
                    pe.wait_ge(qdec_ready, b + 1)
                    after(pe, *opened(b, "ret"))
                m = PE.matmul(ret[:, tile_of(c)], past[:], qT[:, tile_of(c)], start=True, stop=False)
                if c == 1:
                    pe.wait_ge(*emptied(b, "kv0"))
                if c >= 2:
                    pe.wait_ge(state_ready, 2 * b + c - 1)
                if c >= 1:
                    PE.matmul(ret[:, tile_of(c)], state[:, c - 1, :], q_dec[:, c, :], start=False, stop=False)
                pe.wait_ge(*emptied(b, f"r{4 * c + 2}"))
                pe.wait_ge(*emptied(b, f"r{4 * c + 3}"))
                for r in range(4):
                    for g in range(4):
                        at = slice(32 * g, 32 * g + 32)
                        m = PE.matmul(ret[at, tile_of(c)], v_lanes[:, c, r, at], probs[:, c % 2, 4 * g + r, :],
                                      start=False, stop=(r == 3))
                if c < 2:
                    m.then_inc(chunk_done, 1)
                if c == NT - 1:
                    full_inc(m, "ret")

            def gn_moments(b):
                after(pe, *opened(b, "gn"))
                pe.wait_ge(gstat_ready, b + 1)
                full_inc(PE.matmul(bank("gn")[:, 0:2], mean_of[:], gstat[:], start=True, stop=True), "gn")

            def gn_apply(b):
                after(pe, *opened(b, "retT"))
                pe.wait_ge(*emptied(b, "ret"))
                transposes(b, "retT", lambda j: retT[:, tile_of(j)])

            def router(b):
                after(pe, *opened(b, "router"))
                pe.wait_ge(*emptied(b, "xnT1"))
                for j in range(NT):
                    at = bank("router")[:, tile_of(j, NBLK)]
                    m = PE.matmul(at, xnT[:, tile_of(j)], w_router[:], start=True, stop=True)
                full_inc(m, "router")
                hidden_units(b, 0)
                hidden_units(b, 1)

            def hidden_units(b, k):
                after(pe, *opened(b, f"h{k}"))
                PE.matmul(bank(f"h{k}"), w1[:, tile_of(k)], xnT[:], start=True, stop=False)

            def drop_blocks(b, k):
                full_inc(PE.matmul(bank(f"h{k}"), blocks[:, tile_of(k)], dropT[:], start=False, stop=True), f"h{k}")

            def mlp(b):
                after(pe, *opened(b, "dropT"))
                pe.wait_ge(drop_ready, b + 1)
                for j in range(NT):
                    m = PE.matmul(bank("dropT")[0:NBLK, tile_of(j)], dropped[:, j, :], ident[:], start=True, stop=True)
                full_inc(m, "dropT")
                hidden_units(b, 2)
                pe.wait_ge(*emptied(b, "dropT"))
                drop_blocks(b, 0)
                drop_blocks(b, 1)
                drop_blocks(b, 2)
                hidden_units(b, 3)
                drop_blocks(b, 3)
                after(pe, *opened(b, "y0"))
                for k in range(4):
                    pe.wait_ge(*emptied(b, f"h{k}"))
                    for j in range(NT):
                        m = PE.matmul(bank("y0")[:, tile_of(j)], hidden[:, k, tile_of(j)], w2[:, k, :],
                                      start=(k == 0 and j == 0),
                                      stop=(k == 3 and j == NT - 1))
                full_inc(m, "y0")

            def rotate(b):
                pe.wait_ge(*emptied(b, "xnT2"))
                for i in range(2):
                    n = 96 + ROPE * i
                    for k, name in enumerate((f"qa{i}", f"qb{i}")):
                        after(pe, *opened(b, name))
                        full_inc(PE.matmul(bank(name)[0:n, :], w_q[:, 2 * k + i, 0:n], xnT[:], start=True, stop=True),
                                 name)

            def keys(b):
                after(pe, *opened(b, "kn"))
                full_inc(PE.matmul(bank("kn"), w_kv[:, 0:D], xnT[:], start=True, stop=True), "kn")

            def values(b):
                after(pe, *opened(b, "vv"))
                for j in range(NT):
                    m = PE.matmul(bank("vv")[:, tile_of(j)], xnT[:, tile_of(j)], w_kv[:, D:2 * D], start=True, stop=True)
                full_inc(m, "vv")

            def attend(b, lo, hi):
                for n in range(lo, hi):
                    q, un = divmod(n, QUAD_UNITS)
                    if n == 0:
                        pe.wait_ge(rows_in, 128 * (b + 1))
                    after(pe, *opened(b, f"s{n}"))
                    at = bank(f"s{n}")

                    def part(head, col, s, t0, t1):
                        h = 4 * q + head
                        r = slice(64 * (h // 8), 64 * (h // 8) + 36)
                        return PE.matmul(at[:, col:col + t1 - t0], ks[r, h % 8, tile_of(s)], qs[r, h % 8, t0:t1],
                                         start=True, stop=True)

                    kind, g = QUAD_KINDS[un]
                    if kind == "first":
                        m = part(g, 0, 0, 0, T)
                    elif kind == "second":
                        part(g, 0, 1, TOK, T)
                        m = part(g, 384, 3, 3 * TOK, T)
                    else:
                        part(2 * g, 0, 2, 2 * TOK, T)
                        m = part(2 * g + 1, 256, 2, 2 * TOK, T)
                    full_inc(m, f"s{n}")
                    if q and un == WEIGH_AT:
                        weigh(b, q - 1)

            def weigh(b, q):
                u, s = q // 2, q % 2
                acc = bank(f"u{u}")
                if s == 0:
                    after(pe, *opened(b, f"u{u}"))
                if q == 0:
                    pe.wait_ge(*emptied(b, "vv"))
                pe.wait_ge(pt_ready, ATT * b + QUAD_UNITS * (q + 1))
                half = pt[:, q % 2, :, :]
                for j in range(NT):
                    for g in range(4):
                        if j == 0:
                            p = half[:, UNIT_OF["first", g], :]
                        elif j == 2:
                            p = half[:, UNIT_OF["third", g // 2], 256 * (g % 2):256 * (g % 2) + 256]
                        else:
                            p = half[:, UNIT_OF["second", g], 0:384] if j == 1 else \
                                half[:, UNIT_OF["second", g], 384:512]
                        m = PE.matmul(acc[32 * g:32 * g + 32, TOK * j:T], vv[:, j, u, g, s, :], p,
                                      start=(s == 0 and j == 0), stop=(s == 1 and j == NT - 1))
                m.then_inc(pv_done, 1)

            def turn_sums(b, u):
                after(pe, *opened(b, f"om{u}"))
                pe.wait_ge(*emptied(b, f"u{u}"))
                for j in range(NT):
                    m = PE.matmul(bank(f"om{u}")[:, 72 * j:72 * j + 72], u_sb[:, u, tile_of(j)], pick[:],
                                  start=True, stop=True)
                full_inc(m, f"om{u}")

            def sums(b):
                turn_sums(b, 0)
                turn_sums(b, 1)

            def output(b):
                after(pe, *opened(b, "onT"))
                pe.wait_ge(*emptied(b, "om0"))
                pe.wait_ge(*emptied(b, "om1"))
                transposes(b, "onT", lambda j: o_tm[:, j, :])
                after(pe, *opened(b, "y1"))
                pe.wait_ge(*emptied(b, "onT"))
                for j in range(NT):
                    m = PE.matmul(bank("y1")[:, tile_of(j)], oT[:, tile_of(j)], wo[:], start=True, stop=True)
                full_inc(m, "y1")

            def gate(b):
                after(pe, *opened(b, "gate"))
                pe.wait_ge(*emptied(b, "xnT3"))
                for j in range(NT):
                    m = PE.matmul(bank("gate")[:, tile_of(j, NE)], xnT3[:, tile_of(j)], w_gate[:], start=True, stop=True)
                full_inc(m, "gate")

            def route(b):
                after(pe, *opened(b, "rank"))
                pe.wait_ge(oh_ready, b + 1)
                for j in range(NT):
                    at = bank("rank")[:, tile_of(j, NQ)]
                    PE.matmul(at, upto[:], oh[:, j, :, :].rearrange("p k e -> p (k e)"), start=True, stop=False)
                    for i in range(j):
                        PE.matmul(at, ones[:], oh[:, i, :, :].rearrange("p k e -> p (k e)"), start=False, stop=False)
                    m = PE.matmul(at, ones[:], oh_past[:], start=False, stop=True)
                full_inc(m, "rank")

            stages = {"turn0": turn(0, xn), "project": project, "score": score, "state": chunk_state,
                      "last_sum": lambda b: ret_sum(b, NT - 1), "gn_moments": gn_moments, "gn_apply": gn_apply,
                      "turn1": turn(1, xn), "router": router, "mlp": mlp,
                      "turn2": turn(2, xn), "rotate": rotate, "keys": keys, "values": values,
                      "attend": attend, "last_weigh": lambda b: weigh(b, QUADS - 1), "sums": sums,
                      "output": output, "turn3": turn(3, xn3),
                      "gate": gate, "route": route}
            rows_together(stages, None, None, 0)
            pe.wait_ge(const_in, N_CONST)
            PE.matmul(ps[:, 6, 0:4 * 96], w_dqT, w_uq, start=True, stop=True)
            PE.matmul(ps[:, 7, 0:2 * D], w_dkvT, w_ukv, start=True, stop=True).then_inc(weights_full, 1)
            pe.wait_ge(setup_s, 4)
            pe.wait_ge(setup_g, 5)
            pe.wait_ge(setup_v, 4)
            rows_together(stages, 0, None, 1)
            with pe.Fori(1, B - 1) as b:
                rows_together(stages, b, b - 1, b + 1)
            rows_together(stages, B - 1, B - 2, None)
            rows_together(stages, None, B - 1, None)

            def turn_queue(i, w, first=False):
                n = 2 * i + w
                if not first:
                    pe.wait_ge(xqT_ready, n)
                pe.wait_ge(xq_in[w], 16 * (i + 1))
                for j in range(CT):
                    m = PE.transpose(xqT_psum[:, tile_of(j)], xq[:, w, j, :], ident[:])
                m.then_inc(xqT_ps, 1)

            def gate_up(i, w, t):
                n, half, mm = 2 * i + w, t // 2, t % 2
                if t == 0:
                    pe.wait_ge(wgu_in[w], 32 * (i + 1))
                    pe.wait_ge(xqT_ready, n + 1)
                pe.wait_ge(gu_free, 4 * n + t + 1)
                x_half = xqT[:, w, HALF * half:HALF * half + HALF]
                PE.matmul(gu_ps[:, t % 2, 0:HALF], wg[:, w, tile_of(mm)], x_half, start=True, stop=True)
                PE.matmul(gu_ps[:, t % 2, 512:512 + HALF], wu[:, w, tile_of(mm)], x_half,
                          start=True, stop=True).then_inc(gu_full, 1)

            def down(i, w, lo, hi):
                n = 2 * i + w
                if lo == 0:
                    pe.wait_ge(wd_in[w], 16 * (i + 1))
                    after(pe, y_ready, n)
                    pe.wait_ge(gu_free, 4 * n + 6)
                for j in range(lo, hi):
                    for mm in range(2):
                        m = PE.matmul(y_ps[:, tile_of(j)], act_h[:, w, mm, tile_of(j)], wd[:, w, mm, :],
                                      start=(mm == 0), stop=(mm == 1))
                if hi == CT:
                    m.then_inc(queue_done, 1)

            def pe_pair(i):
                for w in range(2):
                    before = None if isinstance(i, int) and i == 0 and w == 0 else (i if w else i - 1, 1 - w)
                    gate_up(i, w, 0)
                    gate_up(i, w, 1)
                    if before:
                        down(*before, 0, 3)
                    gate_up(i, w, 2)
                    gate_up(i, w, 3)
                    if before:
                        down(*before, 3, CT)
                    if not (w and isinstance(i, int) and i == NQ // 2 - 1):
                        turn_queue(i + w, 1 - w)

            turn_queue(0, 0, first=True)
            pe_pair(0)
            with pe.Fori(1, NQ // 2 - 1) as i:
                pe_pair(i)
            pe_pair(NQ // 2 - 1)
            down(NQ // 2 - 1, 1, 0, CT)

        @block.vector
        def _(v):
            V.memset(oh_cnt[:], 0.0).then_inc(setup_v, 1)
            V.memset(oh_past[:], 0.0).then_inc(setup_v, 1)
            V.memset(fence_v[:], 0.0).then_inc(setup_v, 1)
            for k, (semaphore, amount) in enumerate([(gu_free, 2), (queue_done, 2), (x3_kept, 16), (route_kept, 16),
                                                     (y_kept[0], 16), (y_kept[1], 16)] + [(free[k], 1) for k in range(4, 8)]):
                V.memset(credit[:, k:k + 1], 0.0).then_inc(semaphore, amount)
            v.wait_ge(setup_v, 3)
            class Steps:
                def __init__(self, sem, per_row):
                    self.sem, self.per_row, self.n = sem, per_row, 0

                def link(self, b, ins):
                    self.n += 1
                    ins.then_inc(self.sem, 1)
                    v.wait_ge(self.sem, b * self.per_row + self.n)

                def fence(self):
                    self.n += 1
                    V.memset(fence_v[:], 0.0).then_inc(self.sem, 1)

            start, front, back = (Steps(start_step, START_STEPS), Steps(front_step, FRONT_STEPS),
                                  Steps(back_step, BACK_STEPS))

            def read(b, name, ins):
                ins.then_inc(free[BANK[name]], 1)
                v.wait_ge(*emptied(b, name))

            def rsqrt(link, y, x, a):
                link(V.tensor_scalar(y.bitcast(i32), x.bitcast(i32), -0.5, float(0x5F3759DF), ALU.mult, ALU.add))
                for _ in range(3):
                    link(V.tensor_tensor(a, y, y, ALU.mult))
                    link(V.scalar_tensor_tensor(out=a, in0=a, scalar=-0.5, in1=x, op0=ALU.mult, op1=ALU.mult))
                    link(V.scalar_tensor_tensor(out=y, in0=a, scalar=1.5, in1=y, op0=ALU.add, op1=ALU.mult))

            def layer_norm(steps, b, dst, src, st, m, n, y, a, ready):
                def link(ins):
                    steps.link(b, ins)
                for j in range(NT):
                    ins = V.bn_stats(st[:, j, :], src[:, j, :])
                link(ins)
                steps.fence()
                for j in range(NT):
                    ins = V.bn_aggr(m[:, j, :], st[:, j, :])
                link(ins)
                link(V.tensor_scalar(n[:], m[:, :, 1], EPS, None, ALU.add))
                rsqrt(link, y[:], n[:], a[:])
                for j in range(NT):
                    ins = V.tensor_scalar(dst[:, j, :], src[:, j, :], m[:, j, 0:1], y[:, j:j + 1],
                                          ALU.subtract, ALU.mult)
                ins.then_inc(ready, 1)

            def over_tiles(ap):
                return ap.unsqueeze(1).to_broadcast([TOK, NT, ap.shape[1]])

            def norm0(b):
                v.wait_ge(x_got, 16 * (b + 1))
                layer_norm(start, b, xn, x_in, stats, mv, nv, ny, na, xn_ready[0])

            def lanes(b):
                if isinstance(b, int) and b == 0:
                    v.wait_ge(const_in, N_CONST)
                    v.wait_ge(setup_g, 5)
                    V.scalar_tensor_tensor(out=past[:].rearrange("p (h e) -> p h e", h=NH),
                                           in0=past_rows.unsqueeze(1).to_broadcast([D, NH, HD]), scalar=float(NH * HD),
                                           in1=heads[:].rearrange("p (h e) -> p h e", h=NH), op0=ALU.mult,
                                           op1=ALU.mult).then_inc(setup_v, 1)
                for k, (name, hi_ready) in enumerate((("qT", r_qhi_ready), ("kT", r_khi_ready))):
                    v.wait_ge(qT_ready if k == 0 else hi_ready, b + 1)
                    V.tensor_tensor(r_lo[:, k, :], bank(name), r_hi[:, k, :].bitcast(f32), ALU.subtract)\
                     .then_inc(free[BANK[name]], 1)
                v.wait_ge(*filled(b, "ktm"))
                V.tensor_tensor(k_dec[:], tiles(bank("ktm")), over_tiles(kdecay[:]), ALU.mult)\
                 .then_inc(free[BANK["ktm"]], 1)
            def score(b, c, g):
                if c == 0 and g == 0:
                    after(v, qlo_ready, 2 * b)
                if c >= 2 and g == 0:
                    v.wait_ge(chunk_done, 2 * b + c - 1)
                name = f"r{4 * c + g}"
                v.wait_ge(*filled(b, name))
                V.tensor_tensor(probs[:, c % 2, 4 * g:4 * g + 4, :], bank(name).rearrange("p (h t) -> p h t", h=4),
                                decay[:, 4 * g:4 * g + 4, :], ALU.mult).then_inc(free[BANK[name]], 1)

            def chunk_state(b, c):
                if c < NT - 1:
                    v.wait_ge(*filled(b, f"kv{c}"))
                    dst = state[:, 0, :] if c == 0 else kv_own[:]
                    read(b, f"kv{c}", V.tensor_tensor(dst, bank(f"kv{c}")[:, 0:D], heads[:], ALU.mult))
                    if c:
                        V.scalar_tensor_tensor(out=state[:, c, :], in0=state[:, c - 1, :], scalar=gtile[:, 0:1],
                                               in1=kv_own[:], op0=ALU.mult, op1=ALU.add).then_inc(state_ready, 1)
                        v.wait_ge(state_ready, 2 * b + c)

            def gn_moments(b):
                v.wait_ge(*filled(b, "ret"))
                front.link(b, V.bn_stats(stats[:, 0, :], bank("ret")))
                front.fence()
                front.link(b, V.bn_aggr(gstat[:], stats[:, 0, :]))
                V.scalar_tensor_tensor(out=gstat[:, 1:2], in0=gstat[:, 0:1], scalar=gstat[:, 0:1], in1=gstat[:, 1:2],
                                       op0=ALU.mult, op1=ALU.add).then_inc(gstat_ready, 1)

            def gn_affine(b):
                def link(ins):
                    front.link(b, ins)
                v.wait_ge(*filled(b, "gn"))
                read(b, "gn", V.tensor_copy(gsum[:], bank("gn")[:, 0:2]))
                link(V.scalar_tensor_tensor(out=gtmp[:], in0=gsum[:, 0:1], scalar=gsum[:, 0:1], in1=gsum[:, 1:2],
                                            op0=ALU.mult, op1=ALU.subtract))
                link(V.tensor_scalar(gtmp[:], gtmp[:], -1.0, 0.0, ALU.mult, ALU.max))
                link(V.tensor_scalar(nv[:, 0:1], gtmp[:], EPS, None, ALU.add))
                rsqrt(link, ny[:, 0:1], nv[:, 0:1], na[:, 0:1])
                link(V.tensor_tensor(gscale[:], ny[:, 0:1], gn_w[:], ALU.mult))
                link(V.scalar_tensor_tensor(out=gtmp[:], in0=gsum[:, 0:1], scalar=-1.0, in1=gscale[:],
                                            op0=ALU.mult, op1=ALU.mult))
                V.tensor_tensor(gbias[:], gtmp[:], gn_b[:], ALU.add).then_inc(gaff_ready, 1)

            def gn_apply(b):
                v.wait_ge(*filled(b, "retT"))
                after(v, xb_taken, b)
                read(b, "retT", V.tensor_tensor(xr[:], x_in[:], tiles(bank("retT")), ALU.add))

            def norm1(b):
                layer_norm(front, b, xn, xr, stats, mv, nv, ny, na, xn_ready[1])

            def norm2(b):
                if not isinstance(b, int) or b < B - 1:
                    v.wait_ge(*filled(b + 1, "xnT0"))
                layer_norm(front, b, xn, xr, stats, mv, nv, ny, na, xn_ready[2])

            def best(b):
                def link(ins):
                    front.link(b, ins)
                v.wait_ge(*filled(b, "router"))
                read(b, "router", V.tensor_tensor(logits[:], bank("router")[:, 0:NT * NBLK]
                                                  .rearrange("p (j n) -> p j n", j=NT), over_tiles(b_router[:]),
                                                  ALU.add))
                front.fence()
                for j in range(NT):
                    ins = V.max(top[:, j, :], logits[:, j, :])
                link(ins)
                front.fence()
                for j in range(NT):
                    ins = V.max_index(top_i[:, j, :], top[:, j, :], logits[:, j, :])
                link(ins)
                link(V.tensor_copy(top_f[:], top_i[:, :, 0:TOPB]))
                link(V.tensor_tensor(hits[:], iota[:].unsqueeze(1).unsqueeze(3).to_broadcast([TOK, NT, NBLK, TOPB]),
                                     top_f[:].unsqueeze(2).to_broadcast([TOK, NT, NBLK, TOPB]), ALU.is_equal))
                link(V.tensor_reduce(dropped[:], hits[:], AX.X, ALU.add))
                V.tensor_scalar(dropped[:], dropped[:], -1.0, None, ALU.add).then_inc(drop_ready, 1)

            def mlp(b):
                v.wait_ge(bias_added, b + 1)
                v.wait_ge(*filled(b, "y0"))
                read(b, "y0", V.tensor_tensor(xr[:], xr[:], tiles(bank("y0")), ALU.add))

            def rotate(b):
                for i in range(2):
                    n = 96 + ROPE * i
                    for name, dst, table in ((f"qa{i}", rot_a, cos), (f"qb{i}", rot_b, sin)):
                        v.wait_ge(*filled(b, name))
                        V.tensor_tensor(dst[0:n, i, :], bank(name)[0:n, :], table[0:n, :], ALU.mult)\
                         .then_inc(free[BANK[name]], 1)

            def keys(b):
                v.wait_ge(khi_ready, b + 1)
                V.tensor_tensor(k_lo[:], bank("kn"), k_hi[:].bitcast(f32), ALU.subtract).then_inc(free[BANK["kn"]], 1)

            def attend(b, lo, hi):
                for n in range(lo, hi):
                    q, un = divmod(n, QUAD_UNITS)
                    v.wait_ge(*emptied(b, f"s{n}"))
                    p = pt[:, q % 2, un, :]
                    kind = QUAD_KINDS[un][0]
                    if kind == "first":
                        own, rest = p[:, 0:TOK].unsqueeze(1), p[:, TOK:T]
                    elif kind == "second":
                        own, rest = p.rearrange("p (a c) -> p a c", a=4)[:, 0:4:3, :], p[:, TOK:3 * TOK]
                    else:
                        own, rest = (p.rearrange("p (a c) -> p a c", a=4)[:, k:4:2, :] for k in range(2))
                    V.scalar_tensor_tensor(out=own, in0=own, scalar=P_LO,
                                           in1=causal[:].unsqueeze(1).to_broadcast([TOK, own.shape[1], TOK]),
                                           op0=ALU.max, op1=ALU.min)
                    ins = V.tensor_scalar(rest, rest, P_LO, P_HI, ALU.max, ALU.min)
                    ins.then_inc(pt_ready, 1)

            def sums(b):
                v.wait_ge(fence_g, 2 * b + 1)
                for u in range(2):
                    v.wait_ge(*filled(b, f"om{u}"))
                    om = bank(f"om{u}")[:, 0:72 * NT].rearrange("p (j c) -> p j c", j=NT)
                    back.link(b, V.reciprocal(den_r[:, u, :, :], om[:, :, 8 * HD:72]))
                    V.tensor_tensor(o_tm[:, :, 64 * u:64 * u + 64].rearrange("p j (h e) -> p j h e", h=8),
                                    om[:, :, 0:8 * HD].rearrange("p j (h e) -> p j h e", h=8),
                                    den_r[:, u, :, :].unsqueeze(3).to_broadcast([TOK, NT, 8, HD]), ALU.mult)\
                     .then_inc(free[BANK[f"om{u}"]], 1)

            def output(b):
                v.wait_ge(*filled(b, "y1"))
                v.wait_ge(xb_taken, b + 1)
                read(b, "y1", V.tensor_tensor(xb[:], xb[:], tiles(bank("y1")), ALU.add))

            def norm3(b):
                layer_norm(back, b, xn3, xb, stats3, mv3, nv3, ny3, na3, xn_ready[3])

            def gate(b):
                def link(ins):
                    back.link(b, ins)
                v.wait_ge(*filled(b, "gate"))
                read(b, "gate", V.tensor_copy(glog[:], bank("gate")[:, 0:NT * NE].rearrange("p (j n) -> p j n", j=NT)))
                back.fence()
                for j in range(NT):
                    ins = V.max(etop[:, j, :], glog[:, j, :])
                link(ins)
                V.tensor_tensor(esub[:], etop[:], etop[:, :, 0:1].to_broadcast([TOK, NT, 8]), ALU.subtract)\
                 .then_inc(esub_ready, 1)
                for j in range(NT):
                    ins = V.max_index(eidx[:, j, :], etop[:, j, :], glog[:, j, :])
                link(ins)
                link(V.tensor_copy(eidf[:], eidx[:, :, 0:TOPE]))
                V.tensor_tensor(oh[:], iota[:, 0:NE].unsqueeze(1).unsqueeze(1).to_broadcast([TOK, NT, TOPE, NE]),
                                eidf[:].unsqueeze(3).to_broadcast([TOK, NT, TOPE, NE]), ALU.is_equal)\
                 .then_inc(oh_ready, 1)

            def route_rows(b):
                def link(ins):
                    back.link(b, ins)
                v.wait_ge(eexp_ready, b + 1)
                link(V.tensor_reduce(esum[:], eexp[:], AX.X, ALU.add))
                link(V.reciprocal(esum[:], esum[:]))
                link(V.tensor_tensor(ew[:], eexp[:, :, 0:TOPE], esum[:].unsqueeze(2).to_broadcast([TOK, NT, TOPE]),
                                     ALU.mult))
                link(V.tensor_tensor(edn[:], ew[:, :, 0], ew[:, :, 1], ALU.add))
                link(V.tensor_scalar(edn[:], edn[:], 1e-9, None, ALU.add))
                link(V.reciprocal(edn[:], edn[:]))
                link(V.tensor_tensor(ew[:], ew[:], edn[:].unsqueeze(2).to_broadcast([TOK, NT, TOPE]), ALU.mult))
                v.wait_ge(*filled(b, "rank"))
                read(b, "rank", V.tensor_tensor(rank_oh[:], bank("rank")[:, 0:NT * NQ]
                                                .rearrange("p (j k e) -> p j k e", j=NT, k=TOPE), oh[:], ALU.mult))
                link(V.tensor_reduce(rank[:], rank_oh[:], AX.X, ALU.add))
                link(V.tensor_scalar(keep[:], rank[:], CAP + 0.5, None, ALU.is_le))
                link(V.scalar_tensor_tensor(out=slot[:], in0=eidf[:], scalar=float(CAP), in1=rank[:],
                                            op0=ALU.mult, op1=ALU.add))
                link(V.tensor_tensor(slot[:], slot[:], over_tiles(queue_of[:]), ALU.add))
                v.wait_ge(route_kept, 16 * (b + 1))
                slot_g = route[:, 0, :].rearrange("p (j k) -> p j k", j=NT)
                weight = route[:, 1, :].rearrange("p (j k) -> p j k", j=NT)
                link(V.tensor_tensor(slot_g, slot[:], keep[:], ALU.mult))
                link(V.scalar_tensor_tensor(out=slot[:], in0=keep[:], scalar=-PAST_END, in1=slot_g,
                                            op0=ALU.mult, op1=ALU.add))
                V.tensor_scalar(put_at[:], slot[:], PAST_END, None, ALU.add)
                V.tensor_tensor(weight, ew[:], keep[:], ALU.mult).then_inc(route_ready, 1)
                link(V.tensor_reduce(oh_row[:], oh[:].rearrange("p j k e -> p (k e) j"), AX.X, ALU.add))
                link(V.tensor_tensor(oh_cnt[:], oh_cnt[:], oh_row[:], ALU.add))
                link(V.tensor_copy(oh_past[:], oh_cnt[:]))

            stages = {"norm0": norm0, "lanes": lanes, "score": score, "state": chunk_state, "gn_moments": gn_moments, "gn_affine": gn_affine,
                      "gn_apply": gn_apply, "norm1": norm1, "best": best, "mlp": mlp, "norm2": norm2, "rotate": rotate,
                      "keys": keys,
                      "attend": attend, "sums": sums, "output": output, "norm3": norm3,
                      "gate": gate, "route": route_rows}

            def rows(f, a, n):
                front.n = back.n = start.n = 0
                rows_together(stages, f, a, n)

            rows(None, None, 0)
            rows(0, None, 1)
            with v.Fori(1, B - 1) as b:
                rows(b, b - 1, b + 1)
            assert (start.n, front.n, back.n) == (START_STEPS, FRONT_STEPS, BACK_STEPS), (start.n, front.n, back.n)
            rows(B - 1, B - 2, None)
            rows(None, B - 1, None)

            def turned(i, w):
                n = 2 * i + w
                v.wait_ge(xqT_ps, n + 1)
                V.tensor_copy(xqT[:, w, :], xqT_psum[:, 0:CAP]).then_inc(xqT_ready, 1)

            def v_pair(i):
                for w in range(2):
                    n = 2 * i + w
                    v.wait_ge(queue_done, n + 1)
                    for t in range(4):
                        half, mm = t // 2, t % 2
                        v.wait_ge(silu_ready, 4 * n + t + 1)
                        V.tensor_tensor(act_h[:, w, mm, HALF * half:HALF * half + HALF], act_g[:, t % 2, :],
                                        gu_ps[:, t % 2, 512:512 + HALF], ALU.mult).then_inc(gu_free, 1)
                    if not (w and isinstance(i, int) and i == NQ // 2 - 1):
                        turned(i + w, 1 - w)

            v.wait_ge(route_kept, 16 * (B + 1))
            V.tensor_scalar(get_at[:], route_all[:, :, 0:NT * TOPE], 0.0, None, ALU.add).then_inc(slots_ready, 1)
            turned(0, 0)
            v_pair(0)
            with v.Fori(1, NQ // 2 - 1) as i:
                v_pair(i)
            v_pair(NQ // 2 - 1)
            v.wait_ge(x_back, 16)

            def add_rows(k, lo, hi):
                with v.Fori(lo, hi) as b:
                    for j in range(NT):
                        at = route_all[:, b, NT * TOPE + 2 * j + k:NT * TOPE + 2 * j + k + 1]
                        ins = V.scalar_tensor_tensor(out=x_sum[:, b, tile_of(j)], in0=y_got[k][:, b, tile_of(j)],
                                                     scalar=at, in1=x_sum[:, b, tile_of(j)], op0=ALU.mult, op1=ALU.add)
                    ins.then_inc(sum_ready if k else part_ready, 1)

            v.wait_ge(got_first, 16 * NT * B)
            add_rows(0, 0, B)
            v.wait_ge(part_ready, B)
            for group, (lo, hi) in enumerate(LAST_ROWS):
                v.wait_ge(got[group], 16 * NT * (hi - lo))
                add_rows(1, lo, hi)


def kernel(**inputs):
    import concourse.bacc as bacc
    from concourse.bass_utils import run_bass_kernel_spmd as run

    a = {k: np.asarray(v) for k, v in inputs.items()}
    wuq = a["L1_attn_W_UQ"].reshape(LAT, NH, HD)
    wqr = a["L1_attn_W_QR"].reshape(LAT, NH, ROPE)
    swap = [1, 0, 3, 2]
    wqb = np.zeros((LAT, NH, HROW), wuq.dtype)
    wqb[:, :, HD:] = wqr[:, :, swap]
    wkr = a["L1_attn_W_KR"]
    arrays = {
        "x": a["L0_attn_x"], "past_kv": a["L0_attn_past_kv"], "wqkv": a["L0_attn_W_qkv"],
        "gn_w": np.repeat(a["L0_attn_gn_weight"], HD)[:, None], "gn_b": np.repeat(a["L0_attn_gn_bias"], HD)[:, None],
        "w_router": a["L0_ffn_w_router"], "b_router": np.tile(a["L0_ffn_b_router"][None, :], (TOK, 1)),
        "w1": a["L0_ffn_w1"].T, "b1": a["L0_ffn_b1"].reshape(4, D).T, "w2": a["L0_ffn_w2"].T,
        "b2": np.tile(a["L0_ffn_b2"][None, :], (TOK, 1)),
        "w_dqT": a["L1_attn_W_DQ"].T, "w_dkvT": a["L1_attn_W_DKV"].T,
        "w_uq": np.concatenate([np.concatenate([wuq, wqr], axis=2), wqb], axis=1).reshape(LAT, 2 * NH * HROW),
        "w_ukv": np.concatenate([a["L1_attn_W_UK"], a["L1_attn_W_UV"]], axis=1),
        "wkr": np.concatenate([wkr, wkr[:, swap]], axis=1),
        "wo": a["L1_attn_W_O"], "w_gate": a["L1_ffn_gate_w"].T,
        "w_eg": a["L1_ffn_gate_proj_w"].transpose(0, 2, 1), "w_eu": a["L1_ffn_up_proj_w"].transpose(0, 2, 1),
        "w_ed": a["L1_ffn_down_proj_w"].transpose(0, 2, 1).reshape(NE, 2, D, D).transpose(0, 2, 1, 3)
        .reshape(NE, D, 2 * D),
        **constants(),
    }
    arrays = {f"in_{k}": np.ascontiguousarray(v) for k, v in arrays.items()}
    nc = bacc.Bacc("TRN2", target_bir_lowering=False, num_devices=1)
    io = {k[3:]: nc.dram_tensor(k, v.shape, mybir.dt.from_np(v.dtype), kind="ExternalInput").ap()
          for k, v in arrays.items()}
    out = nc.dram_tensor("out", (B, T, D), mybir.dt.float32, kind="ExternalOutput").ap()
    network(nc, io, out)
    return run(nc, [arrays], core_ids=[0]).results[0]["out"]
```
